# Optimizing a Trainium2 kernel written in Bass

```python
import numpy as np
import jax
import jax.numpy as jnp

def _softmax(x, axis=-1):
    return jax.nn.softmax(x, axis=axis)

def _gelu(x):
    return jax.nn.gelu(x, approximate=True)

def _silu(x):
    return jax.nn.silu(x)

def _sigmoid(x):
    return jax.nn.sigmoid(x)

def _layernorm(x, axis=-1, eps=1e-05):
    m = jnp.mean(x, axis=axis, keepdims=True)
    v = jnp.var(x, axis=axis, keepdims=True)
    return (x - m) / jnp.sqrt(v + eps)

def _scatter_add(tgt, idx, src, axis=0):
    return tgt.at[idx].add(src)

def _segment_sum(src, seg, n):
    return jax.ops.segment_sum(src, seg, n)
kernel_name = 'mk_decoder_postln_d1_seqx_r4_689a29'

def setup_inputs(seed: int=0):
    np.random.seed(seed)
    _w = jnp.asarray

    def _rec_inputs():
        import jax
        import jax.numpy as jnp
        _rk = jax.random.key(seed)
        x = -0.0002928 + 1 * jax.random.normal(jax.random.fold_in(_rk, 1), (8, 256, 512), jnp.float32)
        _lenS = 256 - jax.random.randint(jax.random.fold_in(_rk, 7), (8,), 0, max(1, 256 // 4) + 1, jnp.int32)
        _lenS2 = 256 - jax.random.randint(jax.random.fold_in(_rk, 8), (8,), 0, max(1, 256 // 4) + 1, jnp.int32)
        fside_S2_0 = -0.00337071 + 1.01897 * jax.random.normal(jax.random.fold_in(_rk, 11), (256,), jnp.float32)
        _ctx_2048P = jax.random.normal(jax.random.fold_in(_rk, 12), (8, 16, 512), jnp.float32)
        _ctx_2048c = jax.random.dirichlet(jax.random.fold_in(_rk, 512), 0.3 * jnp.ones((16,), jnp.float32), (8, 256))
        _ctx_2048t = jnp.einsum('bsk,bkd->bsd', _ctx_2048c, _ctx_2048P)
        _ctx_2048t = _ctx_2048t * jax.lax.rsqrt(jnp.mean(jnp.square(_ctx_2048t)) + 1e-12) * 0.953939
        ctx_2048 = 0.000675642 + 1.00031 * (_ctx_2048t + 0.3 * jax.random.normal(jax.random.fold_in(_rk, 612), (8, 256, 512), jnp.float32))
        return (x, fside_S2_0, ctx_2048)
    x, fside_S2_0, ctx_2048 = _rec_inputs()

    def _L0_attn_setup():
        import jax, jax.numpy as jnp
        import numpy as np
        D_MODEL = 512
        NUM_HEADS = 16
        HEAD_DIM = D_MODEL // NUM_HEADS
        LAYER_IDX = 0
        NUM_LAYERS = 13
        REINIT_LAMBDA = 0.8

        def _heads(t, B, S):
            return t.reshape(B, S, NUM_HEADS, HEAD_DIM).transpose(0, 2, 1, 3)
        key = jax.random.key(seed)
        ks = jax.random.split(key, 8)
        B, S = (2, 512)
        x = jax.random.normal(ks[0], (B, S, D_MODEL), dtype=jnp.float32)
        init = 1.0 / np.sqrt(D_MODEL)

        def w(k):
            return jax.random.uniform(k, (D_MODEL, D_MODEL), dtype=jnp.float32, minval=-init, maxval=init)
        lam_init = REINIT_LAMBDA * ((LAYER_IDX + 1) / NUM_LAYERS)
        return {'x': x, 'q1_w': w(ks[1]), 'k1_w': w(ks[2]), 'q2_w': w(ks[3]), 'k2_w': w(ks[4]), 'v_w': w(ks[5]), 'o_w': w(ks[6]), 'lambda_param': jnp.full((NUM_HEADS,), lam_init, dtype=jnp.float32)}
    _L0_attn_all = _L0_attn_setup()
    _L0_attn_in = {k: v for k, v in _L0_attn_all.items() if k in ('q1_w', 'k1_w', 'q2_w', 'k2_w', 'v_w', 'o_w', 'lambda_param')}
    del _L0_attn_all

    def _L0_xattn_setup():
        import jax, jax.numpy as jnp
        import numpy as np
        key = jax.random.key(seed)
        ks = jax.random.split(key, 5)
        B, D, L, NH = (2, 256, 512, 8)
        H = D // NH
        return {'v': jax.random.normal(ks[0], (B, D, L), jnp.float32), 'k': jax.random.normal(ks[1], (H, L), jnp.float32) * 0.1, 'bias': jax.random.normal(ks[2], (D,), jnp.float32), 'x1': jax.random.normal(ks[3], (B, D, L), jnp.float32), 'x2': jax.random.normal(ks[4], (B, D, L), jnp.float32), 'num_heads': NH}
    _L0_xattn_all = _L0_xattn_setup()
    _L0_xattn_in = {k: v for k, v in _L0_xattn_all.items() if k in ('k',)}
    del _L0_xattn_all

    def _L0_ffn_setup():
        import jax, jax.numpy as jnp
        import numpy as np
        D_MODEL = 512
        HIDDEN = int(2 * D_MODEL * 4 / 3)

        def ternary_quant(w):
            s = jnp.mean(jnp.abs(w))
            q = jnp.clip(jnp.round(w / s), -1.0, 1.0) * s
            return w + jax.lax.stop_gradient(q - w)
        key = jax.random.key(seed)
        k0, k1, k2, k3 = jax.random.split(key, 4)
        x = jax.random.normal(k0, (4, 1024, D_MODEL), dtype=jnp.float32)
        std_in = 1.0 / np.sqrt(D_MODEL)
        std_h = 1.0 / np.sqrt(HIDDEN)
        w1 = jax.random.uniform(k1, (HIDDEN, D_MODEL), jnp.float32, -std_in, std_in)
        w3 = jax.random.uniform(k2, (HIDDEN, D_MODEL), jnp.float32, -std_in, std_in)
        w2 = jax.random.uniform(k3, (D_MODEL, HIDDEN), jnp.float32, -std_h, std_h)
        return {'x': x, 'w1': w1, 'w3': w3, 'w2': w2}
    _L0_ffn_all = _L0_ffn_setup()
    _L0_ffn_in = {k: v for k, v in _L0_ffn_all.items() if k in ('w1', 'w3', 'w2')}
    del _L0_ffn_all
    return {'x': x, 'fside_S2_0': fside_S2_0, 'ctx_2048': ctx_2048, 'L0_attn_q1_w': _L0_attn_in['q1_w'], 'L0_attn_k1_w': _L0_attn_in['k1_w'], 'L0_attn_q2_w': _L0_attn_in['q2_w'], 'L0_attn_k2_w': _L0_attn_in['k2_w'], 'L0_attn_v_w': _L0_attn_in['v_w'], 'L0_attn_o_w': _L0_attn_in['o_w'], 'L0_attn_lambda_param': _L0_attn_in['lambda_param'], 'L0_xattn_k': _L0_xattn_in['k'], 'L0_ffn_w1': _L0_ffn_in['w1'], 'L0_ffn_w3': _L0_ffn_in['w3'], 'L0_ffn_w2': _L0_ffn_in['w2']}

def reference(x, fside_S2_0, ctx_2048, L0_attn_q1_w, L0_attn_k1_w, L0_attn_q2_w, L0_attn_k2_w, L0_attn_v_w, L0_attn_o_w, L0_attn_lambda_param, L0_xattn_k, L0_ffn_w1, L0_ffn_w3, L0_ffn_w2):
    import jax
    import jax.numpy as jnp

    def _L0_attn_ref(x, q1_w, k1_w, q2_w, k2_w, v_w, o_w, lambda_param):
        import jax, jax.numpy as jnp
        import numpy as np
        D_MODEL = 512
        NUM_HEADS = 16
        HEAD_DIM = D_MODEL // NUM_HEADS
        LAYER_IDX = 0
        NUM_LAYERS = 13
        REINIT_LAMBDA = 0.8

        def _heads(t, B, S):
            return t.reshape(B, S, NUM_HEADS, HEAD_DIM).transpose(0, 2, 1, 3)
        B, S, _ = x.shape
        q1 = _heads(x @ q1_w.T, B, S)
        k1 = _heads(x @ k1_w.T, B, S)
        q2 = _heads(x @ q2_w.T, B, S)
        k2 = _heads(x @ k2_w.T, B, S)
        v = _heads(x @ v_w.T, B, S)
        scale = jnp.sqrt(jnp.float32(HEAD_DIM))
        attn1 = jax.nn.softmax(jnp.einsum('bhqd,bhkd->bhqk', q1, k1) / scale, axis=-1)
        attn2 = jax.nn.softmax(jnp.einsum('bhqd,bhkd->bhqk', q2, k2) / scale, axis=-1)
        lam = lambda_param.reshape(1, NUM_HEADS, 1, 1)
        out = jnp.einsum('bhqk,bhkd->bhqd', attn1 - lam * attn2, v)
        out = out.transpose(0, 2, 1, 3).reshape(B, S, D_MODEL)
        return out @ o_w.T

    def _L0_xattn_ref(v, k, bias, x1, x2, num_heads):
        import jax, jax.numpy as jnp
        import numpy as np
        B, D, L = v.shape
        H = D // num_heads
        fft_size = 2 * L
        vr = v.reshape(B, H, num_heads, L)
        x1r = x1.reshape(B, H, num_heads, L)
        x2r = x2.reshape(B, H, num_heads, L)
        kv = vr[:, :, :, None, :] * x2r[:, :, None, :, :]
        k_f = jnp.fft.rfft(k.astype(jnp.float32), n=fft_size)
        y = jnp.fft.irfft(jnp.fft.rfft(kv, n=fft_size) * k_f[None, :, None, None, :], n=fft_size)[..., :L]
        skip = bias.astype(jnp.float32).reshape(H, num_heads)[None, :, :, None, None]
        y = y + kv * skip
        out = jnp.einsum('bhijl,bhil->bhjl', y, x1r)
        return out.reshape(B, D, L)

    def _L0_ffn_ref(x, w1, w3, w2):
        import jax, jax.numpy as jnp
        import numpy as np
        D_MODEL = 512
        HIDDEN = int(2 * D_MODEL * 4 / 3)

        def ternary_quant(w):
            s = jnp.mean(jnp.abs(w))
            q = jnp.clip(jnp.round(w / s), -1.0, 1.0) * s
            return w + jax.lax.stop_gradient(q - w)
        w1q = ternary_quant(w1)
        w3q = ternary_quant(w3)
        w2q = ternary_quant(w2)
        h1 = jnp.einsum('bsd,hd->bsh', x, w1q)
        h3 = jnp.einsum('bsd,hd->bsh', x, w3q)
        g = jax.nn.silu(h1) * h3
        return jnp.einsum('bsh,dh->bsd', g, w2q)
    x = _layernorm(x + _L0_attn_ref(x, L0_attn_q1_w, L0_attn_k1_w, L0_attn_q2_w, L0_attn_k2_w, L0_attn_v_w, L0_attn_o_w, L0_attn_lambda_param), axis=-1)
    x = _layernorm(x + _L0_xattn_ref(x, L0_xattn_k, fside_S2_0, ctx_2048, ctx_2048, 8), axis=-1)
    x = _layernorm(x + _L0_ffn_ref(x, L0_ffn_w1, L0_ffn_w3, L0_ffn_w2), axis=-1)
    return x

_drawn_inputs = setup_inputs


def setup_inputs(seed=0):
    import zlib

    import numpy as np

    out = dict(_drawn_inputs(seed))
    spreads = {'L0_attn_lambda_param': (0.0615384615957737, 0.6)}
    factors = {'L0_attn_q1_w': 5.916, 'L0_attn_k1_w': 5.494, 'L0_attn_q2_w': 8.0, 'L0_attn_k2_w': 8.0}
    for name, (base, spread) in spreads.items():
        noise = np.random.default_rng([zlib.crc32(name.encode()), seed]).standard_normal(out[name].shape)
        drawn = base * np.exp(spread * noise) if base else spread * noise
        out[name] = jnp.asarray(drawn.astype(out[name].dtype))
    for name, factor in factors.items():
        out[name] = (out[name] * factor).astype(out[name].dtype)
    return out
```

```python
from contextlib import ExitStack

import numpy as np

import concourse.bass as bass
from concourse import mybir

F32 = mybir.dt.float32
F16 = mybir.dt.float16
I32 = mybir.dt.int32
ALU = mybir.AluOpType
ACT = mybir.ActivationFunctionType
AX = mybir.AxisListType.X
RMAX = bass.bass_isa.ReduceOp.max
RADD = bass.bass_isa.ReduceOp.add
ds = bass.ds

P = 128
B, S, D = 8, 256, 512
H, HD = 16, 32
KC = D // P
SB = S // P
PER_BLK = P // HD
NBLK = H // PER_BLK
FILTERS, CH = 32, 8
HID = 1365
HC = -(-HID // P)
WCOLS = KC * HC * P
EPS = 1e-5
EXP_MASK = 0x7F800000
RSQRT_SEED = 1597463007.0
Y2_SCALE = 1024.0
G_SCALE = 2.0 ** -24
CX, CQ1, CK1, CQ2, CK2, CV, CO, CK, CLAM = range(9)
NMAX = 9


def wait(eng, sem, value):
    if not (isinstance(value, int) and value <= 0):
        eng.wait_ge(sem, value)


def wait_alone(eng, sem, value, passed):
    if not (isinstance(value, int) and value <= 0):
        eng.wait_ge(sem, value)
        if not isinstance(value, int):
            eng.sem_inc(passed, 1)


class Chain:

    def __init__(self, eng, sem, base=0, passed=None):
        self.eng, self.sem, self.base, self.passed, self.n = eng, sem, base, passed, 0

    def then(self, ins):
        self.n += 1
        ins.then_inc(self.sem, 1)
        wait_alone(self.eng, self.sem, self.base + self.n, self.passed)


RSQRT_STEPS = 1 + 1 + 3 * 4


def rsqrt(chain, eng, out, var, tmp):
    safe, square = (x[:] for x in tmp)
    chain.then(eng.tensor_scalar(safe, var, EPS, None, ALU.add))
    chain.then(eng.tensor_scalar(out.bitcast(I32), safe.bitcast(I32), -0.5, RSQRT_SEED, ALU.mult, ALU.add))
    for _ in range(3):
        chain.then(eng.tensor_tensor(square, out, out, ALU.mult))
        chain.then(eng.tensor_tensor(square, square, safe, ALU.mult))
        chain.then(eng.tensor_scalar(square, square, -0.5, 1.5, ALU.mult, ALU.add))
        chain.then(eng.tensor_tensor(out, out, square, ALU.mult))


def prepare(nc, t, d):
    with ExitStack() as ctx:
        sb = lambda name, shape, dt: ctx.enter_context(nc.sbuf_tensor(name, shape, dt))
        sem = lambda name: ctx.enter_context(nc.semaphore(name))
        w_stage = sb("w_stage", [P, 6, KC * D], F32)
        x_stage = sb("x_stage", [P, B * KC * S], F32)
        filt = sb("filt", [FILTERS, D + P], F32)
        filt_halves = sb("filt_halves", [FILTERS, 2, D + P], F16)
        lam = sb("lam", [P, H], F32)
        part_max = sb("part_max", [P, NMAX], F32)
        maxima = sb("maxima", [P, NMAX], F32)
        pow2 = sb("pow2", [P, NMAX], F32)
        tmp = sb("prep_tmp", [P, 4], F32)

        w_loaded = [sem(f"w_loaded{i}") for i in range(6)]
        x_loaded, filt_loaded, lam_loaded = sem("x_all_loaded"), sem("filt_loaded"), sem("lam_loaded")
        max_ready, all_max, scaled = sem("max_ready"), sem("all_max"), sem("scales_ready")
        prep_chain = sem("prep_chain")
        w_hi_ready, w_lo_ready = sem("w_hi_ready"), sem("w_lo_ready")
        filt_hi_ready, filt_lo_ready, filt_stored = sem("filt_hi_ready"), sem("filt_lo_ready"), sem("filt_stored")
        ident_zero, ident_ready = sem("ident_zero"), sem("ident_ready")
        block = ctx.enter_context(nc.Block())

        @block.sync
        def _(sp):
            sp.dma_start(filt[:], d["filt"]).then_inc(filt_loaded, 16)
            sp.dma_start(lam[:], d["lam"].rearrange("(o h) -> o h", o=1).broadcast_to([P, H])).then_inc(lam_loaded, 16)
            for i in range(6):
                sp.dma_start(w_stage[:, i, :], d["wproj"][:, i, :]).then_inc(w_loaded[i], 16)
            sp.dma_start(x_stage[:], d["xT"][:, 0:B * KC * S]).then_inc(x_loaded, 16)
            sp.wait_ge(filt_hi_ready, 1)
            sp.wait_ge(filt_lo_ready, 1)
            sp.dma_start(d["filt_halves"].rearrange("a f n -> f a n"), filt_halves[:]).then_inc(filt_stored, 16)
            sp.wait_ge(filt_stored, 16)

        @block.gpsimd
        def _(pool):
            pool.memset(t["ident"][:], 0.0).then_inc(ident_zero, 1)
            pool.wait_ge(ident_zero, 1)
            pool.affine_select(out=t["ident"][:], in_=t["ident"][:], compare_op=ALU.not_equal, fill=1.0, base=0,
                               pattern=[[-1, P]], channel_multiplier=1).then_inc(ident_ready, 1)
            pool.wait_ge(max_ready, 1)
            pool.partition_all_reduce(maxima[:], part_max[:], P, RMAX).then_inc(all_max, 1)
            pool.wait_ge(ident_ready, 1)

        @block.scalar
        def _(act):
            act.wait_ge(scaled, 1)
            act.activation(filt_halves[:, 0, :], filt[:], ACT.Copy, scale=t["scale"][0:FILTERS, CK:CK + 1]).then_inc(filt_hi_ready, 1)
            for i in range(6):
                act.activation(t["w_hi"][:, i, :], w_stage[:, i, :], ACT.Copy, scale=t["scale"][:, CQ1 + i:CQ1 + i + 1]).then_inc(w_hi_ready, 1)
            act.wait_ge(filt_stored, 16)
            for half in range(2):
                src = d["filt_halves"][half]
                src = bass.AP(tensor=src.tensor, offset=half * FILTERS * (D + P) + P, ap=[[D + P, FILTERS], [-1, P], [1, D]])
                act.dma_start(d["toeplitz"][:, half], src).then_inc(t["toep_written"], 16)

        @block.vector
        def _(dve):
            ch = Chain(dve, prep_chain)
            ch.then(dve.memset(part_max[:], 0.0))
            dve.wait_ge(filt_loaded, 16)
            ch.then(dve.tensor_reduce(part_max[0:FILTERS, CK:CK + 1], filt[:], AX, ALU.max, apply_absolute_value=True))
            dve.wait_ge(lam_loaded, 16)
            ch.then(dve.tensor_reduce(part_max[:, CLAM:CLAM + 1], lam[:], AX, ALU.max, apply_absolute_value=True))
            ch.then(dve.tensor_scalar(part_max[:, CLAM:CLAM + 1], part_max[:, CLAM:CLAM + 1], 1.0, None, ALU.add))
            for i in range(6):
                dve.wait_ge(w_loaded[i], 16)
                ch.then(dve.tensor_reduce(part_max[:, CQ1 + i:CQ1 + i + 1], w_stage[:, i, :], AX, ALU.max, apply_absolute_value=True))
            dve.wait_ge(x_loaded, 16)
            dve.tensor_reduce(part_max[:, CX:CX + 1], x_stage[:], AX, ALU.max, apply_absolute_value=True).then_inc(max_ready, 1)
            dve.wait_ge(all_max, 1)
            ch.then(dve.tensor_scalar(maxima[:], maxima[:], 1e-30, None, ALU.max))
            ch.then(dve.tensor_scalar(pow2[:].bitcast(I32), maxima[:].bitcast(I32), EXP_MASK, None, ALU.bitwise_and))
            ch.then(dve.reciprocal(t["scale"][:], pow2[:]))
            ch.then(dve.tensor_scalar(t["scale"][:, CX:CO + 1], t["scale"][:, CX:CO + 1], 4.0, None, ALU.mult))
            ch.then(dve.tensor_scalar(t["scale"][:, CK:CK + 1], t["scale"][:, CK:CK + 1], 8192.0, None, ALU.mult))
            ch.then(dve.tensor_scalar(t["scale"][:, CLAM:CLAM + 1], t["scale"][:, CLAM:CLAM + 1], 0.5, None, ALU.mult))
            ch.then(dve.reciprocal(t["unscale"][:], t["scale"][:]))
            un = t["unscale"]
            ch.then(dve.tensor_tensor(tmp[:, 0:1], un[:, CX:CX + 1], un[:, CX:CX + 1], ALU.mult))
            ch.then(dve.tensor_tensor(tmp[:, 2:3], un[:, CQ1:CQ1 + 1], un[:, CK1:CK1 + 1], ALU.mult))
            ch.then(dve.tensor_tensor(tmp[:, 3:4], un[:, CQ2:CQ2 + 1], un[:, CK2:CK2 + 1], ALU.mult))
            ch.then(dve.tensor_scalar(t["score_scale"][:], tmp[:, 2:4], tmp[:, 0:1], float(HD) ** -0.5, ALU.mult, ALU.mult))
            ch.then(dve.tensor_tensor(tmp[:, 1:2], un[:, CX:CX + 1], un[:, CLAM:CLAM + 1], ALU.mult))
            ch.then(dve.tensor_tensor(tmp[:, 2:3], un[:, CV:CV + 1], un[:, CO:CO + 1], ALU.mult))
            ch.then(dve.tensor_tensor(t["attn_unscale"][:], tmp[:, 1:2], tmp[:, 2:3], ALU.mult))
            ch.then(dve.memset(t["mix_factor"][:, :, 0], 1.0))
            ch.then(dve.tensor_scalar(t["mix_factor"][:, :, 0], t["mix_factor"][:, :, 0], t["scale"][:, CLAM:CLAM + 1], None, ALU.mult))
            ch.then(dve.tensor_scalar(t["mix_factor"][:, :, 1], lam[:], t["scale"][:, CLAM:CLAM + 1], -1.0, ALU.mult, ALU.mult))
            ch.then(dve.tensor_scalar(t["neg_score_scale"][:], t["score_scale"][:], -1.0, None, ALU.mult))
            dve.nop().then_inc(scaled, 1)
            dve.wait_ge(filt_hi_ready, 1)
            dve.scalar_tensor_tensor(out=filt_halves[:, 1, :], in0=filt[:], scalar=t["scale"][0:FILTERS, CK:CK + 1],
                                     in1=filt_halves[:, 0, :], op0=ALU.mult, op1=ALU.subtract).then_inc(filt_lo_ready, 1)
            for i in range(6):
                dve.wait_ge(w_hi_ready, i + 1)
                dve.scalar_tensor_tensor(out=t["w_lo"][:, i, :], in0=w_stage[:, i, :], scalar=t["scale"][:, CQ1 + i:CQ1 + i + 1],
                                         in1=t["w_hi"][:, i, :], op0=ALU.mult, op1=ALU.subtract).then_inc(w_lo_ready, 1)



MIX_LAG, TR_LAG, PV_LAG, O_LO_LAG = 1, 2, 3, 4
QK_LO_LAG = 1
V_SLOTS, O_SLOTS, YT_SLOTS = (12, 14), (4, 5), (11, 13)
CHUNK = WCOLS // B
COPIES = PER_BLK * 6


def general_uses(project, close):
    uses, n = [], 0
    for slot in range(H):
        here = [("qk", slot)]
        here += [(kind, slots.index(slot)) for kind, slots in (("v", V_SLOTS), ("o", O_SLOTS), ("yT", YT_SLOTS)) if slot in slots]
        for kind, k in here:
            if (project if kind in ("qk", "v") else close):
                uses.append((slot, kind, k, n % 2))
            n += 1
    assert n % 2 == 0
    return uses


BANK = {(kind, k): bank for _, kind, k, bank in general_uses(True, True)}


def attention(nc, t, d):
    with ExitStack() as ctx:
        sb = lambda name, shape, dt: ctx.enter_context(nc.sbuf_tensor(name, shape, dt))
        sem = lambda name: ctx.enter_context(nc.semaphore(name))
        w_hi, w_lo, ident = t["w_hi"], t["w_lo"], t["ident"]
        w4 = lambda w, i: w[:, i, :].rearrange("p (c n) -> p c n", c=KC)
        xT = sb("xT", [P, 2, KC * S], F32)
        x_hi = sb("x_hi", [P, 2, KC * S], F16)
        x_lo = sb("x_lo", [P, 2, KC * S], F16)
        qk = sb("qk", [P, 2, 2, 2, 2, S], F16)
        stack = sb("stack", [3 * HD, 2, NBLK, PER_BLK, 2, S], F16)
        v = sb("v", [P, 2, SB, D], F32)
        row_max = sb("row_max", [P, 2, 2, SB], F32)
        neg_bias = sb("neg_bias", [P, 2, 2, SB], F32)
        probs = sb("probs", [P, 2, 2, SB, S], F32)
        sums = sb("sums", [P, 2, 2, SB], F32)
        inv = sb("inv", [P, 2, 2, SB], F32)
        coef = sb("coef", [P, 2, 2, SB], F32)
        scaled2 = sb("scaled2", [P, 2, SB, S], F32)
        mixed = sb("mixed", [P, 2, SB, S], F32)
        mixedT = sb("mixedT", [P, 2, SB, S], F32)
        o_hi = sb("o_hi", [P, NBLK, S], F16)
        o_lo = sb("o_lo", [P, NBLK, S], F16)
        x_rows = sb("x_rows", [P, SB, D], F32)
        resid = sb("resid", [P, SB, D], F32)
        stats = sb("stats", [P, SB, 6], F32)
        moments = sb("moments", [P, SB, 2], F32)
        rstd = sb("rstd", [P, SB], F32)
        nt = [sb(f"newton{k}", [P, SB], F32) for k in range(2)]
        y1 = sb("y1", [P, 2, SB, D], F32)
        w_chunk = sb("w_chunk", [P, 3, CHUNK], F32)
        ps_s = ctx.enter_context(nc.psum_tensor("ps_s", [P, 4, SB, S], F32))
        ps_t = ctx.enter_context(nc.psum_tensor("ps_t", [P, SB, S], F32))
        ps_o = ctx.enter_context(nc.psum_tensor("ps_o", [P, 512], F32))
        ps_g = ctx.enter_context(nc.psum_tensor("ps_g", [P, 2, 512], F32))

        xT_loaded, rows_loaded, chunk_loaded, y1_stored = sem("xT_loaded"), sem("rows_loaded"), sem("chunk_loaded"), sem("y1_stored")
        chunk_summed = sem("chunk_summed")
        x_hi_ready, x_lo_ready = sem("x_hi_ready"), sem("x_lo_ready")
        qk_done, qk_hi, qk_lo, stacked = sem("qk_done"), sem("qk_hi"), sem("qk_lo"), sem("stacked")
        v_done, v_ready = sem("v_done"), sem("v_ready")
        scores_done, max_done, bias_ready, exp_done = sem("scores_done"), sem("max_done"), sem("bias_ready"), sem("exp_done")
        inv_done, coef_ready, scaled2_ready, mix_done = sem("inv_done"), sem("coef_ready"), sem("scaled2_ready"), sem("mix_done")
        tr_done, mixedT_ready, pv_done, o_hi_ready, o_lo_ready = (
            sem("tr_done"), sem("mixedT_ready"), sem("pv_done"), sem("o_hi_ready"), sem("o_lo_ready"))
        proj_done, resid_done, stats_done, moments_done = sem("proj_done"), sem("resid_done"), sem("stats_done"), sem("moments_done")
        rstd_chain, y1_ready, yT_done, yT_ready = sem("rstd_chain"), sem("y1_ready"), sem("yT_done"), sem("yT_ready")
        passed = sem("passed_attention")
        block = ctx.enter_context(nc.Block())

        PREPARE, FIRST, FULL, LAST, DRAIN = (
            dict(project=p, attend=a, close=c) for p, a, c in
            ((True, False, False), (True, True, False), (True, True, True), (False, True, True), (False, False, True)))

        def steps(eng, step):
            step(-1, 1, PREPARE, None)
            step(0, 0, FIRST, PREPARE)
            with eng.Fori(1, B - 2, 2) as b:
                step(b, 1, FULL, FIRST)
                step(b + 1, 0, FULL, FULL)
            step(B - 1, 1, LAST, FULL)
            step(B, 0, DRAIN, LAST)

        def lagging(b, par, slot, lag, now):
            if slot >= lag:
                return (b, slot - lag, par) if now["attend"] else None
            return (b - 1, slot - lag + H, 1 - par) if now["close"] else None

        @block.sync
        def _(sp):
            def step(b, par, now, before):
                n, m = b + 1, b - 1
                if now["project"]:
                    if before is None:
                        sp.dma_start(xT[:, 0, :], d["xT"][:, 0:KC * S]).then_inc(xT_loaded, 16)
                    wait_alone(sp, x_hi_ready, n, passed)
                    wait_alone(sp, x_lo_ready, n, passed)
                    wait_alone(sp, xT_loaded, 16 * (n + 1), passed)
                    sp.dma_start(xT[:, par, :], d["xT"][:, ds((n + 1) * (KC * S), KC * S)]).then_inc(xT_loaded, 16)
                    wait_alone(sp, chunk_summed, n, passed)
                    sp.dma_start(w_chunk[:], d["wffn"][:, :, ds(n * CHUNK, CHUNK)]).then_inc(chunk_loaded, 16)
                for blk in range(NBLK):
                    if now["attend"] and blk == 2:
                        wait_alone(sp, resid_done, b * SB, passed)
                        sp.dma_start(x_rows[:].rearrange("p (o s) n -> p o s n", o=1),
                                     d["x"][ds(b, 1)].rearrange("o (s p) n -> p o s n", p=P)).then_inc(rows_loaded, 16)
                    if now["close"] and blk == 3:
                        wait_alone(sp, y1_ready, (m + 1) * SB, passed)
                        sp.dma_start(d["y1_rows"][ds(m, 1)].rearrange("o (s p) n -> p o s n", p=P),
                                     y1[:, 1 - par, :, :].rearrange("p (o s) n -> p o s n", o=1)).then_inc(y1_stored, 16)
                        wait_alone(sp, y1_stored, 16 * (m + 1), passed)
                    if now["project"]:
                        wait_alone(sp, qk_lo, n * H + 4 * blk + 4, passed)
                        if now["attend"]:
                            wait_alone(sp, scores_done, b * H + 4 * blk + 4, passed)
                        wait_alone(sp, stacked, (n * NBLK + blk) * COPIES * 16, passed)
                        for j in range(PER_BLK):
                            for row, halves in enumerate(((0, 0), (0, 1), (1, 0))):
                                for which, half in enumerate(halves):
                                    sp.dma_start(stack[HD * row:HD * row + HD, which, blk, j, :, :],
                                                 qk[HD * j:HD * j + HD, blk % 2, half, which, :, :]).then_inc(stacked, 16)

            steps(sp, step)

        @block.tensor
        def _(pe):
            def freed(b, now, before, kind, k):
                uses = general_uses(now["project"], now["close"])
                at = next(i for i, (_, kd, kk, _) in enumerate(uses) if (kd, kk) == (kind, k))
                bank = BANK[kind, k]
                earlier = [(u, 0) for u in uses[:at] if u[3] == bank]
                if not earlier and before is not None:
                    earlier = [(u, 1) for u in general_uses(before["project"], before["close"]) if u[3] == bank]
                if earlier:
                    (_, kd, kk, _), back = earlier[-1]
                    s, per, batch = {"qk": (qk_lo, H, 1), "v": (v_ready, SB, 1), "o": (resid_done, SB, -1), "yT": (yT_ready, 2, -1)}[kd]
                    wait(pe, s, (b + (batch - back)) * per + kk + 1)
                return bank

            def step(b, par, now, before):
                n, m = b + 1, b - 1
                if now["project"]:
                    pe.wait_ge(x_lo_ready, n + 1)
                for slot in range(H):
                    if now["attend"]:
                        blk, j = slot // PER_BLK, slot % PER_BLK
                        if j == 0:
                            pe.wait_ge(stacked, (b * NBLK + blk + 1) * COPIES * 16)
                        wait(pe, exp_done, b * H + slot - 1)
                        for w in range(2):
                            for s in range(SB):
                                ins = pe.matmul(ps_s[:, 2 * (slot % 2) + w, s, :], stack[:, 0, blk, j, w, s * P:s * P + P],
                                                stack[:, 1, blk, j, w, :], start=True, stop=True)
                        ins.then_inc(scores_done, 1)
                    if now["project"]:
                        blk, which = slot // 4, slot % 4
                        bank = freed(b, now, before, "qk", slot)
                        for c in range(KC):
                            for k, (w, x) in enumerate(((w_hi, x_hi), (w_hi, x_lo), (w_lo, x_hi))):
                                ins = pe.matmul(ps_g[:, bank, 0:S], w4(w, which)[:, c, blk * P:blk * P + P],
                                                x[:, 1 - par, c * S:c * S + S], start=(c == 0 and k == 0), stop=(c == KC - 1 and k == 2))
                        ins.then_inc(qk_done, 1)
                    if (at := lagging(b, par, slot, TR_LAG, now)) is not None:
                        q, h, _ = at
                        pe.wait_ge(mix_done, q * H + h + 1)
                        wait(pe, mixedT_ready, q * H + h)
                        for kb in range(SB):
                            for s in range(SB):
                                ins = pe.matmul(ps_t[:, kb, s * P:s * P + P], mixed[:, h % 2, s, kb * P:kb * P + P], ident[:],
                                                start=True, stop=True, is_transpose=True, skip_group_check=True)
                        ins.then_inc(tr_done, 1)
                    if (at := lagging(b, par, slot, PV_LAG, now)) is not None:
                        q, h, qp = at
                        blk, j = h // PER_BLK, h % PER_BLK
                        if h == 0:
                            pe.wait_ge(v_ready, (q + 1) * SB)
                        if j == 0:
                            wait(pe, o_lo_ready, q * NBLK + blk)
                        pe.wait_ge(mixedT_ready, q * H + h + 1)
                        for kb in range(SB):
                            ins = pe.matmul(ps_o[HD * j:HD * j + HD, 0:S], v[:, qp, kb, h * HD:h * HD + HD], mixedT[:, h % 2, kb, :],
                                            start=(kb == 0), stop=(kb == SB - 1), skip_group_check=True)
                        if j == PER_BLK - 1:
                            ins.then_inc(pv_done, 1)
                    if now["project"] and slot in V_SLOTS:
                        s = V_SLOTS.index(slot)
                        bank = freed(b, now, before, "v", s)
                        for c in range(KC):
                            for k, (x, w) in enumerate(((x_hi, w_hi), (x_lo, w_hi), (x_hi, w_lo))):
                                ins = pe.matmul(ps_g[:, bank, :], x[:, 1 - par, c * S + s * P:c * S + s * P + P], w4(w, 4)[:, c, :],
                                                start=(c == 0 and k == 0), stop=(c == KC - 1 and k == 2))
                        ins.then_inc(v_done, 1)
                    if now["close"] and slot in O_SLOTS:
                        s = O_SLOTS.index(slot)
                        pe.wait_ge(o_lo_ready, (m + 1) * NBLK)
                        bank = freed(b, now, before, "o", s)
                        for c in range(KC):
                            for k, (o, w) in enumerate(((o_hi, w_hi), (o_lo, w_hi), (o_hi, w_lo))):
                                ins = pe.matmul(ps_g[:, bank, :], o[:, c, s * P:s * P + P], w4(w, 5)[:, c, :],
                                                start=(c == 0 and k == 0), stop=(c == KC - 1 and k == 2))
                        ins.then_inc(proj_done, 1)
                    if now["close"] and slot in YT_SLOTS:
                        k = YT_SLOTS.index(slot)
                        pe.wait_ge(y1_ready, (m + 1) * SB)
                        bank = freed(b, now, before, "yT", k)
                        for c in range(2):
                            for s in range(SB):
                                ins = pe.matmul(ps_g[:, bank, c * S + s * P:c * S + s * P + P],
                                                y1[:, 1 - par, s, (2 * k + c) * P:(2 * k + c + 1) * P], ident[:],
                                                start=True, stop=True, is_transpose=True, skip_group_check=True)
                        ins.then_inc(yT_done, 1)

            steps(pe, step)

        @block.scalar
        def _(act):
            def load_scale(name, at):
                reg = act.alloc_register(name)
                act.reg_load(reg, at.bitcast(I32))
                return reg

            x_scale = load_scale("x_scale", t["scale"][0:1, CX:CX + 1])
            score_scale = [load_scale(f"score_scale{w}", t["score_scale"][0:1, w:w + 1]) for w in range(2)]

            def split_x(n, par):
                act.wait_ge(xT_loaded, (n + 1) * 16)
                wait(act, v_done, (n - 1) * SB)
                act.activation(x_hi[:, par, :], xT[:, par, :], ACT.Copy, scale=x_scale).then_inc(x_hi_ready, 1)

            def step(b, par, now, before):
                n, m = b + 1, b - 1
                if before is None:
                    split_x(0, 0)
                for slot in range(H):
                    if now["attend"]:
                        act.wait_ge(bias_ready, b * H + slot + 1)
                        wait(act, mix_done, b * H + slot - 1)
                        for w in range(2):
                            for s in range(SB):
                                ins = act.activation(probs[:, slot % 2, w, s, :], ps_s[:, 2 * (slot % 2) + w, s, :], ACT.Exp,
                                                     bias=neg_bias[:, slot % 2, w, s:s + 1], scale=score_scale[w],
                                                     accum_out=sums[:, slot % 2, w, s:s + 1])
                        ins.then_inc(exp_done, 1)
                    if now["project"]:
                        blk, which = slot // 4, slot % 4
                        act.wait_ge(qk_done, n * H + slot + 1)
                        if which == 0:
                            wait(act, stacked, (n * NBLK + blk - 1) * COPIES * 16)
                        act.copy(qk[:, blk % 2, 0, which % 2, which // 2, :], ps_g[:, BANK["qk", slot], 0:S]).then_inc(qk_hi, 1)
                    if (at := lagging(b, par, slot, TR_LAG, now)) is not None:
                        q, h, _ = at
                        act.wait_ge(tr_done, q * H + h + 1)
                        act.copy(mixedT[:, h % 2, :, :], ps_t[:]).then_inc(mixedT_ready, 1)
                    if (at := lagging(b, par, slot, PV_LAG, now)) is not None and at[1] % PER_BLK == PER_BLK - 1:
                        q, h, _ = at
                        blk = h // PER_BLK
                        act.wait_ge(pv_done, q * NBLK + blk + 1)
                        act.copy(o_hi[:, blk, :], ps_o[:, 0:S]).then_inc(o_hi_ready, 1)
                    if now["project"] and slot in V_SLOTS:
                        s = V_SLOTS.index(slot)
                        act.wait_ge(v_done, n * SB + s + 1)
                        wait(act, pv_done, (n - 1) * NBLK)
                        act.copy(v[:, 1 - par, s, :], ps_g[:, BANK["v", s], :]).then_inc(v_ready, 1)
                    if now["close"] and slot in YT_SLOTS:
                        k = YT_SLOTS.index(slot)
                        act.wait_ge(yT_done, m * 2 + k + 1)
                        act.copy(t["y1T"][:, 2 * k:2 * k + 2, ds(m, 1), :],
                                 ps_g[:, BANK["yT", k], :].rearrange("p (c o s) -> p c o s", c=2, o=1)).then_inc(yT_ready, 1)
                    if now["project"] and slot == H - 2:
                        split_x(n + 1, par)

            steps(act, step)
            act.wait_ge(yT_ready, 2 * B)

        @block.gpsimd
        def _(pool):
            def step(b, par, now, before):
                m = b - 1
                for slot in range(H):
                    if (at := lagging(b, par, slot, MIX_LAG, now)) is not None:
                        q, h, _ = at
                        wait_alone(pool, coef_ready, q * H + h + 1, passed)
                        wait_alone(pool, mix_done, q * H + h - 1, passed)
                        pool.tensor_tensor(scaled2[:, h % 2], probs[:, h % 2, 1], coef[:, h % 2, 1].unsqueeze(2).broadcast_to([P, SB, S]),
                                           ALU.mult).then_inc(scaled2_ready, 1)
                    if now["close"] and slot == 7:
                        wait_alone(pool, moments_done, (m + 1) * SB, passed)
                        rsqrt(Chain(pool, rstd_chain, m * RSQRT_STEPS, passed), pool, rstd[:], moments[:, :, 1], nt)

            steps(pool, step)

        @block.vector
        def _(dve):
            def split_x(n, par):
                dve.wait_ge(x_hi_ready, n + 1)
                wait(dve, v_done, (n - 1) * SB)
                dve.scalar_tensor_tensor(out=x_lo[:, par, :], in0=xT[:, par, :], scalar=t["scale"][:, CX:CX + 1],
                                         in1=x_hi[:, par, :], op0=ALU.mult, op1=ALU.subtract).then_inc(x_lo_ready, 1)

            def step(b, par, now, before):
                n, m = b + 1, b - 1
                if before is None:
                    split_x(0, 0)
                for slot in range(H):
                    if now["attend"]:
                        dve.wait_ge(scores_done, b * H + slot + 1)
                        if isinstance(b, int) and b * H + slot >= 2 or not isinstance(b, int):
                            dve.wait_ge(exp_done, b * H + slot - 1)
                        hp = slot % 2
                        dve.tensor_reduce(row_max[:, hp], ps_s[:, 2 * hp:2 * hp + 2], AX, ALU.max).then_inc(max_done, 1)
                        dve.wait_ge(max_done, b * H + slot + 1)
                        dve.tensor_tensor(neg_bias[:, hp], row_max[:, hp], t["neg_score_scale"][:].unsqueeze(2).broadcast_to([P, 2, SB]),
                                          ALU.mult).then_inc(bias_ready, 1)
                    mix = lagging(b, par, slot, MIX_LAG, now)
                    if mix is not None:
                        q, h, _ = mix
                        hp = h % 2
                        dve.wait_ge(exp_done, q * H + h + 1)
                        dve.reciprocal(inv[:, hp], sums[:, hp]).then_inc(inv_done, 1)
                        dve.wait_ge(inv_done, q * H + h + 1)
                        dve.tensor_tensor(coef[:, hp], inv[:, hp], t["mix_factor"][:, h, :].unsqueeze(2).broadcast_to([P, 2, SB]),
                                          ALU.mult).then_inc(coef_ready, 1)
                    at = (n, slot - QK_LO_LAG) if slot >= QK_LO_LAG and now["project"] else (
                        (b, slot - QK_LO_LAG + H) if slot < QK_LO_LAG and before is not None and before["project"] else None)
                    if at is not None:
                        q, k = at
                        blk, which = k // 4, k % 4
                        dve.wait_ge(qk_hi, q * H + k + 1)
                        dst = qk[:, blk % 2, :, which % 2, which // 2, :]
                        dve.tensor_tensor(dst[:, 1, :], ps_g[:, BANK["qk", k], 0:S], dst[:, 0, :], ALU.subtract).then_inc(qk_lo, 1)
                    if (at := lagging(b, par, slot, O_LO_LAG, now)) is not None and at[1] % PER_BLK == PER_BLK - 1:
                        q, h, _ = at
                        blk = h // PER_BLK
                        dve.wait_ge(o_hi_ready, q * NBLK + blk + 1)
                        dve.tensor_tensor(o_lo[:, blk, :], ps_o[:, 0:S], o_hi[:, blk, :], ALU.subtract).then_inc(o_lo_ready, 1)
                    if mix is not None:
                        q, h, _ = mix
                        hp = h % 2
                        dve.wait_ge(scaled2_ready, q * H + h + 1)
                        wait(dve, tr_done, q * H + h - 1)
                        for s in range(SB):
                            ins = dve.scalar_tensor_tensor(out=mixed[:, hp, s, :], in0=probs[:, hp, 0, s, :], scalar=coef[:, hp, 0, s:s + 1],
                                                           in1=scaled2[:, hp, s, :], op0=ALU.mult, op1=ALU.add)
                        ins.then_inc(mix_done, 1)
                    if now["close"] and slot - 1 in O_SLOTS:
                        s = O_SLOTS.index(slot - 1)
                        dve.wait_ge(proj_done, m * SB + s + 1)
                        if s == 0:
                            dve.wait_ge(rows_loaded, (m + 1) * 16)
                            if isinstance(b, int):
                                wait(dve, y1_ready, m * SB)
                        dve.scalar_tensor_tensor(out=resid[:, s, :], in0=ps_g[:, BANK["o", s], :], scalar=t["attn_unscale"][:, 0:1],
                                                 in1=x_rows[:, s, :], op0=ALU.mult, op1=ALU.add).then_inc(resid_done, 1)
                        dve.wait_ge(resid_done, m * SB + s + 1)
                        dve.bn_stats(stats[:, s, :], resid[:, s, :]).then_inc(stats_done, 1)
                        wait_alone(dve, stats_done, m * SB + s + 1, passed)
                        dve.bn_aggr(moments[:, s, :], stats[:, s, :]).then_inc(moments_done, 1)
                    if now["project"] and slot == 7:
                        dve.wait_ge(chunk_loaded, (n + 1) * 16)
                        dve.tensor_reduce(t["w_sums"][:, ds(n, 1), :], w_chunk[:].unsqueeze(1), AX, ALU.add,
                                          apply_absolute_value=True).then_inc(chunk_summed, 1)
                    if now["close"] and slot == 9:
                        dve.wait_ge(rstd_chain, (m + 1) * RSQRT_STEPS)
                        if isinstance(b, int):
                            wait(dve, yT_done, (m - 1) * 2)
                            wait(dve, y1_stored, (m - 1) * 16)
                        for s in range(SB):
                            dve.tensor_scalar(y1[:, 1 - par, s, :], resid[:, s, :], moments[:, s, 0:1], rstd[:, s:s + 1],
                                              ALU.subtract, ALU.mult).then_inc(y1_ready, 1)
                    if now["project"] and slot == H - 1:
                        split_x(n + 1, par)

            steps(dve, step)
            dve.wait_ge(y1_ready, B * SB)


FW = WCOLS // FILTERS
GROUPS = KC * B


def convolution(nc, t, d):
    with ExitStack() as ctx:
        sb = lambda name, shape, dt: ctx.enter_context(nc.sbuf_tensor(name, shape, dt))
        sem = lambda name: ctx.enter_context(nc.semaphore(name))
        ctx_T = sb("ctx_T", [P, GROUPS, S], F32)
        skip = sb("skip", [P, S], F32)
        toep = sb("toep", [P, 2, 2, D], F16)
        prod = sb("prod", [P, 2, GROUPS, CH, CH], F32)
        prod_hi = sb("prod_hi", [P, 2, GROUPS, CH, CH], F16)
        prod_lo = sb("prod_lo", [P, 2, GROUPS, CH, CH], F16)
        gated = sb("gated", [P, GROUPS, CH, CH], F32)
        summed = sb("summed", [P, GROUPS, CH], F32)
        vx = sb("vx", [P, GROUPS, CH], F32)
        vxs = sb("vxs", [P, 2, GROUPS, CH], F32)
        u = sb("u", [P, 2, GROUPS], F32)
        skip_term = sb("skip_term", [P, 2, GROUPS, CH], F32)
        w_part = sb("w_part", [P, 2, 3, FW], F32)
        below = sb("below", [P, 3, FW], F16)
        cmax = sb("cmax", [P, KC + 1], F32)
        call_max = sb("call_max", [P, 1], F32)
        wsum = sb("wsum", [P, 3], F32)
        wall = sb("wall", [P, 3], F32)
        limit = sb("limit", [P, 2, 3], F32)
        tmp = sb("conv_tmp", [P, 4], F32)
        ps = ctx.enter_context(nc.psum_tensor("ps_conv", [P, 2, KC, 512], F32))

        ctx_loaded = [sem(f"ctx_loaded{c}") for c in range(KC)]
        skip_loaded, toep_loaded, part_loaded = sem("skip_loaded"), sem("toep_loaded"), sem("part_loaded")
        conv_chain, cmax_ready, wsum_ready, all_ready, ctx_scaled = (
            sem("conv_chain"), sem("cmax_ready"), sem("wsum_ready"), sem("all_ready"), sem("ctx_scaled"))
        prod_ready, hi_ready, lo_ready, conv_done, gated_done, summed_done = (
            sem("prod_ready"), sem("hi_ready"), sem("lo_ready"), sem("conv_done"), sem("gated_done"), sem("summed_done"))
        vx_done, vxs_done, u_done, skip_done, out_done = sem("vx_done"), sem("vxs_done"), sem("u_done"), sem("skip_done"), sem("out_done")
        below_done, ternary_done = sem("below_done"), sem("ternary_done")
        passed = sem("passed_convolution")
        block = ctx.enter_context(nc.Block())
        y1T = t["y1T"][:].rearrange("p c b s -> p (c b) s")
        conv_T = t["conv_T"]

        @block.sync
        def _(sp):
            for c in range(KC):
                sp.dma_start(ctx_T[:, c * B:c * B + B, :], d["ctxT"][:, c * B:c * B + B, :]).then_inc(ctx_loaded[c], 16)
            sp.dma_start(skip[:], d["skip"].rearrange("(o n) -> o n", o=1).broadcast_to([P, S])).then_inc(skip_loaded, 16)

            def load(h, par):
                wait_alone(sp, conv_done, (h - 1) * KC, passed)
                wait_alone(sp, toep_loaded, h * 16, passed)
                sp.dma_start(toep[:, par, :, :].unsqueeze(1), d["toeplitz"][ds(h, 1)].rearrange("o a p n -> p o a n")).then_inc(toep_loaded, 16)
                wait_alone(sp, ternary_done, (h - 1) * 3, passed)
                wait_alone(sp, part_loaded, h * 16, passed)
                sp.dma_start(w_part[:, par], d["wffn"][:, :, ds(h * FW, FW)]).then_inc(part_loaded, 16)

            sp.wait_ge(t["toep_written"], 32)
            filters(sp, load)

        @block.tensor
        def _(pe):
            def conv(h, par):
                wait(pe, gated_done, (h - 1) * 2)
                pe.wait_ge(toep_loaded, (h + 1) * 16)
                pe.wait_ge(hi_ready, h + 1)
                rhs = lambda half, mb: half[:, par, mb * B:mb * B + B].rearrange("p b i j -> p (b i j)")
                for lb in range(KC):
                    terms = [(w, half, mb) for w, half in ((0, prod_hi), (1, prod_hi), (0, prod_lo)) for mb in range(lb + 1)]
                    for k, (w, half, mb) in enumerate(terms):
                        if lb == 0 and half is prod_lo:
                            pe.wait_ge(lo_ready, h + 1)
                        at = (lb - mb) * P
                        ins = pe.matmul(ps[:, par, lb, :], toep[:, par, w, at:at + P], rhs(half, mb),
                                        start=(k == 0), stop=(k == len(terms) - 1))
                    ins.then_inc(conv_done, 1)

            filters(pe, conv)

        of_filter = lambda tile, h: tile[:, :, ds(h * CH, CH)]
        rows_of = lambda at: at.unsqueeze(3).broadcast_to([P, GROUPS, CH, CH])
        cols_of = lambda at: at.unsqueeze(2).broadcast_to([P, GROUPS, CH, CH])

        @block.scalar
        def _(act):
            def split(h, par):
                act.wait_ge(prod_ready, h + 1)
                wait(act, conv_done, (h - 1) * KC)
                act.copy(prod_hi[:, par], prod[:, par]).then_inc(hi_ready, 1)

            filters(act, split)

        @block.gpsimd
        def _(pool):
            pool.wait_ge(cmax_ready, 1)
            pool.partition_all_reduce(call_max[:], cmax[:, KC:KC + 1], P, RMAX).then_inc(all_ready, 1)
            pool.wait_ge(wsum_ready, 1)
            pool.partition_all_reduce(wall[:], wsum[:], P, RADD).then_inc(all_ready, 1)
            pool.wait_ge(ctx_scaled, 2)

            def step(h, par):
                wait_alone(pool, hi_ready, h + 1, passed)
                wait_alone(pool, conv_done, (h - 1) * KC, passed)
                pool.tensor_tensor(prod_lo[:, par], prod[:, par], prod_hi[:, par], ALU.subtract).then_inc(lo_ready, 1)
                wait_alone(pool, vxs_done, h, passed)
                pool.tensor_tensor(vx[:], of_filter(y1T, h), of_filter(ctx_T, h), ALU.mult).then_inc(vx_done, 1)
                wait_alone(pool, vx_done, h + 1, passed)
                wait_alone(pool, u_done, h - 1, passed)
                pool.tensor_tensor(vxs[:, par], vx[:], skip[:, ds(h * CH, CH)].unsqueeze(1).broadcast_to([P, GROUPS, CH]),
                                   ALU.mult).then_inc(vxs_done, 1)
                wait_alone(pool, u_done, h + 1, passed)
                wait_alone(pool, out_done, h - 1, passed)
                pool.tensor_tensor(skip_term[:, par], of_filter(ctx_T, h), u[:, par].unsqueeze(2).broadcast_to([P, GROUPS, CH]),
                                   ALU.mult).then_inc(skip_done, 1)

            filters(pool, step)

        @block.vector
        def _(dve):
            ch = Chain(dve, conv_chain)
            for c in range(KC):
                dve.wait_ge(ctx_loaded[c], 16)
                ch.then(dve.tensor_reduce(cmax[:, c:c + 1], ctx_T[:, c * B:c * B + B, :].rearrange("p b s -> p (b s)"), AX, ALU.max,
                                          apply_absolute_value=True))
            dve.tensor_reduce(cmax[:, KC:KC + 1], cmax[:, 0:KC], AX, ALU.max).then_inc(cmax_ready, 1)
            dve.tensor_reduce(wsum[:], t["w_sums"][:].rearrange("p b k -> p k b"), AX, ALU.add).then_inc(wsum_ready, 1)
            dve.wait_ge(all_ready, 1)
            ch.then(dve.tensor_scalar(call_max[:], call_max[:], 1e-30, None, ALU.max))
            ch.then(dve.tensor_scalar(tmp[:, 0:1].bitcast(I32), call_max[:].bitcast(I32), EXP_MASK, None, ALU.bitwise_and))
            ch.then(dve.reciprocal(tmp[:, 1:2], tmp[:, 0:1]))
            ch.then(dve.tensor_scalar(tmp[:, 1:2], tmp[:, 1:2], 512.0, None, ALU.mult))
            for c in range(KC):
                ins = dve.tensor_scalar(ctx_T[:, c * B:c * B + B, :], ctx_T[:, c * B:c * B + B, :], tmp[:, 1:2], None, ALU.mult)
                ch.then(ins)
            dve.nop().then_inc(ctx_scaled, 1)
            dve.wait_ge(skip_loaded, 16)
            ch.then(dve.tensor_scalar(skip[:], skip[:], t["scale"][:, CK:CK + 1], None, ALU.mult))
            dve.nop().then_inc(ctx_scaled, 1)
            ch.then(dve.tensor_scalar(tmp[:, 2:3], tmp[:, 0:1], 1.0 / 512.0, None, ALU.mult))
            ch.then(dve.tensor_tensor(tmp[:, 3:4], tmp[:, 2:3], tmp[:, 2:3], ALU.mult))
            ch.then(dve.tensor_tensor(t["conv_unscale"][:], tmp[:, 3:4], t["unscale"][:, CK:CK + 1], ALU.mult))
            dve.wait_ge(all_ready, 2)
            ch.then(dve.tensor_scalar(t["w_mean"][:], wall[:], float(np.float32(1.0 / (HID * D))), None, ALU.mult))
            ch.then(dve.tensor_scalar(limit[:, 0, :], t["w_mean"][:], 0.5, None, ALU.mult))
            ch.then(dve.tensor_scalar(limit[:, 1, :], t["w_mean"][:], -0.5, None, ALU.mult))

            def product(h, par):
                wait(dve, lo_ready, h - 1)
                dve.tensor_tensor(prod[:, par], rows_of(of_filter(y1T, h)), cols_of(of_filter(ctx_T, h)), ALU.mult).then_inc(prod_ready, 1)

            def step(h, par):
                if not isinstance(h, int) or h < FILTERS - 1:
                    product(h + 1, 1 - par)
                dve.wait_ge(part_loaded, (h + 1) * 16)
                for k in range(3):
                    if isinstance(h, int) and h > 0 or not isinstance(h, int):
                        dve.wait_ge(ternary_done, (h - 1) * 3 + k + 1)
                    dve.tensor_scalar(below[:, k, :], w_part[:, par, k, :], limit[:, 1, k:k + 1], None, ALU.is_lt).then_inc(below_done, 1)
                for k in range(3):
                    dve.wait_ge(below_done, h * 3 + k + 1)
                    dve.scalar_tensor_tensor(out=t["ternary"][:, k, ds(h * FW, FW)], in0=w_part[:, par, k, :], scalar=limit[:, 0, k:k + 1],
                                             in1=below[:, k, :], op0=ALU.is_gt, op1=ALU.subtract).then_inc(ternary_done, 1)
                dve.wait_ge(vxs_done, h + 1)
                wait(dve, skip_done, h - 1)
                dve.tensor_reduce(u[:, par], vxs[:, par], AX, ALU.add).then_inc(u_done, 1)
                wait(dve, summed_done, h)
                x1 = ctx_T[:].rearrange("p (c b) s -> p c b s", c=KC)
                for k in range(2):
                    dve.wait_ge(conv_done, h * KC + 2 * k + 2)
                    half = GROUPS // 2
                    dve.tensor_tensor(gated[:, k * half:(k + 1) * half], ps[:, par, 2 * k:2 * k + 2, :].rearrange("p c (b i j) -> p (c b) i j", b=B, i=CH),
                                      ctx_T[:, k * half:(k + 1) * half, ds(h * CH, CH)].unsqueeze(3).broadcast_to([P, half, CH, CH]),
                                      ALU.mult).then_inc(gated_done, 1)
                dve.wait_ge(gated_done, h * 2 + 2)
                wait(dve, out_done, h)
                dve.tensor_reduce(summed[:], gated[:].rearrange("p g i j -> p g j i"), AX, ALU.add).then_inc(summed_done, 1)
                dve.wait_ge(summed_done, h + 1)
                dve.wait_ge(skip_done, h + 1)
                dve.tensor_tensor(of_filter(conv_T, h), summed[:], skip_term[:, par], ALU.add).then_inc(out_done, 1)

            product(0, 0)
            filters(dve, step)
            dve.wait_ge(out_done, FILTERS)
            dve.wait_ge(ternary_done, 3 * FILTERS)


def filters(eng, step):
    step(0, 0)
    step(1, 1)
    with eng.Fori(2, FILTERS - 3, 2) as h:
        step(h, 0)
        step(h + 1, 1)
    step(FILTERS - 2, 0)
    step(FILTERS - 1, 1)


OUT_LAG = 2


def feed_forward(nc, t, d):
    with ExitStack() as ctx:
        sb = lambda name, shape, dt: ctx.enter_context(nc.sbuf_tensor(name, shape, dt))
        sem = lambda name: ctx.enter_context(nc.semaphore(name))
        ident = t["ident"]
        conv_b = sb("conv_b", [P, 2, KC, S], F32)
        y1 = sb("y1_back", [P, 2, SB, D], F32)
        resid = sb("resid2", [P, SB, D], F32)
        resid3 = sb("resid3", [P, SB, D], F32)
        stats = sb("stats2", [P, 2, SB, 6], F32)
        moments = sb("moments2", [P, 2, SB, 2], F32)
        rstd = sb("rstd2", [P, 2, SB], F32)
        nt = [sb(f"newton2_{k}", [P, SB], F32) for k in range(2)]
        y2 = sb("y2", [P, 2, SB, D], F32)
        y2_hi = sb("y2_hi", [P, 2, KC, S], F16)
        y2_lo = sb("y2_lo", [P, 2, KC, S], F16)
        th = sb("th", [P, 2, S], F32)
        act_h1 = sb("act_h1", [P, 2, S], F32)
        g = sb("g", [P, 2, S], F32)
        g_hi = sb("g_hi", [P, 4, S], F16)
        g_lo = sb("g_lo", [P, 4, S], F16)
        out = sb("out", [P, 2, SB, D], F32)
        scal = sb("ffn_scal", [P, 2], F32)
        ps_f = ctx.enter_context(nc.psum_tensor("ps_f", [P, 2, 512], F32))
        ps_h = ctx.enter_context(nc.psum_tensor("ps_h", [P, 4, 2, S], F32))
        ps_y = ctx.enter_context(nc.psum_tensor("ps_y", [P, SB, D], F32))

        conv_loaded, y1_loaded, stored = sem("conv_loaded"), sem("y1_loaded"), sem("stored")
        scal_chain, scal_ready = sem("scal_chain"), sem("scal_ready")
        back_done, resid_done, stats_done, moments_done = sem("back_done"), sem("resid2_done"), sem("stats2_done"), sem("moments2_done")
        rstd_chain, y2_ready, y2T_done, y2_hi_ready, y2_lo_ready = (
            sem("rstd2_chain"), sem("y2_ready"), sem("y2T_done"), sem("y2_hi_ready"), sem("y2_lo_ready"))
        h_done, th_ready, h1_ready, g_ready, g_hi_ready, g_lo_ready, y_done = (
            sem("h_done"), sem("th_ready"), sem("h1_ready"), sem("g_ready"), sem("g_hi_ready"), sem("g_lo_ready"), sem("y_done"))
        resid3_done, stats3_done, moments3_done, rstd3_chain, out_ready = (
            sem("resid3_done"), sem("stats3_done"), sem("moments3_done"), sem("rstd3_chain"), sem("out_ready"))
        passed = sem("passed_feed_forward")
        block = ctx.enter_context(nc.Block())
        conv_T = t["conv_T"][:].rearrange("p (c b) s -> p c b s", c=KC)
        w13 = t["ternary"][:].rearrange("p k (c n) -> p k c n", c=KC)
        w2 = t["ternary"][:, 2, :].rearrange("p (c n) -> p c n", c=HC)

        def steps(eng, step):
            step(-1, 1, True, False)
            step(0, 0, True, True)
            step(1, 1, True, True)
            with eng.Fori(2, B - 3, 2) as b:
                step(b, 0, True, True)
                step(b + 1, 1, True, True)
            step(B - 2, 0, True, True)
            step(B - 1, 1, False, True)

        @block.sync
        def _(sp):
            def store(m, par):
                wait_alone(sp, out_ready, (m + 1) * SB, passed)
                sp.dma_start(d["out"][ds(m, 1)].rearrange("o (s p) n -> p o s n", p=P),
                             out[:, par, :, :].rearrange("p (o s) n -> p o s n", o=1)).then_inc(stored, 16)
                wait_alone(sp, stored, (m + 1) * 16, passed)

            def step(b, par, front, main):
                if front:
                    n = b + 1
                    wait_alone(sp, back_done, (n - 1) * SB, passed)
                    wait_alone(sp, resid_done, (n - 1) * SB, passed)
                    wait_alone(sp, conv_loaded, n * 16, passed)
                    sp.dma_start(conv_b[:, 1 - par].unsqueeze(2), conv_T[:, :, ds(n, 1), :]).then_inc(conv_loaded, 16)
                    wait_alone(sp, y1_loaded, n * 16, passed)
                    sp.dma_start(y1[:, 1 - par].rearrange("p (o s) n -> p o s n", o=1),
                                 d["y1_rows"][ds(n, 1)].rearrange("o (s p) n -> p o s n", p=P)).then_inc(y1_loaded, 16)
                if main and not (isinstance(b, int) and b == 0):
                    store(b - 1, 1 - par)

            steps(sp, step)
            store(B - 1, 1)

        @block.tensor
        def _(pe):
            def back(n, par):
                pe.wait_ge(conv_loaded, (n + 1) * 16)
                for s in range(SB):
                    wait(pe, y2_lo_ready, n * 2)
                    for c in range(KC):
                        ins = pe.matmul(ps_f[:, s, c * P:c * P + P], conv_b[:, par, c, s * P:s * P + P], ident[:],
                                        start=True, stop=True, is_transpose=True, skip_group_check=True)
                    ins.then_inc(back_done, 1)

            def y2_transposes(n, par):
                pe.wait_ge(y2_ready, (n + 1) * SB)
                for k in range(2):
                    for c in range(2):
                        for s in range(SB):
                            ins = pe.matmul(ps_f[:, k, c * S + s * P:c * S + s * P + P], y2[:, par, s, (2 * k + c) * P:(2 * k + c + 1) * P],
                                            ident[:], start=True, stop=True, is_transpose=True, skip_group_check=True)
                    ins.then_inc(y2T_done, 1)

            def hidden(b, par, c):
                wait(pe, g_ready, b * HC + c - 3)
                for k in range(2):
                    for kc in range(KC):
                        for half, x in enumerate((y2_hi, y2_lo)):
                            ins = pe.matmul(ps_h[:, c % 4, k, :], w13[:, k, kc, c * P:c * P + P], x[:, par, kc, :],
                                            start=(kc == 0 and half == 0), stop=(kc == KC - 1 and half == 1), skip_group_check=True)
                ins.then_inc(h_done, 1)

            def down(b, par, c):
                pe.wait_ge(g_lo_ready, b * HC + c + 1)
                if c == 0:
                    wait(pe, resid3_done, b * SB)
                for s in range(SB):
                    for half, x in enumerate((g_hi, g_lo)):
                        ins = pe.matmul(ps_y[:, s, :], x[:, c % 4, s * P:s * P + P], w2[:, c, :],
                                        start=(c == 0 and half == 0), stop=(c == HC - 1 and half == 1), skip_group_check=True)
                    if c == HC - 1:
                        ins.then_inc(y_done, 1)

            def step(b, par, front, main):
                if not main:
                    back(b + 1, 1 - par)
                    y2_transposes(b + 1, 1 - par)
                    return
                pe.wait_ge(y2_lo_ready, (b + 1) * 2)
                for c in range(HC + OUT_LAG):
                    if c < HC:
                        hidden(b, par, c)
                    if c == 1 and front:
                        back(b + 1, 1 - par)
                    if c == 8 and front:
                        y2_transposes(b + 1, 1 - par)
                    if c >= OUT_LAG:
                        down(b, par, c - OUT_LAG)

            steps(pe, step)

        @block.scalar
        def _(act):
            act.wait_ge(scal_ready, 1)
            tanh_scale = act.alloc_register("tanh_scale")
            act.reg_load(tanh_scale, scal[0:1, 0:1].bitcast(I32))

            def y2_split(n, par):
                for k in range(2):
                    act.wait_ge(y2T_done, n * 2 + k + 1)
                    if k == 0:
                        wait(act, h_done, (n - 1) * HC)
                    act.activation(y2_hi[:, par, 2 * k:2 * k + 2, :], ps_f[:, k, :].rearrange("p (c s) -> p c s", c=2), ACT.Copy,
                                   scale=Y2_SCALE).then_inc(y2_hi_ready, 1)

            def step(b, par, front, main):
                if not main:
                    y2_split(b + 1, 1 - par)
                    return
                for c in range(HC + 1):
                    if c < HC:
                        u = b * HC + c
                        act.wait_ge(h_done, u + 1)
                        wait(act, h1_ready, u - 1)
                        act.activation(th[:, c % 2, :], ps_h[:, c % 4, 0, :], ACT.Tanh, scale=tanh_scale).then_inc(th_ready, 1)
                    if c >= 1:
                        u = b * HC + c - 1
                        act.wait_ge(g_ready, u + 1)
                        act.copy(g_hi[:, (c - 1) % 4, :], g[:, (c - 1) % 2, :]).then_inc(g_hi_ready, 1)
                    if c == 9 and front:
                        y2_split(b + 1, 1 - par)

            steps(act, step)

        @block.gpsimd
        def _(pool):
            def step(b, par, front, main):
                n = b + 1
                if not main:
                    wait_alone(pool, moments_done, (n + 1) * SB, passed)
                    rsqrt(Chain(pool, rstd_chain, n * RSQRT_STEPS, passed), pool, rstd[:, 0], moments[:, 0, :, 1], nt)
                    return
                for c in range(HC):
                    if c == 4 and front:
                        wait_alone(pool, moments_done, (n + 1) * SB, passed)
                        rsqrt(Chain(pool, rstd_chain, n * RSQRT_STEPS, passed), pool, rstd[:, 0], moments[:, 0, :, 1], nt)
                    u = b * HC + c
                    wait_alone(pool, g_hi_ready, u + 1, passed)
                    pool.tensor_tensor(g_lo[:, c % 4, :], g[:, c % 2, :], g_hi[:, c % 4, :], ALU.subtract).then_inc(g_lo_ready, 1)
                wait_alone(pool, moments3_done, (b + 1) * SB, passed)
                rsqrt(Chain(pool, rstd3_chain, b * RSQRT_STEPS, passed), pool, rstd[:, 1], moments[:, 1, :, 1], nt)

            steps(pool, step)

        @block.vector
        def _(dve):
            ch = Chain(dve, scal_chain)
            mean = t["w_mean"]
            ch.then(dve.tensor_scalar(scal[:, 0:1], mean[:, 0:1], 0.5 / Y2_SCALE, None, ALU.mult))
            ch.then(dve.tensor_tensor(scal[:, 1:2], mean[:, 0:1], mean[:, 1:2], ALU.mult))
            ch.then(dve.tensor_scalar(scal[:, 1:2], scal[:, 1:2], mean[:, 2:3], 0.5 / (Y2_SCALE * Y2_SCALE * G_SCALE), ALU.mult, ALU.mult))
            dve.nop().then_inc(scal_ready, 1)

            def normalise_in(n, par):
                dve.wait_ge(y1_loaded, (n + 1) * 16)
                for s in range(SB):
                    dve.wait_ge(back_done, n * SB + s + 1)
                    dve.scalar_tensor_tensor(out=resid[:, s, :], in0=ps_f[:, s, :], scalar=t["conv_unscale"][:, 0:1], in1=y1[:, par, s, :],
                                             op0=ALU.mult, op1=ALU.add).then_inc(resid_done, 1)
                    dve.wait_ge(resid_done, n * SB + s + 1)
                    dve.bn_stats(stats[:, 0, s, :], resid[:, s, :]).then_inc(stats_done, 1)
                    wait_alone(dve, stats_done, n * SB + s + 1, passed)
                    dve.bn_aggr(moments[:, 0, s, :], stats[:, 0, s, :]).then_inc(moments_done, 1)

            def normalise_out(n, par):
                dve.wait_ge(rstd_chain, (n + 1) * RSQRT_STEPS)
                for s in range(SB):
                    dve.tensor_scalar(y2[:, par, s, :], resid[:, s, :], moments[:, 0, s, 0:1], rstd[:, 0, s:s + 1],
                                      ALU.subtract, ALU.mult).then_inc(y2_ready, 1)

            def y2_split(n, par):
                for k in range(2):
                    dve.wait_ge(y2_hi_ready, n * 2 + k + 1)
                    dve.scalar_tensor_tensor(out=y2_lo[:, par, 2 * k:2 * k + 2, :], in0=ps_f[:, k, :].rearrange("p (c s) -> p c s", c=2),
                                             scalar=Y2_SCALE, in1=y2_hi[:, par, 2 * k:2 * k + 2, :], op0=ALU.mult, op1=ALU.subtract)\
                       .then_inc(y2_lo_ready, 1)

            def step(b, par, front, main):
                n = b + 1
                if not main:
                    normalise_in(n, 1 - par)
                    normalise_out(n, 1 - par)
                    y2_split(n, 1 - par)
                    return
                for c in range(HC):
                    u = b * HC + c
                    dve.wait_ge(th_ready, u + 1)
                    dve.scalar_tensor_tensor(out=act_h1[:, c % 2, :], in0=th[:, c % 2, :], scalar=1.0, in1=ps_h[:, c % 4, 0, :],
                                             op0=ALU.add, op1=ALU.mult).then_inc(h1_ready, 1)
                    dve.wait_ge(h1_ready, u + 1)
                    wait(dve, g_lo_ready, u - 1)
                    dve.scalar_tensor_tensor(out=g[:, c % 2, :], in0=act_h1[:, c % 2, :], scalar=G_SCALE, in1=ps_h[:, c % 4, 1, :],
                                             op0=ALU.mult, op1=ALU.mult).then_inc(g_ready, 1)
                    if c == 2 and front:
                        normalise_in(n, 1 - par)
                    if c == 6 and front:
                        normalise_out(n, 1 - par)
                    if c == HC - 1 and front:
                        y2_split(n, 1 - par)
                for s in range(SB):
                    dve.wait_ge(y_done, b * SB + s + 1)
                    dve.scalar_tensor_tensor(out=resid3[:, s, :], in0=ps_y[:, s, :], scalar=scal[:, 1:2], in1=y2[:, par, s, :],
                                             op0=ALU.mult, op1=ALU.add).then_inc(resid3_done, 1)
                    dve.wait_ge(resid3_done, b * SB + s + 1)
                    dve.bn_stats(stats[:, 1, s, :], resid3[:, s, :]).then_inc(stats3_done, 1)
                    wait_alone(dve, stats3_done, b * SB + s + 1, passed)
                    dve.bn_aggr(moments[:, 1, s, :], stats[:, 1, s, :]).then_inc(moments3_done, 1)
                dve.wait_ge(rstd3_chain, (b + 1) * RSQRT_STEPS)
                if not isinstance(b, int) or b >= 2:
                    dve.wait_ge(stored, (b - 1) * 16)
                for s in range(SB):
                    dve.tensor_scalar(out[:, par, s, :], resid3[:, s, :], moments[:, 1, s, 0:1], rstd[:, 1, s:s + 1],
                                      ALU.subtract, ALU.mult).then_inc(out_ready, 1)

            steps(dve, step)


def build(nc, d):
    t = {}
    with ExitStack() as ctx:
        def keep(scope, name, shape, dt=F32):
            t[name] = scope.enter_context(nc.sbuf_tensor(name, shape, dt))

        keep(ctx, "ident", [P, P])
        keep(ctx, "scale", [P, NMAX])
        keep(ctx, "unscale", [P, NMAX])
        keep(ctx, "score_scale", [P, 2])
        keep(ctx, "neg_score_scale", [P, 2])
        keep(ctx, "attn_unscale", [P, 1])
        keep(ctx, "conv_unscale", [P, 1])
        keep(ctx, "mix_factor", [P, H, 2])
        keep(ctx, "w_sums", [P, B, 3])
        keep(ctx, "w_mean", [P, 3])
        keep(ctx, "y1T", [P, KC, B, S])
        t["toep_written"] = ctx.enter_context(nc.semaphore("toep_written"))
        with ExitStack() as first:
            keep(first, "w_hi", [P, 6, KC * D], F16)
            keep(first, "w_lo", [P, 6, KC * D], F16)
            prepare(nc, t, d)
            attention(nc, t, d)
        keep(ctx, "conv_T", [P, GROUPS, S])
        keep(ctx, "ternary", [P, 3, WCOLS], F16)
        convolution(nc, t, d)
        feed_forward(nc, t, d)


def kernel(x, fside_S2_0, ctx_2048, L0_attn_q1_w, L0_attn_k1_w, L0_attn_q2_w, L0_attn_k2_w, L0_attn_v_w, L0_attn_o_w,
           L0_attn_lambda_param, L0_xattn_k, L0_ffn_w1, L0_ffn_w3, L0_ffn_w2):
    import concourse.bacc as bacc
    from concourse.bass_utils import run_bass_kernel_spmd

    f = lambda a: np.asarray(a)
    chunks = lambda a: a.reshape(-1, P, a.shape[1]).transpose(1, 0, 2)
    x = f(x)
    xT = x.transpose(2, 0, 1).reshape(KC, P, B, S).transpose(1, 2, 0, 3).reshape(P, B * KC * S)
    xT = np.concatenate([xT, np.zeros((P, KC * S), xT.dtype)], axis=1)
    ctxT = f(ctx_2048).transpose(2, 0, 1).reshape(KC, P, B, S).transpose(1, 0, 2, 3).reshape(P, KC * B, S)
    wproj = np.stack([chunks(f(w).T) for w in (L0_attn_q1_w, L0_attn_k1_w, L0_attn_q2_w, L0_attn_k2_w, L0_attn_v_w, L0_attn_o_w)], axis=1)
    pad = lambda a, n, axis: np.concatenate([a, np.zeros([n - s if i == axis else s for i, s in enumerate(a.shape)], a.dtype)], axis=axis)
    w1, w3 = (chunks(pad(f(w).T, HC * P, 1)).reshape(P, WCOLS) for w in (L0_ffn_w1, L0_ffn_w3))
    w2 = chunks(pad(f(L0_ffn_w2).T, HC * P, 0)).reshape(P, WCOLS)
    filt = f(L0_xattn_k)
    filt = np.concatenate([np.zeros((FILTERS, P), filt.dtype), filt], axis=1)
    arrays = {"x": x, "xT": xT, "ctxT": ctxT, "skip": f(fside_S2_0), "wproj": wproj.reshape(P, 6, KC * D), "lam": f(L0_attn_lambda_param),
              "filt": filt, "wffn": np.stack([w1, w3, w2], axis=1)}
    arrays = {k: np.ascontiguousarray(a) for k, a in arrays.items()}

    nc = bacc.Bacc("TRN2", target_bir_lowering=False, num_devices=1)
    d = {k: nc.dram_tensor(f"in_{k}", a.shape, mybir.dt.from_np(a.dtype), kind="ExternalInput").ap() for k, a in arrays.items()}
    d["out"] = nc.dram_tensor("out_y", (B, S, D), F32, kind="ExternalOutput").ap()
    d["y1_rows"] = nc.dram_tensor("y1_rows", (B, S, D), F32, kind="Internal").ap()
    d["filt_halves"] = nc.dram_tensor("filt_halves_dram", (2, FILTERS, D + P), F16, kind="Internal").ap()
    d["toeplitz"] = nc.dram_tensor("toeplitz", (FILTERS, 2, P, D), F16, kind="Internal").ap()
    build(nc, d)
    r = run_bass_kernel_spmd(nc, [{f"in_{k}": a for k, a in arrays.items()}], core_ids=[0])
    return r.results[0]["out_y"]
```

```python
from contextlib import ExitStack

import numpy as np

import concourse.bass as bass
from concourse import mybir

F32 = mybir.dt.float32
F16 = mybir.dt.float16
I32 = mybir.dt.int32
ALU = mybir.AluOpType
ACT = mybir.ActivationFunctionType
AX = mybir.AxisListType.X
RMAX = bass.bass_isa.ReduceOp.max
RADD = bass.bass_isa.ReduceOp.add
ds = bass.ds

P = 128
B, S, D = 8, 256, 512
H, HD = 16, 32
KC = D // P
SB = S // P
PER_BLK = P // HD
NBLK = H // PER_BLK
FILTERS, CH = 32, 8
CUT = 2
NEAR = (KC - CUT) * P
HID = 1365
HC = -(-HID // P)
WCOLS = KC * HC * P
EPS = 1e-5
EXP_MASK = 0x7F800000
RSQRT_SEED = 1597463007.0
Y2_SCALE = 1024.0
G_SCALE = 2.0 ** -24
CX, CQ1, CK1, CQ2, CK2, CV, CO, CK, CLAM = range(9)
NMAX = 9


def wait(eng, sem, value):
    if not (isinstance(value, int) and value <= 0):
        eng.wait_ge(sem, value)


def wait_alone(eng, sem, value, passed):
    if not (isinstance(value, int) and value <= 0):
        eng.wait_ge(sem, value)
        if not isinstance(value, int):
            eng.sem_inc(passed, 1)


class Chain:

    def __init__(self, eng, sem, base=0, passed=None):
        self.eng, self.sem, self.base, self.passed, self.n = eng, sem, base, passed, 0

    def then(self, ins):
        self.n += 1
        ins.then_inc(self.sem, 1)
        wait_alone(self.eng, self.sem, self.base + self.n, self.passed)


RSQRT_STEPS = 1 + 1 + 3 * 4


def rsqrt(chain, eng, out, var, tmp):
    safe, square = (x[:] for x in tmp)
    chain.then(eng.tensor_scalar(safe, var, EPS, None, ALU.add))
    chain.then(eng.tensor_scalar(out.bitcast(I32), safe.bitcast(I32), -0.5, RSQRT_SEED, ALU.mult, ALU.add))
    for _ in range(3):
        chain.then(eng.tensor_tensor(square, out, out, ALU.mult))
        chain.then(eng.tensor_tensor(square, square, safe, ALU.mult))
        chain.then(eng.tensor_scalar(square, square, -0.5, 1.5, ALU.mult, ALU.add))
        chain.then(eng.tensor_tensor(out, out, square, ALU.mult))


def prepare(nc, t, d):
    with ExitStack() as ctx:
        sb = lambda name, shape, dt: ctx.enter_context(nc.sbuf_tensor(name, shape, dt))
        sem = lambda name: ctx.enter_context(nc.semaphore(name))
        w_stage = sb("w_stage", [P, 6, KC * D], F32)
        x_stage = sb("x_stage", [P, B * KC * S], F32)
        filt = sb("filt", [FILTERS, D + P], F32)
        filt_halves = sb("filt_halves", [FILTERS, 2, D + P], F16)
        filt_whole = sb("filt_whole", [FILTERS, NEAR + P], F32)
        lam = sb("lam", [P, H], F32)
        part_max = sb("part_max", [P, NMAX], F32)
        maxima = sb("maxima", [P, NMAX], F32)
        pow2 = sb("pow2", [P, NMAX], F32)
        tmp = sb("prep_tmp", [P, 4], F32)

        w_loaded = [sem(f"w_loaded{i}") for i in range(6)]
        x_loaded, filt_loaded, lam_loaded = sem("x_all_loaded"), sem("filt_loaded"), sem("lam_loaded")
        max_ready, all_max, scaled = sem("max_ready"), sem("all_max"), sem("scales_ready")
        prep_chain = sem("prep_chain")
        w_hi_ready, w_lo_ready = sem("w_hi_ready"), sem("w_lo_ready")
        filt_hi_ready, filt_lo_ready, filt_stored = sem("filt_hi_ready"), sem("filt_lo_ready"), sem("filt_stored")
        filt_whole_ready = sem("filt_whole_ready")
        ident_zero, ident_ready = sem("ident_zero"), sem("ident_ready")
        block = ctx.enter_context(nc.Block())

        @block.sync
        def _(sp):
            sp.dma_start(filt[:], d["filt"]).then_inc(filt_loaded, 16)
            sp.dma_start(lam[:], d["lam"].rearrange("(o h) -> o h", o=1).broadcast_to([P, H])).then_inc(lam_loaded, 16)
            for i in range(6):
                sp.dma_start(w_stage[:, i, :], d["wproj"][:, i, :]).then_inc(w_loaded[i], 16)
            sp.dma_start(x_stage[:], d["xT"][:, 0:B * KC * S]).then_inc(x_loaded, 16)
            sp.wait_ge(filt_hi_ready, 1)
            sp.wait_ge(filt_lo_ready, 1)
            sp.dma_start(d["filt_halves"].rearrange("a f n -> f a n"), filt_halves[:]).then_inc(filt_stored, 16)
            sp.wait_ge(filt_whole_ready, 1)
            sp.dma_start(d["filt_whole"], filt_whole[:]).then_inc(filt_stored, 16)
            sp.wait_ge(filt_stored, 32)

        @block.gpsimd
        def _(pool):
            pool.memset(t["ident"][:], 0.0).then_inc(ident_zero, 1)
            pool.wait_ge(ident_zero, 1)
            pool.affine_select(out=t["ident"][:], in_=t["ident"][:], compare_op=ALU.not_equal, fill=1.0, base=0,
                               pattern=[[-1, P]], channel_multiplier=1).then_inc(ident_ready, 1)
            pool.wait_ge(max_ready, 1)
            pool.partition_all_reduce(maxima[:], part_max[:], P, RMAX).then_inc(all_max, 1)
            pool.wait_ge(ident_ready, 1)

        @block.scalar
        def _(act):
            act.wait_ge(scaled, 1)
            act.activation(filt_halves[:, 0, :], filt[:], ACT.Copy, scale=t["scale"][0:FILTERS, CK:CK + 1]).then_inc(filt_hi_ready, 1)
            act.activation(filt_whole[:], filt[:, 0:NEAR + P], ACT.Copy, scale=t["scale"][0:FILTERS, CK:CK + 1]).then_inc(filt_whole_ready, 1)
            for i in range(6):
                act.activation(t["w_hi"][:, i, :], w_stage[:, i, :], ACT.Copy, scale=t["scale"][:, CQ1 + i:CQ1 + i + 1]).then_inc(w_hi_ready, 1)

        @block.vector
        def _(dve):
            ch = Chain(dve, prep_chain)
            ch.then(dve.memset(part_max[:], 0.0))
            dve.wait_ge(filt_loaded, 16)
            ch.then(dve.tensor_reduce(part_max[0:FILTERS, CK:CK + 1], filt[:], AX, ALU.max, apply_absolute_value=True))
            dve.wait_ge(lam_loaded, 16)
            ch.then(dve.tensor_reduce(part_max[:, CLAM:CLAM + 1], lam[:], AX, ALU.max, apply_absolute_value=True))
            ch.then(dve.tensor_scalar(part_max[:, CLAM:CLAM + 1], part_max[:, CLAM:CLAM + 1], 1.0, None, ALU.add))
            for i in range(6):
                dve.wait_ge(w_loaded[i], 16)
                ch.then(dve.tensor_reduce(part_max[:, CQ1 + i:CQ1 + i + 1], w_stage[:, i, :], AX, ALU.max, apply_absolute_value=True))
            dve.wait_ge(x_loaded, 16)
            dve.tensor_reduce(part_max[:, CX:CX + 1], x_stage[:], AX, ALU.max, apply_absolute_value=True).then_inc(max_ready, 1)
            dve.wait_ge(all_max, 1)
            ch.then(dve.tensor_scalar(maxima[:], maxima[:], 1e-30, None, ALU.max))
            ch.then(dve.tensor_scalar(pow2[:].bitcast(I32), maxima[:].bitcast(I32), EXP_MASK, None, ALU.bitwise_and))
            ch.then(dve.reciprocal(t["scale"][:], pow2[:]))
            ch.then(dve.tensor_scalar(t["scale"][:, CX:CO + 1], t["scale"][:, CX:CO + 1], 4.0, None, ALU.mult))
            ch.then(dve.tensor_scalar(t["scale"][:, CK:CK + 1], t["scale"][:, CK:CK + 1], 8192.0, None, ALU.mult))
            ch.then(dve.tensor_scalar(t["scale"][:, CLAM:CLAM + 1], t["scale"][:, CLAM:CLAM + 1], 0.5, None, ALU.mult))
            ch.then(dve.reciprocal(t["unscale"][:], t["scale"][:]))
            un = t["unscale"]
            ch.then(dve.tensor_tensor(tmp[:, 0:1], un[:, CX:CX + 1], un[:, CX:CX + 1], ALU.mult))
            ch.then(dve.tensor_tensor(tmp[:, 2:3], un[:, CQ1:CQ1 + 1], un[:, CK1:CK1 + 1], ALU.mult))
            ch.then(dve.tensor_tensor(tmp[:, 3:4], un[:, CQ2:CQ2 + 1], un[:, CK2:CK2 + 1], ALU.mult))
            ch.then(dve.tensor_scalar(t["score_scale"][:], tmp[:, 2:4], tmp[:, 0:1], float(HD) ** -0.5, ALU.mult, ALU.mult))
            ch.then(dve.tensor_tensor(tmp[:, 1:2], un[:, CX:CX + 1], un[:, CLAM:CLAM + 1], ALU.mult))
            ch.then(dve.tensor_tensor(tmp[:, 2:3], un[:, CV:CV + 1], un[:, CO:CO + 1], ALU.mult))
            ch.then(dve.tensor_tensor(t["attn_unscale"][:], tmp[:, 1:2], tmp[:, 2:3], ALU.mult))
            ch.then(dve.memset(t["mix_factor"][:, :, 0], 1.0))
            ch.then(dve.tensor_scalar(t["mix_factor"][:, :, 0], t["mix_factor"][:, :, 0], t["scale"][:, CLAM:CLAM + 1], None, ALU.mult))
            ch.then(dve.tensor_scalar(t["mix_factor"][:, :, 1], lam[:], t["scale"][:, CLAM:CLAM + 1], -1.0, ALU.mult, ALU.mult))
            ch.then(dve.tensor_scalar(t["neg_score_scale"][:], t["score_scale"][:], -1.0, None, ALU.mult))
            dve.nop().then_inc(scaled, 1)
            dve.wait_ge(filt_hi_ready, 1)
            dve.scalar_tensor_tensor(out=filt_halves[:, 1, :], in0=filt[:], scalar=t["scale"][0:FILTERS, CK:CK + 1],
                                     in1=filt_halves[:, 0, :], op0=ALU.mult, op1=ALU.subtract).then_inc(filt_lo_ready, 1)
            for i in range(6):
                dve.wait_ge(w_hi_ready, i + 1)
                dve.scalar_tensor_tensor(out=t["w_lo"][:, i, :], in0=w_stage[:, i, :], scalar=t["scale"][:, CQ1 + i:CQ1 + i + 1],
                                         in1=t["w_hi"][:, i, :], op0=ALU.mult, op1=ALU.subtract).then_inc(w_lo_ready, 1)



COEF_LAG, MIX_LAG, TR_LAG, PV_LAG, O_LO_LAG = 1, 2, 3, 4, 5
O_SLOTS, RESID_SLOTS, STATS_SLOTS, Y1_SLOTS, YT_SLOTS = (5, 7), (6, 8), (7, 9), (11, 12), (13, 15)
V_SLOTS = (9, 11)
SUM_SLOTS = (3, 5, 13)
SPLIT_SLOT = 14
CHUNK = WCOLS // B
TOEP_FILTERS = 8
TOEP_PARTS = 3 * FILTERS // TOEP_FILTERS
PAIRS = 2 * NBLK
COPIES = PER_BLK * 3


def attention(nc, t, d):
    with ExitStack() as ctx:
        sb = lambda name, shape, dt: ctx.enter_context(nc.sbuf_tensor(name, shape, dt))
        sem = lambda name: ctx.enter_context(nc.semaphore(name))
        w_hi, w_lo, ident = t["w_hi"], t["w_lo"], t["ident"]
        w4 = lambda w, i: w[:, i, :].rearrange("p (c n) -> p c n", c=KC)
        xT = sb("xT", [P, 2, KC * S], F32)
        x_hi = sb("x_hi", [P, 2, KC * S], F16)
        x_lo = sb("x_lo", [P, 2, KC * S], F16)
        qk = sb("qk", [P, 2, 4, 2, S], F16)
        stack = sb("stack", [3 * HD, 2, NBLK, PER_BLK, 2, S], F16)
        v = sb("v", [P, 2, SB, D], F32)
        row_max = sb("row_max", [P, 2, 2, SB], F32)
        neg_bias = sb("neg_bias", [P, 2, 2, SB], F32)
        probs = sb("probs", [P, 4, 2, SB, S], F32)
        sums = sb("sums", [P, 4, 2, SB], F32)
        inv = sb("inv", [P, 4, 2, SB], F32)
        coef = sb("coef", [P, 4, 2, SB], F32)
        scaled2 = sb("scaled2", [P, 2, SB, S], F32)
        mixed = sb("mixed", [P, 2, SB, S], F32)
        mixedT = sb("mixedT", [P, 2, SB, S], F32)
        o_hi = sb("o_hi", [P, NBLK, S], F16)
        o_lo = sb("o_lo", [P, NBLK, S], F16)
        x_rows = sb("x_rows", [P, SB, D], F32)
        resid = sb("resid", [P, SB, D], F32)
        stats = sb("stats", [P, SB, 6], F32)
        moments = sb("moments", [P, SB, 2], F32)
        rstd = sb("rstd", [P, SB], F32)
        nt = [sb(f"newton{k}", [P, SB], F32) for k in range(2)]
        y1 = sb("y1", [P, 2, SB, D], F32)
        w_chunk = sb("w_chunk", [P, 3, CHUNK], F32)
        ps_s = ctx.enter_context(nc.psum_tensor("ps_s", [P, 4, SB, S], F32))
        ps_t = ctx.enter_context(nc.psum_tensor("ps_t", [P, SB, S], F32))
        ps_o = ctx.enter_context(nc.psum_tensor("ps_o", [P, 512], F32))
        ps_p = ctx.enter_context(nc.psum_tensor("ps_p", [P, 2, S], F32))
        ps_g = ctx.enter_context(nc.psum_tensor("ps_g", [P, 512], F32))

        xT_loaded, rows_loaded, chunk_loaded, y1_stored = sem("xT_loaded"), sem("rows_loaded"), sem("chunk_loaded"), sem("y1_stored")
        chunk_summed = sem("chunk_summed")
        x_hi_ready, x_lo_ready = sem("x_hi_ready"), sem("x_lo_ready")
        qk_done, qk_hi, qk_lo, stacked = sem("qk_done"), sem("qk_hi"), sem("qk_lo"), sem("stacked")
        v_done, v_ready = sem("v_done"), sem("v_ready")
        scores_done, max_done, bias_ready, exp_done = sem("scores_done"), sem("max_done"), sem("bias_ready"), sem("exp_done")
        inv_done, coef_ready, scaled2_ready, mix_done = sem("inv_done"), sem("coef_ready"), sem("scaled2_ready"), sem("mix_done")
        tr_done, mixedT_ready, pv_done, o_hi_ready, o_lo_ready = (
            sem("tr_done"), sem("mixedT_ready"), sem("pv_done"), sem("o_hi_ready"), sem("o_lo_ready"))
        proj_done, resid_done, stats_done, moments_done = sem("proj_done"), sem("resid_done"), sem("stats_done"), sem("moments_done")
        rstd_chain, y1_ready, yT_done, yT_ready = sem("rstd_chain"), sem("y1_ready"), sem("yT_done"), sem("yT_ready")
        passed = sem("passed_attention")
        block = ctx.enter_context(nc.Block())

        PREPARE, FIRST, FULL, LAST, DRAIN = (
            dict(project=p, attend=a, close=c) for p, a, c in
            ((True, False, False), (True, True, False), (True, True, True), (False, True, True), (False, False, True)))

        def steps(eng, step):
            step(-1, 1, PREPARE, None)
            step(0, 0, FIRST, PREPARE)
            with eng.Fori(1, B - 2, 2) as b:
                step(b, 1, FULL, FIRST)
                step(b + 1, 0, FULL, FULL)
            step(B - 1, 1, LAST, FULL)
            step(B, 0, DRAIN, LAST)

        def lagging(b, par, slot, lag, now):
            if slot >= lag:
                return (b, slot - lag, par) if now["attend"] else None
            return (b - 1, slot - lag + H, 1 - par) if now["close"] else None

        @block.sync
        def _(sp):
            def step(b, par, now, before):
                n, m = b + 1, b - 1
                if now["project"]:
                    if before is None:
                        sp.dma_start(xT[:, 0, :], d["xT"][:, 0:KC * S]).then_inc(xT_loaded, 16)
                    wait_alone(sp, x_hi_ready, n, passed)
                    wait_alone(sp, x_lo_ready, n, passed)
                    wait_alone(sp, xT_loaded, 16 * (n + 1), passed)
                    sp.dma_start(xT[:, par, :], d["xT"][:, ds((n + 1) * (KC * S), KC * S)]).then_inc(xT_loaded, 16)
                    wait_alone(sp, chunk_summed, n * 3, passed)
                    sp.dma_start(w_chunk[:], d["wffn"][:, :, ds(n * CHUNK, CHUNK)]).then_inc(chunk_loaded, 16)
                for blk in range(NBLK):
                    if now["attend"] and blk == 2:
                        wait_alone(sp, resid_done, b * SB, passed)
                        sp.dma_start(x_rows[:].rearrange("p (o s) n -> p o s n", o=1),
                                     d["x"][ds(b, 1)].rearrange("o (s p) n -> p o s n", p=P)).then_inc(rows_loaded, 16)
                    if now["close"] and blk == 3:
                        wait_alone(sp, y1_ready, (m + 1) * SB, passed)
                        sp.dma_start(d["y1_rows"][ds(m, 1)].rearrange("o (s p) n -> p o s n", p=P),
                                     y1[:, 1 - par, :, :].rearrange("p (o s) n -> p o s n", o=1)).then_inc(y1_stored, 16)
                        wait_alone(sp, y1_stored, 16 * (m + 1), passed)
                    if now["project"]:
                        wait_alone(sp, qk_lo, n * PAIRS + 2 * blk + 2, passed)
                        if now["attend"]:
                            wait_alone(sp, scores_done, b * H + 4 * blk + 4, passed)
                        wait_alone(sp, stacked, (n * NBLK + blk) * COPIES * 16, passed)
                        for j in range(PER_BLK):
                            for row, halves in enumerate((slice(0, 3, 2), slice(0, 4, 3), slice(1, 3))):
                                sp.dma_start(stack[HD * row:HD * row + HD, :, blk, j, :, :],
                                             qk[HD * j:HD * j + HD, blk % 2, halves, :, :]).then_inc(stacked, 16)

            steps(sp, step)

        @block.tensor
        def _(pe):
            def freed(b, now, kind, k):
                n, m = b + 1, b - 1
                if k == 1:
                    s, value = {"o": (resid_done, m * SB + 1), "v": (v_ready, n * SB + 1), "yT": (yT_ready, m * 2 + 1)}[kind]
                elif kind == "o":
                    s, value = yT_ready, m * 2
                elif kind == "v" and now["close"]:
                    s, value = resid_done, (m + 1) * SB
                elif now["project"]:
                    s, value = v_ready, (n + (kind == "yT")) * SB
                else:
                    s, value = resid_done, (m + 1) * SB
                wait(pe, s, value)

            def step(b, par, now, before):
                n, m = b + 1, b - 1
                if now["project"]:
                    pe.wait_ge(x_lo_ready, n + 1)
                for slot in range(H):
                    if now["attend"]:
                        blk, j = slot // PER_BLK, slot % PER_BLK
                        if j == 0:
                            pe.wait_ge(stacked, (b * NBLK + blk + 1) * COPIES * 16)
                        wait(pe, exp_done, b * H + slot - 1)
                        for w in range(2):
                            for s in range(SB):
                                ins = pe.matmul(ps_s[:, 2 * (slot % 2) + w, s, :], stack[:, 0, blk, j, w, s * P:s * P + P],
                                                stack[:, 1, blk, j, w, :], start=True, stop=True)
                        ins.then_inc(scores_done, 1)
                    if now["project"] and slot % 2 == 0:
                        blk, w_at = slot // 4, slot % 4
                        wait(pe, qk_lo, n * PAIRS + slot // 2)
                        for i in range(2):
                            for c in range(KC):
                                for k, (w, x) in enumerate(((w_hi, x_hi), (w_hi, x_lo), (w_lo, x_hi))):
                                    ins = pe.matmul(ps_p[:, i, :], w4(w, w_at + i)[:, c, blk * P:blk * P + P],
                                                    x[:, 1 - par, c * S:c * S + S], start=(c == 0 and k == 0), stop=(c == KC - 1 and k == 2))
                        ins.then_inc(qk_done, 1)
                    if now["project"] and slot in V_SLOTS:
                        s = V_SLOTS.index(slot)
                        freed(b, now, "v", s)
                        for c in range(KC):
                            for k, (x, w) in enumerate(((x_hi, w_hi), (x_lo, w_hi), (x_hi, w_lo))):
                                ins = pe.matmul(ps_g[:], x[:, 1 - par, c * S + s * P:c * S + s * P + P], w4(w, 4)[:, c, :],
                                                start=(c == 0 and k == 0), stop=(c == KC - 1 and k == 2))
                        ins.then_inc(v_done, 1)
                    if now["close"] and slot in O_SLOTS:
                        s = O_SLOTS.index(slot)
                        pe.wait_ge(o_lo_ready, (m + 1) * NBLK)
                        freed(b, now, "o", s)
                        for c in range(KC):
                            for k, (o, w) in enumerate(((o_hi, w_hi), (o_lo, w_hi), (o_hi, w_lo))):
                                ins = pe.matmul(ps_g[:], o[:, c, s * P:s * P + P], w4(w, 5)[:, c, :],
                                                start=(c == 0 and k == 0), stop=(c == KC - 1 and k == 2))
                        ins.then_inc(proj_done, 1)
                    if now["close"] and slot in YT_SLOTS:
                        k = YT_SLOTS.index(slot)
                        pe.wait_ge(y1_ready, (m + 1) * SB)
                        freed(b, now, "yT", k)
                        for c in range(2):
                            for s in range(SB):
                                ins = pe.matmul(ps_g[:, c * S + s * P:c * S + s * P + P],
                                                y1[:, 1 - par, s, (2 * k + c) * P:(2 * k + c + 1) * P], ident[:],
                                                start=True, stop=True, is_transpose=True, skip_group_check=True)
                        ins.then_inc(yT_done, 1)
                    if (at := lagging(b, par, slot, TR_LAG, now)) is not None:
                        q, h, _ = at
                        pe.wait_ge(mix_done, q * H + h + 1)
                        wait(pe, mixedT_ready, q * H + h)
                        for kb in range(SB):
                            for s in range(SB):
                                ins = pe.matmul(ps_t[:, kb, s * P:s * P + P], mixed[:, h % 2, s, kb * P:kb * P + P], ident[:],
                                                start=True, stop=True, is_transpose=True, skip_group_check=True)
                        ins.then_inc(tr_done, 1)
                    if (at := lagging(b, par, slot, PV_LAG, now)) is not None:
                        q, h, qp = at
                        blk, j = h // PER_BLK, h % PER_BLK
                        if h == 0:
                            pe.wait_ge(v_ready, (q + 1) * SB)
                        if j == 0:
                            wait(pe, o_lo_ready, q * NBLK + blk)
                        pe.wait_ge(mixedT_ready, q * H + h + 1)
                        for kb in range(SB):
                            ins = pe.matmul(ps_o[HD * j:HD * j + HD, 0:S], v[:, qp, kb, h * HD:h * HD + HD], mixedT[:, h % 2, kb, :],
                                            start=(kb == 0), stop=(kb == SB - 1), skip_group_check=True)
                        if j == PER_BLK - 1:
                            ins.then_inc(pv_done, 1)

            steps(pe, step)

        @block.scalar
        def _(act):
            def load_scale(name, at):
                reg = act.alloc_register(name)
                act.reg_load(reg, at.bitcast(I32))
                return reg

            x_scale = load_scale("x_scale", t["scale"][0:1, CX:CX + 1])
            score_scale = [load_scale(f"score_scale{w}", t["score_scale"][0:1, w:w + 1]) for w in range(2)]

            def split_x(n, par):
                act.wait_ge(xT_loaded, (n + 1) * 16)
                wait(act, v_done, (n - 1) * SB)
                act.activation(x_hi[:, par, :], xT[:, par, :], ACT.Copy, scale=x_scale).then_inc(x_hi_ready, 1)

            def toeplitz(part):
                which, at = part % 3, part // 3 * TOEP_FILTERS
                if which < 2:
                    src, width, dst = d["filt_halves"], D, d["toeplitz"][at:at + TOEP_FILTERS, which]
                else:
                    src, width, dst = d["filt_whole"], NEAR, d["toeplitz_near"][at:at + TOEP_FILTERS]
                src = bass.AP(tensor=src.tensor, offset=(which % 2 * FILTERS + at) * (width + P) + P,
                              ap=[[width + P, TOEP_FILTERS], [-1, P], [1, width]])
                act.dma_start(dst, src).then_inc(t["toep_written"], 16)

            def step(b, par, now, before):
                n, m = b + 1, b - 1
                if before is None:
                    split_x(0, 0)
                for slot in range(H):
                    if before == PREPARE and slot < TOEP_PARTS:
                        toeplitz(slot)
                    if now["attend"]:
                        act.wait_ge(bias_ready, b * H + slot + 1)
                        wait(act, mix_done, b * H + slot - 3)
                        for w in range(2):
                            for s in range(SB):
                                ins = act.activation(probs[:, slot % 4, w, s, :], ps_s[:, 2 * (slot % 2) + w, s, :], ACT.Exp,
                                                     bias=neg_bias[:, slot % 2, w, s:s + 1], scale=score_scale[w],
                                                     accum_out=sums[:, slot % 4, w, s:s + 1])
                        ins.then_inc(exp_done, 1)
                    if now["project"] and slot % 2 == 0:
                        blk, w = slot // 4, slot // 2 % 2
                        act.wait_ge(qk_done, n * PAIRS + slot // 2 + 1)
                        if w == 0:
                            wait(act, stacked, (n * NBLK + blk - 1) * COPIES * 16)
                        act.copy(qk[:, blk % 2, 0:4:2, w, :], ps_p[:]).then_inc(qk_hi, 1)
                    if (at := lagging(b, par, slot, TR_LAG, now)) is not None:
                        q, h, _ = at
                        act.wait_ge(tr_done, q * H + h + 1)
                        act.copy(mixedT[:, h % 2, :, :], ps_t[:]).then_inc(mixedT_ready, 1)
                    if (at := lagging(b, par, slot, PV_LAG, now)) is not None and at[1] % PER_BLK == PER_BLK - 1:
                        q, h, _ = at
                        blk = h // PER_BLK
                        act.wait_ge(pv_done, q * NBLK + blk + 1)
                        act.copy(o_hi[:, blk, :], ps_o[:, 0:S]).then_inc(o_hi_ready, 1)
                    if now["project"] and slot in V_SLOTS:
                        s = V_SLOTS.index(slot)
                        act.wait_ge(v_done, n * SB + s + 1)
                        wait(act, pv_done, (n - 1) * NBLK)
                        act.copy(v[:, 1 - par, s, :], ps_g[:]).then_inc(v_ready, 1)
                    if now["close"] and slot in YT_SLOTS:
                        k = YT_SLOTS.index(slot)
                        act.wait_ge(yT_done, m * 2 + k + 1)
                        act.copy(t["y1T"][:, 2 * k:2 * k + 2, ds(m, 1), :],
                                 ps_g[:].rearrange("p (c o s) -> p c o s", c=2, o=1)).then_inc(yT_ready, 1)
                    if now["project"] and slot == SPLIT_SLOT:
                        split_x(n + 1, par)

            steps(act, step)
            act.wait_ge(yT_ready, 2 * B)

        @block.gpsimd
        def _(pool):
            def step(b, par, now, before):
                m = b - 1
                for slot in range(H):
                    if (at := lagging(b, par, slot, COEF_LAG, now)) is not None:
                        q, h, _ = at
                        wait_alone(pool, coef_ready, q * H + h + 1, passed)
                        wait_alone(pool, mix_done, q * H + h - 1, passed)
                        pool.tensor_tensor(scaled2[:, h % 2], probs[:, h % 4, 1], coef[:, h % 4, 1].unsqueeze(2).broadcast_to([P, SB, S]),
                                           ALU.mult).then_inc(scaled2_ready, 1)
                    if now["close"] and slot == STATS_SLOTS[-1]:
                        wait_alone(pool, moments_done, (m + 1) * SB, passed)
                        rsqrt(Chain(pool, rstd_chain, m * RSQRT_STEPS, passed), pool, rstd[:], moments[:, :, 1], nt)

            steps(pool, step)

        @block.vector
        def _(dve):
            def split_x(n, par):
                dve.wait_ge(x_hi_ready, n + 1)
                wait(dve, v_done, (n - 1) * SB)
                dve.scalar_tensor_tensor(out=x_lo[:, par, :], in0=xT[:, par, :], scalar=t["scale"][:, CX:CX + 1],
                                         in1=x_hi[:, par, :], op0=ALU.mult, op1=ALU.subtract).then_inc(x_lo_ready, 1)

            def step(b, par, now, before):
                n, m = b + 1, b - 1
                if before is None:
                    split_x(0, 0)
                for slot in range(H):
                    if now["attend"]:
                        dve.wait_ge(scores_done, b * H + slot + 1)
                        if isinstance(b, int) and b * H + slot >= 2 or not isinstance(b, int):
                            dve.wait_ge(exp_done, b * H + slot - 1)
                        hp = slot % 2
                        dve.tensor_reduce(row_max[:, hp], ps_s[:, 2 * hp:2 * hp + 2], AX, ALU.max).then_inc(max_done, 1)
                    coefs = lagging(b, par, slot, COEF_LAG, now)
                    if coefs is not None:
                        q, h, _ = coefs
                        dve.wait_ge(exp_done, q * H + h + 1)
                        dve.reciprocal(inv[:, h % 4], sums[:, h % 4]).then_inc(inv_done, 1)
                    if now["attend"]:
                        dve.wait_ge(max_done, b * H + slot + 1)
                        dve.tensor_tensor(neg_bias[:, hp], row_max[:, hp], t["neg_score_scale"][:].unsqueeze(2).broadcast_to([P, 2, SB]),
                                          ALU.mult).then_inc(bias_ready, 1)
                    if coefs is not None:
                        q, h, _ = coefs
                        dve.wait_ge(inv_done, q * H + h + 1)
                        dve.tensor_tensor(coef[:, h % 4], inv[:, h % 4], t["mix_factor"][:, h, :].unsqueeze(2).broadcast_to([P, 2, SB]),
                                          ALU.mult).then_inc(coef_ready, 1)
                    if now["project"] and slot % 2 == 1:
                        blk, w = slot // 4, slot // 2 % 2
                        dve.wait_ge(qk_hi, n * PAIRS + slot // 2 + 1)
                        dve.tensor_tensor(qk[:, blk % 2, 1:4:2, w, :], ps_p[:], qk[:, blk % 2, 0:4:2, w, :], ALU.subtract).then_inc(qk_lo, 1)
                    if (at := lagging(b, par, slot, MIX_LAG, now)) is not None:
                        q, h, _ = at
                        dve.wait_ge(scaled2_ready, q * H + h + 1)
                        wait(dve, tr_done, q * H + h - 1)
                        for s in range(SB):
                            ins = dve.scalar_tensor_tensor(out=mixed[:, h % 2, s, :], in0=probs[:, h % 4, 0, s, :], scalar=coef[:, h % 4, 0, s:s + 1],
                                                           in1=scaled2[:, h % 2, s, :], op0=ALU.mult, op1=ALU.add)
                        ins.then_inc(mix_done, 1)
                    if (at := lagging(b, par, slot, O_LO_LAG, now)) is not None and at[1] % PER_BLK == PER_BLK - 1:
                        q, h, _ = at
                        blk = h // PER_BLK
                        dve.wait_ge(o_hi_ready, q * NBLK + blk + 1)
                        dve.tensor_tensor(o_lo[:, blk, :], ps_o[:, 0:S], o_hi[:, blk, :], ALU.subtract).then_inc(o_lo_ready, 1)
                    if now["close"] and slot in STATS_SLOTS:
                        s = STATS_SLOTS.index(slot)
                        dve.wait_ge(resid_done, m * SB + s + 1)
                        dve.bn_stats(stats[:, s, :], resid[:, s, :]).then_inc(stats_done, 1)
                    if now["close"] and slot in RESID_SLOTS:
                        s = RESID_SLOTS.index(slot)
                        dve.wait_ge(proj_done, m * SB + s + 1)
                        if s == 0:
                            dve.wait_ge(rows_loaded, (m + 1) * 16)
                            if isinstance(b, int):
                                wait(dve, y1_ready, m * SB)
                        dve.scalar_tensor_tensor(out=resid[:, s, :], in0=ps_g[:], scalar=t["attn_unscale"][:, 0:1],
                                                 in1=x_rows[:, s, :], op0=ALU.mult, op1=ALU.add).then_inc(resid_done, 1)
                    if now["project"] and slot in SUM_SLOTS:
                        k = SUM_SLOTS.index(slot)
                        dve.wait_ge(chunk_loaded, (n + 1) * 16)
                        dve.tensor_reduce(t["w_sums"][:, ds(n, 1), k:k + 1], w_chunk[:, k:k + 1, :].unsqueeze(1), AX, ALU.add,
                                          apply_absolute_value=True).then_inc(chunk_summed, 1)
                    if now["close"] and slot in STATS_SLOTS:
                        s = STATS_SLOTS.index(slot)
                        wait_alone(dve, stats_done, m * SB + s + 1, passed)
                        dve.bn_aggr(moments[:, s, :], stats[:, s, :]).then_inc(moments_done, 1)
                    if now["close"] and slot in Y1_SLOTS:
                        s = Y1_SLOTS.index(slot)
                        dve.wait_ge(rstd_chain, (m + 1) * RSQRT_STEPS)
                        if isinstance(b, int):
                            wait(dve, yT_done, (m - 1) * 2)
                            wait(dve, y1_stored, (m - 1) * 16)
                        dve.tensor_scalar(y1[:, 1 - par, s, :], resid[:, s, :], moments[:, s, 0:1], rstd[:, s:s + 1],
                                          ALU.subtract, ALU.mult).then_inc(y1_ready, 1)
                    if now["project"] and slot == SPLIT_SLOT:
                        split_x(n + 1, par)

            steps(dve, step)
            dve.wait_ge(y1_ready, B * SB)


FW = WCOLS // FILTERS
GROUPS = KC * B


def convolution(nc, t, d):
    with ExitStack() as ctx:
        sb = lambda name, shape, dt: ctx.enter_context(nc.sbuf_tensor(name, shape, dt))
        sem = lambda name: ctx.enter_context(nc.semaphore(name))
        ctx_T = sb("ctx_T", [P, GROUPS, S], F32)
        skip = sb("skip", [P, S], F32)
        toep = sb("toep", [P, 2, 2, D], F16)
        toep_near = sb("toep_near", [P, 2, NEAR], F32)
        prod = sb("prod", [P, 2, GROUPS, CH, CH], F32)
        prod_hi = sb("prod_hi", [P, 2, CUT * B, CH, CH], F16)
        prod_lo = sb("prod_lo", [P, 2, CUT * B, CH, CH], F16)
        gated = sb("gated", [P, 2, GROUPS, CH, CH], F32)
        half_sum = sb("half_sum", [P, 2, GROUPS, CH // 2, CH], F32)
        summed = sb("summed", [P, GROUPS, CH], F32)
        vx = sb("vx", [P, GROUPS, CH], F32)
        vxs = sb("vxs", [P, 2, GROUPS, CH], F32)
        u = sb("u", [P, 2, GROUPS], F32)
        skip_term = sb("skip_term", [P, 2, GROUPS, CH], F32)
        w_part = sb("w_part", [P, 2, 3, FW], F32)
        below = sb("below", [P, 3, FW], F16)
        cmax = sb("cmax", [P, KC + 1], F32)
        call_max = sb("call_max", [P, 1], F32)
        wsum = sb("wsum", [P, 3], F32)
        wall = sb("wall", [P, 3], F32)
        limit = sb("limit", [P, 2, 3], F32)
        tmp = sb("conv_tmp", [P, 4], F32)
        ps = ctx.enter_context(nc.psum_tensor("ps_conv", [P, 2, KC, 512], F32))

        ctx_loaded = [sem(f"ctx_loaded{c}") for c in range(KC)]
        skip_loaded, toep_loaded, part_loaded = sem("skip_loaded"), sem("toep_loaded"), sem("part_loaded")
        conv_chain, cmax_ready, wsum_ready, all_ready, ctx_scaled = (
            sem("conv_chain"), sem("cmax_ready"), sem("wsum_ready"), sem("all_ready"), sem("ctx_scaled"))
        cut_ready, whole_ready, hi_ready, lo_ready = sem("cut_ready"), sem("whole_ready"), sem("hi_ready"), sem("lo_ready")
        conv_done, gated_done, half_done, summed_done = sem("conv_done"), sem("gated_done"), sem("half_done"), sem("summed_done")
        vx_done, vxs_done, u_done, skip_done, out_done = sem("vx_done"), sem("vxs_done"), sem("u_done"), sem("skip_done"), sem("out_done")
        below_done, ternary_done = sem("below_done"), sem("ternary_done")
        passed = sem("passed_convolution")
        block = ctx.enter_context(nc.Block())
        y1T = t["y1T"][:].rearrange("p c b s -> p (c b) s")
        conv_T = t["conv_T"]

        @block.sync
        def _(sp):
            for c in range(KC):
                sp.dma_start(ctx_T[:, c * B:c * B + B, :], d["ctxT"][:, c * B:c * B + B, :]).then_inc(ctx_loaded[c], 16)
            sp.dma_start(skip[:], d["skip"].rearrange("(o n) -> o n", o=1).broadcast_to([P, S])).then_inc(skip_loaded, 16)

            def load(h, par):
                wait_alone(sp, conv_done, (h - 1) * 2, passed)
                wait_alone(sp, toep_loaded, h * 32, passed)
                sp.dma_start(toep[:, par, :, :].unsqueeze(1), d["toeplitz"][ds(h, 1)].rearrange("o a p n -> p o a n")).then_inc(toep_loaded, 16)
                sp.dma_start(toep_near[:, par, :].unsqueeze(1), d["toeplitz_near"][ds(h, 1)].rearrange("o p n -> p o n")).then_inc(toep_loaded, 16)
                wait_alone(sp, ternary_done, (h - 1) * 3, passed)
                wait_alone(sp, part_loaded, h * 16, passed)
                sp.dma_start(w_part[:, par], d["wffn"][:, :, ds(h * FW, FW)]).then_inc(part_loaded, 16)

            sp.wait_ge(t["toep_written"], 16 * TOEP_PARTS)
            filters(sp, load)

        @block.tensor
        def _(pe):
            def conv(h, par):
                wait(pe, gated_done, (h - 1) * 2)
                pe.wait_ge(toep_loaded, (h + 1) * 32)
                pe.wait_ge(hi_ready, h + 1)
                near = lambda lb, mb: toep_near[:, par, (lb - mb) * P:(lb - mb + 1) * P]
                cut = lambda half, lb, mb: toep[:, par, half, (lb - mb) * P:(lb - mb + 1) * P]
                for k in range(2):
                    if k == 1:
                        pe.wait_ge(whole_ready, h + 1)
                    lbs = range(2 * k, 2 * k + 2)
                    terms = [(lb, cut(w, lb, mb), prod_hi, mb) for lb in lbs for mb in range(min(lb + 1, CUT)) for w in range(2)]
                    terms += [(lb, near(lb, mb), prod, mb) for lb in lbs for mb in range(CUT, lb + 1)]
                    terms += [(lb, cut(0, lb, mb), prod_lo, mb) for lb in lbs for mb in range(min(lb + 1, CUT))]
                    for n, (lb, w, products, mb) in enumerate(terms):
                        if k == 0 and products is prod_lo:
                            pe.wait_ge(lo_ready, h + 1)
                        ins = pe.matmul(ps[:, par, lb, :], w, products[:, par, mb * B:mb * B + B].rearrange("p b i j -> p (b i j)"),
                                        start=all(x[0] != lb for x in terms[:n]), stop=all(x[0] != lb for x in terms[n + 1:]),
                                        skip_group_check=True)
                    ins.then_inc(conv_done, 1)

            filters(pe, conv)

        of_filter = lambda tile, h: tile[:, :, ds(h * CH, CH)]
        cut, whole = slice(0, CUT * B), slice(CUT * B, GROUPS)

        @block.scalar
        def _(act):
            def split(h, par):
                act.wait_ge(cut_ready, h + 1)
                wait(act, conv_done, (h - 1) * 2)
                act.copy(prod_hi[:, par], prod[:, par, cut]).then_inc(hi_ready, 1)

            filters(act, split)

        @block.gpsimd
        def _(pool):
            pool.wait_ge(cmax_ready, 1)
            pool.partition_all_reduce(call_max[:], cmax[:, KC:KC + 1], P, RMAX).then_inc(all_ready, 1)
            pool.wait_ge(wsum_ready, 1)
            pool.partition_all_reduce(wall[:], wsum[:], P, RADD).then_inc(all_ready, 1)
            pool.wait_ge(ctx_scaled, 2)

            def low(h, par):
                wait_alone(pool, hi_ready, h + 1, passed)
                wait_alone(pool, conv_done, (h - 1) * 2, passed)
                pool.tensor_tensor(prod_lo[:, par], prod[:, par, cut], prod_hi[:, par], ALU.subtract).then_inc(lo_ready, 1)

            def halve(h, par):
                wait_alone(pool, gated_done, h * 2 + 2, passed)
                wait_alone(pool, summed_done, h - 1, passed)
                pool.tensor_tensor(half_sum[:, par], gated[:, par, :, 0:CH // 2], gated[:, par, :, CH // 2:CH], ALU.add).then_inc(half_done, 1)

            def skip_rows(h, par):
                wait_alone(pool, vxs_done, h, passed)
                pool.tensor_tensor(vx[:], of_filter(y1T, h), of_filter(ctx_T, h), ALU.mult).then_inc(vx_done, 1)
                wait_alone(pool, vx_done, h + 1, passed)
                wait_alone(pool, u_done, h - 1, passed)
                pool.tensor_tensor(vxs[:, par], vx[:], skip[:, ds(h * CH, CH)].unsqueeze(1).broadcast_to([P, GROUPS, CH]),
                                   ALU.mult).then_inc(vxs_done, 1)

            def step(h, par):
                static = isinstance(h, int)
                if not static or h < FILTERS - 2:
                    low(h + 2, par)
                halve(h, par)
                if not static or h < FILTERS - 1:
                    skip_rows(h + 1, 1 - par)
                wait_alone(pool, u_done, h + 1, passed)
                wait_alone(pool, out_done, h - 1, passed)
                pool.tensor_tensor(skip_term[:, par], of_filter(ctx_T, h), u[:, par].unsqueeze(2).broadcast_to([P, GROUPS, CH]),
                                   ALU.mult).then_inc(skip_done, 1)

            low(0, 0)
            low(1, 1)
            skip_rows(0, 0)
            filters(pool, step)

        @block.vector
        def _(dve):
            ch = Chain(dve, conv_chain)
            for c in range(KC):
                dve.wait_ge(ctx_loaded[c], 16)
                ch.then(dve.tensor_reduce(cmax[:, c:c + 1], ctx_T[:, c * B:c * B + B, :].rearrange("p b s -> p (b s)"), AX, ALU.max,
                                          apply_absolute_value=True))
            dve.tensor_reduce(cmax[:, KC:KC + 1], cmax[:, 0:KC], AX, ALU.max).then_inc(cmax_ready, 1)
            dve.tensor_reduce(wsum[:], t["w_sums"][:].rearrange("p b k -> p k b"), AX, ALU.add).then_inc(wsum_ready, 1)
            dve.wait_ge(all_ready, 1)
            ch.then(dve.tensor_scalar(call_max[:], call_max[:], 1e-30, None, ALU.max))
            ch.then(dve.tensor_scalar(tmp[:, 0:1].bitcast(I32), call_max[:].bitcast(I32), EXP_MASK, None, ALU.bitwise_and))
            ch.then(dve.reciprocal(tmp[:, 1:2], tmp[:, 0:1]))
            ch.then(dve.tensor_scalar(tmp[:, 1:2], tmp[:, 1:2], 512.0, None, ALU.mult))
            for c in range(KC):
                ins = dve.tensor_scalar(ctx_T[:, c * B:c * B + B, :], ctx_T[:, c * B:c * B + B, :], tmp[:, 1:2], None, ALU.mult)
                ch.then(ins)
            dve.nop().then_inc(ctx_scaled, 1)
            dve.wait_ge(skip_loaded, 16)
            ch.then(dve.tensor_scalar(skip[:], skip[:], t["scale"][:, CK:CK + 1], None, ALU.mult))
            dve.nop().then_inc(ctx_scaled, 1)
            ch.then(dve.tensor_scalar(tmp[:, 2:3], tmp[:, 0:1], 1.0 / 512.0, None, ALU.mult))
            ch.then(dve.tensor_tensor(tmp[:, 3:4], tmp[:, 2:3], tmp[:, 2:3], ALU.mult))
            ch.then(dve.tensor_tensor(t["conv_unscale"][:], tmp[:, 3:4], t["unscale"][:, CK:CK + 1], ALU.mult))
            dve.wait_ge(all_ready, 2)
            ch.then(dve.tensor_scalar(t["w_mean"][:], wall[:], float(np.float32(1.0 / (HID * D))), None, ALU.mult))
            ch.then(dve.tensor_scalar(limit[:, 0, :], t["w_mean"][:], 0.5, None, ALU.mult))
            ch.then(dve.tensor_scalar(limit[:, 1, :], t["w_mean"][:], -0.5, None, ALU.mult))

            def product(h, par, groups, ready):
                n = groups.stop - groups.start
                at = (slice(None), groups, ds(h * CH, CH))
                dve.tensor_tensor(prod[:, par, groups], y1T[at].unsqueeze(3).broadcast_to([P, n, CH, CH]),
                                  ctx_T[at].unsqueeze(2).broadcast_to([P, n, CH, CH]), ALU.mult).then_inc(ready, 1)

            def product_cut(h, par):
                wait(dve, lo_ready, h - 1)
                product(h, par, cut, cut_ready)

            def product_whole(h, par):
                wait(dve, conv_done, (h - 1) * 2)
                product(h, par, whole, whole_ready)

            def row_sum(h, par):
                dve.wait_ge(half_done, h + 1)
                wait(dve, out_done, h)
                dve.tensor_reduce(summed[:], half_sum[:, par].rearrange("p g i j -> p g j i"), AX, ALU.add).then_inc(summed_done, 1)

            def add_skip(h, par):
                dve.wait_ge(summed_done, h + 1)
                dve.wait_ge(skip_done, h + 1)
                dve.tensor_tensor(of_filter(conv_T, h), summed[:], skip_term[:, par], ALU.add).then_inc(out_done, 1)

            def skip_sum(h, par):
                dve.wait_ge(vxs_done, h + 1)
                wait(dve, skip_done, h - 1)
                dve.tensor_reduce(u[:, par], vxs[:, par], AX, ALU.add).then_inc(u_done, 1)

            def step(h, par):
                static = isinstance(h, int)
                wait(dve, half_done, h - 1)
                half = GROUPS // 2
                for k in range(2):
                    dve.wait_ge(conv_done, h * 2 + k + 1)
                    dve.tensor_tensor(gated[:, par, k * half:(k + 1) * half], ps[:, par, 2 * k:2 * k + 2, :].rearrange("p c (b i j) -> p (c b) i j", b=B, i=CH),
                                      ctx_T[:, k * half:(k + 1) * half, ds(h * CH, CH)].unsqueeze(3).broadcast_to([P, half, CH, CH]),
                                      ALU.mult).then_inc(gated_done, 1)
                    if k == 0 and (not static or h < FILTERS - 2):
                        product_cut(h + 2, par)
                if not static or h < FILTERS - 1:
                    product_whole(h + 1, 1 - par)
                dve.wait_ge(part_loaded, (h + 1) * 16)
                for k in range(3):
                    if isinstance(h, int) and h > 0 or not isinstance(h, int):
                        dve.wait_ge(ternary_done, (h - 1) * 3 + k + 1)
                    dve.tensor_scalar(below[:, k, :], w_part[:, par, k, :], limit[:, 1, k:k + 1], None, ALU.is_lt).then_inc(below_done, 1)
                for k in range(3):
                    dve.wait_ge(below_done, h * 3 + k + 1)
                    dve.scalar_tensor_tensor(out=t["ternary"][:, k, ds(h * FW, FW)], in0=w_part[:, par, k, :], scalar=limit[:, 0, k:k + 1],
                                             in1=below[:, k, :], op0=ALU.is_gt, op1=ALU.subtract).then_inc(ternary_done, 1)
                if not static or h > 0:
                    row_sum(h - 1, 1 - par)
                skip_sum(h, par)
                if not static or h > 0:
                    add_skip(h - 1, 1 - par)

            product_cut(0, 0)
            product_whole(0, 0)
            product_cut(1, 1)
            filters(dve, step)
            row_sum(FILTERS - 1, 1)
            add_skip(FILTERS - 1, 1)
            dve.wait_ge(out_done, FILTERS)
            dve.wait_ge(ternary_done, 3 * FILTERS)


def filters(eng, step):
    step(0, 0)
    step(1, 1)
    with eng.Fori(2, FILTERS - 3, 2) as h:
        step(h, 0)
        step(h + 1, 1)
    step(FILTERS - 2, 0)
    step(FILTERS - 1, 1)


OUT_LAG = 2


def feed_forward(nc, t, d):
    with ExitStack() as ctx:
        sb = lambda name, shape, dt: ctx.enter_context(nc.sbuf_tensor(name, shape, dt))
        sem = lambda name: ctx.enter_context(nc.semaphore(name))
        ident = t["ident"]
        conv_b = sb("conv_b", [P, 2, KC, S], F32)
        y1 = sb("y1_back", [P, 2, SB, D], F32)
        resid = sb("resid2", [P, SB, D], F32)
        resid3 = sb("resid3", [P, SB, D], F32)
        stats = sb("stats2", [P, 2, SB, 6], F32)
        moments = sb("moments2", [P, 2, SB, 2], F32)
        rstd = sb("rstd2", [P, 2, SB], F32)
        nt = [sb(f"newton2_{k}", [P, SB], F32) for k in range(2)]
        y2 = sb("y2", [P, 2, SB, D], F32)
        y2_hi = sb("y2_hi", [P, 2, KC, S], F16)
        y2_lo = sb("y2_lo", [P, 2, KC, S], F16)
        th = sb("th", [P, 2, S], F32)
        act_h1 = sb("act_h1", [P, 2, S], F32)
        g = sb("g", [P, 2, S], F32)
        g_hi = sb("g_hi", [P, 4, S], F16)
        g_lo = sb("g_lo", [P, 4, S], F16)
        out = sb("out", [P, 2, SB, D], F32)
        scal = sb("ffn_scal", [P, 2], F32)
        ps_f = ctx.enter_context(nc.psum_tensor("ps_f", [P, 2, 512], F32))
        ps_h = ctx.enter_context(nc.psum_tensor("ps_h", [P, 4, 2, S], F32))
        ps_y = ctx.enter_context(nc.psum_tensor("ps_y", [P, SB, D], F32))

        conv_loaded, y1_loaded, stored = sem("conv_loaded"), sem("y1_loaded"), sem("stored")
        scal_chain, scal_ready = sem("scal_chain"), sem("scal_ready")
        back_done, resid_done, stats_done, moments_done = sem("back_done"), sem("resid2_done"), sem("stats2_done"), sem("moments2_done")
        rstd_chain, y2_ready, y2T_done, y2_hi_ready, y2_lo_ready = (
            sem("rstd2_chain"), sem("y2_ready"), sem("y2T_done"), sem("y2_hi_ready"), sem("y2_lo_ready"))
        h_done, th_ready, h1_ready, g_ready, g_hi_ready, g_lo_ready, y_done = (
            sem("h_done"), sem("th_ready"), sem("h1_ready"), sem("g_ready"), sem("g_hi_ready"), sem("g_lo_ready"), sem("y_done"))
        resid3_done, stats3_done, moments3_done, rstd3_chain, out_ready = (
            sem("resid3_done"), sem("stats3_done"), sem("moments3_done"), sem("rstd3_chain"), sem("out_ready"))
        passed = sem("passed_feed_forward")
        block = ctx.enter_context(nc.Block())
        conv_T = t["conv_T"][:].rearrange("p (c b) s -> p c b s", c=KC)
        w13 = t["ternary"][:].rearrange("p k (c n) -> p k c n", c=KC)
        w2 = t["ternary"][:, 2, :].rearrange("p (c n) -> p c n", c=HC)

        def steps(eng, step):
            step(-1, 1, True, False)
            step(0, 0, True, True)
            step(1, 1, True, True)
            with eng.Fori(2, B - 3, 2) as b:
                step(b, 0, True, True)
                step(b + 1, 1, True, True)
            step(B - 2, 0, True, True)
            step(B - 1, 1, False, True)

        @block.sync
        def _(sp):
            def store(m, par):
                wait_alone(sp, out_ready, (m + 1) * SB, passed)
                sp.dma_start(d["out"][ds(m, 1)].rearrange("o (s p) n -> p o s n", p=P),
                             out[:, par, :, :].rearrange("p (o s) n -> p o s n", o=1)).then_inc(stored, 16)
                wait_alone(sp, stored, (m + 1) * 16, passed)

            def step(b, par, front, main):
                if front:
                    n = b + 1
                    wait_alone(sp, back_done, (n - 1) * SB, passed)
                    wait_alone(sp, resid_done, (n - 1) * SB, passed)
                    wait_alone(sp, conv_loaded, n * 16, passed)
                    sp.dma_start(conv_b[:, 1 - par].unsqueeze(2), conv_T[:, :, ds(n, 1), :]).then_inc(conv_loaded, 16)
                    wait_alone(sp, y1_loaded, n * 16, passed)
                    sp.dma_start(y1[:, 1 - par].rearrange("p (o s) n -> p o s n", o=1),
                                 d["y1_rows"][ds(n, 1)].rearrange("o (s p) n -> p o s n", p=P)).then_inc(y1_loaded, 16)
                if main and not (isinstance(b, int) and b == 0):
                    store(b - 1, 1 - par)

            steps(sp, step)
            store(B - 1, 1)

        @block.tensor
        def _(pe):
            def back(n, par):
                pe.wait_ge(conv_loaded, (n + 1) * 16)
                for s in range(SB):
                    wait(pe, y2_lo_ready, n * 2)
                    for c in range(KC):
                        ins = pe.matmul(ps_f[:, s, c * P:c * P + P], conv_b[:, par, c, s * P:s * P + P], ident[:],
                                        start=True, stop=True, is_transpose=True, skip_group_check=True)
                    ins.then_inc(back_done, 1)

            def y2_transposes(n, par):
                pe.wait_ge(y2_ready, (n + 1) * SB)
                for k in range(2):
                    for c in range(2):
                        for s in range(SB):
                            ins = pe.matmul(ps_f[:, k, c * S + s * P:c * S + s * P + P], y2[:, par, s, (2 * k + c) * P:(2 * k + c + 1) * P],
                                            ident[:], start=True, stop=True, is_transpose=True, skip_group_check=True)
                    ins.then_inc(y2T_done, 1)

            def hidden(b, par, c):
                wait(pe, g_ready, b * HC + c - 3)
                for k in range(2):
                    for kc in range(KC):
                        for half, x in enumerate((y2_hi, y2_lo)):
                            ins = pe.matmul(ps_h[:, c % 4, k, :], w13[:, k, kc, c * P:c * P + P], x[:, par, kc, :],
                                            start=(kc == 0 and half == 0), stop=(kc == KC - 1 and half == 1), skip_group_check=True)
                ins.then_inc(h_done, 1)

            def down(b, par, c):
                pe.wait_ge(g_lo_ready, b * HC + c + 1)
                if c == 0:
                    wait(pe, resid3_done, b * SB)
                for s in range(SB):
                    for half, x in enumerate((g_hi, g_lo)):
                        ins = pe.matmul(ps_y[:, s, :], x[:, c % 4, s * P:s * P + P], w2[:, c, :],
                                        start=(c == 0 and half == 0), stop=(c == HC - 1 and half == 1), skip_group_check=True)
                    if c == HC - 1:
                        ins.then_inc(y_done, 1)

            def step(b, par, front, main):
                if not main:
                    back(b + 1, 1 - par)
                    y2_transposes(b + 1, 1 - par)
                    return
                pe.wait_ge(y2_lo_ready, (b + 1) * 2)
                for c in range(HC + OUT_LAG):
                    if c < HC:
                        hidden(b, par, c)
                    if c == 1 and front:
                        back(b + 1, 1 - par)
                    if c == 8 and front:
                        y2_transposes(b + 1, 1 - par)
                    if c >= OUT_LAG:
                        down(b, par, c - OUT_LAG)

            steps(pe, step)

        @block.scalar
        def _(act):
            act.wait_ge(scal_ready, 1)
            tanh_scale = act.alloc_register("tanh_scale")
            act.reg_load(tanh_scale, scal[0:1, 0:1].bitcast(I32))

            def y2_split(n, par):
                for k in range(2):
                    act.wait_ge(y2T_done, n * 2 + k + 1)
                    if k == 0:
                        wait(act, h_done, (n - 1) * HC)
                    act.activation(y2_hi[:, par, 2 * k:2 * k + 2, :], ps_f[:, k, :].rearrange("p (c s) -> p c s", c=2), ACT.Copy,
                                   scale=Y2_SCALE).then_inc(y2_hi_ready, 1)

            def step(b, par, front, main):
                if not main:
                    y2_split(b + 1, 1 - par)
                    return
                for c in range(HC + 1):
                    if c < HC:
                        u = b * HC + c
                        act.wait_ge(h_done, u + 1)
                        wait(act, h1_ready, u - 1)
                        act.activation(th[:, c % 2, :], ps_h[:, c % 4, 0, :], ACT.Tanh, scale=tanh_scale).then_inc(th_ready, 1)
                    if c >= 1:
                        u = b * HC + c - 1
                        act.wait_ge(g_ready, u + 1)
                        act.copy(g_hi[:, (c - 1) % 4, :], g[:, (c - 1) % 2, :]).then_inc(g_hi_ready, 1)
                    if c == 9 and front:
                        y2_split(b + 1, 1 - par)

            steps(act, step)

        @block.gpsimd
        def _(pool):
            def step(b, par, front, main):
                n = b + 1
                if not main:
                    wait_alone(pool, moments_done, (n + 1) * SB, passed)
                    rsqrt(Chain(pool, rstd_chain, n * RSQRT_STEPS, passed), pool, rstd[:, 0], moments[:, 0, :, 1], nt)
                    return
                for c in range(HC):
                    if c == 4 and front:
                        wait_alone(pool, moments_done, (n + 1) * SB, passed)
                        rsqrt(Chain(pool, rstd_chain, n * RSQRT_STEPS, passed), pool, rstd[:, 0], moments[:, 0, :, 1], nt)
                    u = b * HC + c
                    wait_alone(pool, g_hi_ready, u + 1, passed)
                    pool.tensor_tensor(g_lo[:, c % 4, :], g[:, c % 2, :], g_hi[:, c % 4, :], ALU.subtract).then_inc(g_lo_ready, 1)
                wait_alone(pool, moments3_done, (b + 1) * SB, passed)
                rsqrt(Chain(pool, rstd3_chain, b * RSQRT_STEPS, passed), pool, rstd[:, 1], moments[:, 1, :, 1], nt)

            steps(pool, step)

        @block.vector
        def _(dve):
            ch = Chain(dve, scal_chain)
            mean = t["w_mean"]
            ch.then(dve.tensor_scalar(scal[:, 0:1], mean[:, 0:1], 0.5 / Y2_SCALE, None, ALU.mult))
            ch.then(dve.tensor_tensor(scal[:, 1:2], mean[:, 0:1], mean[:, 1:2], ALU.mult))
            ch.then(dve.tensor_scalar(scal[:, 1:2], scal[:, 1:2], mean[:, 2:3], 0.5 / (Y2_SCALE * Y2_SCALE * G_SCALE), ALU.mult, ALU.mult))
            dve.nop().then_inc(scal_ready, 1)

            def normalise_in(n, par):
                dve.wait_ge(y1_loaded, (n + 1) * 16)
                for s in range(SB):
                    dve.wait_ge(back_done, n * SB + s + 1)
                    dve.scalar_tensor_tensor(out=resid[:, s, :], in0=ps_f[:, s, :], scalar=t["conv_unscale"][:, 0:1], in1=y1[:, par, s, :],
                                             op0=ALU.mult, op1=ALU.add).then_inc(resid_done, 1)
                    dve.wait_ge(resid_done, n * SB + s + 1)
                    dve.bn_stats(stats[:, 0, s, :], resid[:, s, :]).then_inc(stats_done, 1)
                    wait_alone(dve, stats_done, n * SB + s + 1, passed)
                    dve.bn_aggr(moments[:, 0, s, :], stats[:, 0, s, :]).then_inc(moments_done, 1)

            def normalise_out(n, par):
                dve.wait_ge(rstd_chain, (n + 1) * RSQRT_STEPS)
                for s in range(SB):
                    dve.tensor_scalar(y2[:, par, s, :], resid[:, s, :], moments[:, 0, s, 0:1], rstd[:, 0, s:s + 1],
                                      ALU.subtract, ALU.mult).then_inc(y2_ready, 1)

            def y2_split(n, par):
                for k in range(2):
                    dve.wait_ge(y2_hi_ready, n * 2 + k + 1)
                    dve.scalar_tensor_tensor(out=y2_lo[:, par, 2 * k:2 * k + 2, :], in0=ps_f[:, k, :].rearrange("p (c s) -> p c s", c=2),
                                             scalar=Y2_SCALE, in1=y2_hi[:, par, 2 * k:2 * k + 2, :], op0=ALU.mult, op1=ALU.subtract)\
                       .then_inc(y2_lo_ready, 1)

            def step(b, par, front, main):
                n = b + 1
                if not main:
                    normalise_in(n, 1 - par)
                    normalise_out(n, 1 - par)
                    y2_split(n, 1 - par)
                    return
                for c in range(HC):
                    u = b * HC + c
                    dve.wait_ge(th_ready, u + 1)
                    dve.scalar_tensor_tensor(out=act_h1[:, c % 2, :], in0=th[:, c % 2, :], scalar=1.0, in1=ps_h[:, c % 4, 0, :],
                                             op0=ALU.add, op1=ALU.mult).then_inc(h1_ready, 1)
                    dve.wait_ge(h1_ready, u + 1)
                    wait(dve, g_lo_ready, u - 1)
                    dve.scalar_tensor_tensor(out=g[:, c % 2, :], in0=act_h1[:, c % 2, :], scalar=G_SCALE, in1=ps_h[:, c % 4, 1, :],
                                             op0=ALU.mult, op1=ALU.mult).then_inc(g_ready, 1)
                    if c == 2 and front:
                        normalise_in(n, 1 - par)
                    if c == 6 and front:
                        normalise_out(n, 1 - par)
                    if c == HC - 1 and front:
                        y2_split(n, 1 - par)
                for s in range(SB):
                    dve.wait_ge(y_done, b * SB + s + 1)
                    dve.scalar_tensor_tensor(out=resid3[:, s, :], in0=ps_y[:, s, :], scalar=scal[:, 1:2], in1=y2[:, par, s, :],
                                             op0=ALU.mult, op1=ALU.add).then_inc(resid3_done, 1)
                    dve.wait_ge(resid3_done, b * SB + s + 1)
                    dve.bn_stats(stats[:, 1, s, :], resid3[:, s, :]).then_inc(stats3_done, 1)
                    wait_alone(dve, stats3_done, b * SB + s + 1, passed)
                    dve.bn_aggr(moments[:, 1, s, :], stats[:, 1, s, :]).then_inc(moments3_done, 1)
                dve.wait_ge(rstd3_chain, (b + 1) * RSQRT_STEPS)
                if not isinstance(b, int) or b >= 2:
                    dve.wait_ge(stored, (b - 1) * 16)
                for s in range(SB):
                    dve.tensor_scalar(out[:, par, s, :], resid3[:, s, :], moments[:, 1, s, 0:1], rstd[:, 1, s:s + 1],
                                      ALU.subtract, ALU.mult).then_inc(out_ready, 1)

            steps(dve, step)


def build(nc, d):
    t = {}
    with ExitStack() as ctx:
        def keep(scope, name, shape, dt=F32):
            t[name] = scope.enter_context(nc.sbuf_tensor(name, shape, dt))

        keep(ctx, "ident", [P, P])
        keep(ctx, "scale", [P, NMAX])
        keep(ctx, "unscale", [P, NMAX])
        keep(ctx, "score_scale", [P, 2])
        keep(ctx, "neg_score_scale", [P, 2])
        keep(ctx, "attn_unscale", [P, 1])
        keep(ctx, "conv_unscale", [P, 1])
        keep(ctx, "mix_factor", [P, H, 2])
        keep(ctx, "w_sums", [P, B, 3])
        keep(ctx, "w_mean", [P, 3])
        keep(ctx, "y1T", [P, KC, B, S])
        t["toep_written"] = ctx.enter_context(nc.semaphore("toep_written"))
        with ExitStack() as first:
            keep(first, "w_hi", [P, 6, KC * D], F16)
            keep(first, "w_lo", [P, 6, KC * D], F16)
            prepare(nc, t, d)
            attention(nc, t, d)
        keep(ctx, "conv_T", [P, GROUPS, S])
        keep(ctx, "ternary", [P, 3, WCOLS], F16)
        convolution(nc, t, d)
        feed_forward(nc, t, d)


def kernel(x, fside_S2_0, ctx_2048, L0_attn_q1_w, L0_attn_k1_w, L0_attn_q2_w, L0_attn_k2_w, L0_attn_v_w, L0_attn_o_w,
           L0_attn_lambda_param, L0_xattn_k, L0_ffn_w1, L0_ffn_w3, L0_ffn_w2):
    import concourse.bacc as bacc
    from concourse.bass_utils import run_bass_kernel_spmd

    f = lambda a: np.asarray(a)
    chunks = lambda a: a.reshape(-1, P, a.shape[1]).transpose(1, 0, 2)
    x = f(x)
    xT = x.transpose(2, 0, 1).reshape(KC, P, B, S).transpose(1, 2, 0, 3).reshape(P, B * KC * S)
    xT = np.concatenate([xT, np.zeros((P, KC * S), xT.dtype)], axis=1)
    ctxT = f(ctx_2048).transpose(2, 0, 1).reshape(KC, P, B, S).transpose(1, 0, 2, 3).reshape(P, KC * B, S)
    wproj = np.stack([chunks(f(w).T) for w in (L0_attn_q1_w, L0_attn_k1_w, L0_attn_q2_w, L0_attn_k2_w, L0_attn_v_w, L0_attn_o_w)], axis=1)
    pad = lambda a, n, axis: np.concatenate([a, np.zeros([n - s if i == axis else s for i, s in enumerate(a.shape)], a.dtype)], axis=axis)
    w1, w3 = (chunks(pad(f(w).T, HC * P, 1)).reshape(P, WCOLS) for w in (L0_ffn_w1, L0_ffn_w3))
    w2 = chunks(pad(f(L0_ffn_w2).T, HC * P, 0)).reshape(P, WCOLS)
    filt = f(L0_xattn_k)
    filt = np.concatenate([np.zeros((FILTERS, P), filt.dtype), filt], axis=1)
    arrays = {"x": x, "xT": xT, "ctxT": ctxT, "skip": f(fside_S2_0), "wproj": wproj.reshape(P, 6, KC * D), "lam": f(L0_attn_lambda_param),
              "filt": filt, "wffn": np.stack([w1, w3, w2], axis=1)}
    arrays = {k: np.ascontiguousarray(a) for k, a in arrays.items()}

    nc = bacc.Bacc("TRN2", target_bir_lowering=False, num_devices=1)
    d = {k: nc.dram_tensor(f"in_{k}", a.shape, mybir.dt.from_np(a.dtype), kind="ExternalInput").ap() for k, a in arrays.items()}
    d["out"] = nc.dram_tensor("out_y", (B, S, D), F32, kind="ExternalOutput").ap()
    d["y1_rows"] = nc.dram_tensor("y1_rows", (B, S, D), F32, kind="Internal").ap()
    d["filt_halves"] = nc.dram_tensor("filt_halves_dram", (2, FILTERS, D + P), F16, kind="Internal").ap()
    d["filt_whole"] = nc.dram_tensor("filt_whole_dram", (FILTERS, NEAR + P), F32, kind="Internal").ap()
    d["toeplitz_near"] = nc.dram_tensor("toeplitz_near", (FILTERS, P, NEAR), F32, kind="Internal").ap()
    d["toeplitz"] = nc.dram_tensor("toeplitz", (FILTERS, 2, P, D), F16, kind="Internal").ap()
    build(nc, d)
    r = run_bass_kernel_spmd(nc, [{f"in_{k}": a for k, a in arrays.items()}], core_ids=[0])
    return r.results[0]["out_y"]
```

```python
from contextlib import ExitStack

import numpy as np

import concourse.bass as bass
from concourse import mybir

F32 = mybir.dt.float32
F16 = mybir.dt.float16
I32 = mybir.dt.int32
ALU = mybir.AluOpType
ACT = mybir.ActivationFunctionType
AX = mybir.AxisListType.X
RMAX = bass.bass_isa.ReduceOp.max
RADD = bass.bass_isa.ReduceOp.add
ds = bass.ds

P = 128
B, S, D = 8, 256, 512
H, HD = 16, 32
KC = D // P
SB = S // P
PER_BLK = P // HD
NBLK = H // PER_BLK
FILTERS, CH = 32, 8
CUT = 2
NEAR = (KC - CUT) * P
HID = 1365
HC = -(-HID // P)
WCOLS = KC * HC * P
EPS = 1e-5
EXP_MASK = 0x7F800000
RSQRT_SEED = 1597463007.0
Y2_SCALE = 1024.0
G_SCALE = 2.0 ** -24
CX, CQ1, CK1, CQ2, CK2, CV, CO, CK, CLAM = range(9)
NMAX = 9


def wait(eng, sem, value):
    if not (isinstance(value, int) and value <= 0):
        eng.wait_ge(sem, value)


def wait_alone(eng, sem, value, passed):
    if not (isinstance(value, int) and value <= 0):
        eng.wait_ge(sem, value)
        if not isinstance(value, int):
            eng.sem_inc(passed, 1)


class Chain:

    def __init__(self, eng, sem, base=0, passed=None):
        self.eng, self.sem, self.base, self.passed, self.n = eng, sem, base, passed, 0

    def then(self, ins):
        self.n += 1
        ins.then_inc(self.sem, 1)
        wait_alone(self.eng, self.sem, self.base + self.n, self.passed)


RSQRT_STEPS = 1 + 1 + 3 * 4


def rsqrt(chain, eng, out, var, tmp, which=slice(None)):
    safe, square = (x[:, which] for x in tmp)
    chain.then(eng.tensor_scalar(safe, var, EPS, None, ALU.add))
    chain.then(eng.tensor_scalar(out.bitcast(I32), safe.bitcast(I32), -0.5, RSQRT_SEED, ALU.mult, ALU.add))
    for _ in range(3):
        chain.then(eng.tensor_tensor(square, out, out, ALU.mult))
        chain.then(eng.tensor_tensor(square, square, safe, ALU.mult))
        chain.then(eng.tensor_scalar(square, square, -0.5, 1.5, ALU.mult, ALU.add))
        chain.then(eng.tensor_tensor(out, out, square, ALU.mult))


EARLY = 4
X_PIECES = 4
X_PART = KC * S // 2


def x_part(k):
    return slice(k * X_PART, (k + 1) * X_PART)


def weight_hi(act, t, staged, i):
    act.activation(t["w"](0, i), staged, ACT.Copy, scale=t["scale"][:, CQ1 + i:CQ1 + i + 1]).then_inc(t["w_hi_ready"], 1)


def weight_lo(dve, t, staged, i):
    dve.wait_ge(t["w_hi_ready"], i + 1)
    dve.scalar_tensor_tensor(out=t["w"](1, i), in0=staged, scalar=t["scale"][:, CQ1 + i:CQ1 + i + 1],
                             in1=t["w"](0, i), op0=ALU.mult, op1=ALU.subtract).then_inc(t["w_lo_ready"], 1)


def prepare(nc, t, d):
    with ExitStack() as ctx:
        sb = lambda name, shape, dt: ctx.enter_context(nc.sbuf_tensor(name, shape, dt))
        sem = lambda name: ctx.enter_context(nc.semaphore(name))
        w_stage = sb("w_stage", [P, EARLY, KC * D], F32)
        staged = lambda i: w_stage[:, i, :] if i < EARLY else t["late_stage"](i)
        x_stage = sb("x_stage", [P, B * KC * S], F32)
        filt = sb("filt", [FILTERS, D + P], F32)
        filt_halves = sb("filt_halves", [FILTERS, 2, D + P], F16)
        filt_whole = sb("filt_whole", [FILTERS, NEAR + P], F32)
        lam = sb("lam", [P, H], F32)
        part_max = sb("part_max", [P, NMAX], F32)
        x_max = sb("x_max", [P, X_PIECES], F32)
        maxima = sb("maxima", [P, NMAX], F32)
        pow2 = sb("pow2", [P, NMAX], F32)
        tmp = sb("prep_tmp", [P, 4], F32)

        w_loaded = [sem(f"w_loaded{i}") for i in range(6)]
        x_loaded = [sem(f"x_all_loaded{k}") for k in range(X_PIECES)]
        x_piece = lambda k: slice(k * (B * KC * S // X_PIECES), (k + 1) * (B * KC * S // X_PIECES))
        filt_loaded, lam_loaded = sem("filt_loaded"), sem("lam_loaded")
        max_ready, all_max, scaled = sem("max_ready"), sem("all_max"), sem("scales_ready")
        prep_chain = sem("prep_chain")
        filt_hi_ready, filt_lo_ready, filt_stored = sem("filt_hi_ready"), sem("filt_lo_ready"), sem("filt_stored")
        filt_whole_ready = sem("filt_whole_ready")
        ident_zero, ident_ready = sem("ident_zero"), sem("ident_ready")
        block = ctx.enter_context(nc.Block())

        @block.sync
        def _(sp):
            sp.dma_start(filt[:], d["filt"]).then_inc(filt_loaded, 16)
            sp.dma_start(lam[:], d["lam"].rearrange("(o h) -> o h", o=1).broadcast_to([P, H])).then_inc(lam_loaded, 16)
            for k in range(X_PIECES):
                sp.dma_start(x_stage[:, x_piece(k)], d["xT"][:, x_piece(k)]).then_inc(x_loaded[k], 16)
            for i in range(6):
                sp.dma_start(staged(i), d["wproj"][:, i, :]).then_inc(w_loaded[i], 16)
            sp.wait_ge(filt_hi_ready, 1)
            sp.wait_ge(filt_lo_ready, 1)
            sp.dma_start(d["filt_halves"].rearrange("a f n -> f a n"), filt_halves[:]).then_inc(filt_stored, 16)
            sp.wait_ge(filt_whole_ready, 1)
            sp.dma_start(d["filt_whole"], filt_whole[:]).then_inc(filt_stored, 16)
            sp.wait_ge(filt_stored, 32)

        @block.gpsimd
        def _(pool):
            pool.memset(t["ident"][:], 0.0).then_inc(ident_zero, 1)
            pool.wait_ge(ident_zero, 1)
            pool.affine_select(out=t["ident"][:], in_=t["ident"][:], compare_op=ALU.not_equal, fill=1.0, base=0,
                               pattern=[[-1, P]], channel_multiplier=1).then_inc(ident_ready, 1)
            pool.wait_ge(max_ready, 1)
            pool.partition_all_reduce(maxima[:], part_max[:], P, RMAX).then_inc(all_max, 1)
            pool.wait_ge(ident_ready, 1)

        @block.scalar
        def _(act):
            act.wait_ge(scaled, 1)
            for k in range(2):
                act.activation(t["x_hi"][:, 0, x_part(k)], x_stage[:, x_part(k)], ACT.Copy, scale=t["scale"][:, CX:CX + 1]).then_inc(t["x_hi_ready"], 1)
            act.activation(filt_halves[:, 0, :], filt[:], ACT.Copy, scale=t["scale"][0:FILTERS, CK:CK + 1]).then_inc(filt_hi_ready, 1)
            act.activation(filt_whole[:], filt[:, 0:NEAR + P], ACT.Copy, scale=t["scale"][0:FILTERS, CK:CK + 1]).then_inc(filt_whole_ready, 1)
            for i in range(EARLY):
                weight_hi(act, t, staged(i), i)

        @block.vector
        def _(dve):
            ch = Chain(dve, prep_chain)
            ch.then(dve.memset(part_max[:], 0.0))
            dve.wait_ge(filt_loaded, 16)
            ch.then(dve.tensor_reduce(part_max[0:FILTERS, CK:CK + 1], filt[:], AX, ALU.max, apply_absolute_value=True))
            dve.wait_ge(lam_loaded, 16)
            ch.then(dve.tensor_reduce(part_max[:, CLAM:CLAM + 1], lam[:], AX, ALU.max, apply_absolute_value=True))
            ch.then(dve.tensor_scalar(part_max[:, CLAM:CLAM + 1], part_max[:, CLAM:CLAM + 1], 1.0, None, ALU.add))
            for k in range(X_PIECES):
                dve.wait_ge(x_loaded[k], 16)
                ch.then(dve.tensor_reduce(x_max[:, k:k + 1], x_stage[:, x_piece(k)], AX, ALU.max, apply_absolute_value=True))
            ch.then(dve.tensor_reduce(part_max[:, CX:CX + 1], x_max[:], AX, ALU.max))
            for i in range(6):
                dve.wait_ge(w_loaded[i], 16)
                ch.then(dve.tensor_reduce(part_max[:, CQ1 + i:CQ1 + i + 1], staged(i), AX, ALU.max, apply_absolute_value=True))
            dve.nop().then_inc(max_ready, 1)
            dve.wait_ge(all_max, 1)
            ch.then(dve.tensor_scalar(maxima[:], maxima[:], 1e-30, None, ALU.max))
            ch.then(dve.tensor_scalar(pow2[:].bitcast(I32), maxima[:].bitcast(I32), EXP_MASK, None, ALU.bitwise_and))
            ch.then(dve.reciprocal(t["scale"][:], pow2[:]))
            ch.then(dve.tensor_scalar(t["scale"][:, CX:CO + 1], t["scale"][:, CX:CO + 1], 4.0, None, ALU.mult))
            ch.then(dve.tensor_scalar(t["scale"][:, CK:CK + 1], t["scale"][:, CK:CK + 1], 8192.0, None, ALU.mult))
            ch.then(dve.tensor_scalar(t["scale"][:, CLAM:CLAM + 1], t["scale"][:, CLAM:CLAM + 1], 0.5, None, ALU.mult))
            dve.nop().then_inc(scaled, 1)
            ch.then(dve.reciprocal(t["unscale"][:], t["scale"][:]))
            un = t["unscale"]
            ch.then(dve.tensor_tensor(tmp[:, 0:1], un[:, CX:CX + 1], un[:, CX:CX + 1], ALU.mult))
            ch.then(dve.tensor_tensor(tmp[:, 2:3], un[:, CQ1:CQ1 + 1], un[:, CK1:CK1 + 1], ALU.mult))
            ch.then(dve.tensor_tensor(tmp[:, 3:4], un[:, CQ2:CQ2 + 1], un[:, CK2:CK2 + 1], ALU.mult))
            ch.then(dve.tensor_scalar(t["score_scale"][:], tmp[:, 2:4], tmp[:, 0:1], float(HD) ** -0.5, ALU.mult, ALU.mult))
            ch.then(dve.tensor_tensor(tmp[:, 1:2], un[:, CX:CX + 1], un[:, CLAM:CLAM + 1], ALU.mult))
            ch.then(dve.tensor_tensor(tmp[:, 2:3], un[:, CV:CV + 1], un[:, CO:CO + 1], ALU.mult))
            ch.then(dve.tensor_tensor(t["attn_unscale"][:], tmp[:, 1:2], tmp[:, 2:3], ALU.mult))
            ch.then(dve.memset(t["mix_factor"][:, :, 0], 1.0))
            ch.then(dve.tensor_scalar(t["mix_factor"][:, :, 0], t["mix_factor"][:, :, 0], t["scale"][:, CLAM:CLAM + 1], None, ALU.mult))
            ch.then(dve.tensor_scalar(t["mix_factor"][:, :, 1], lam[:], t["scale"][:, CLAM:CLAM + 1], -1.0, ALU.mult, ALU.mult))
            ch.then(dve.tensor_scalar(t["neg_score_scale"][:], t["score_scale"][:], -1.0, None, ALU.mult))
            for k in range(2):
                dve.wait_ge(t["x_hi_ready"], k + 1)
                dve.scalar_tensor_tensor(out=t["x_lo"][:, 0, x_part(k)], in0=x_stage[:, x_part(k)], scalar=t["scale"][:, CX:CX + 1],
                                         in1=t["x_hi"][:, 0, x_part(k)], op0=ALU.mult, op1=ALU.subtract).then_inc(t["x_lo_ready"], 1)
            dve.wait_ge(filt_hi_ready, 1)
            dve.scalar_tensor_tensor(out=filt_halves[:, 1, :], in0=filt[:], scalar=t["scale"][0:FILTERS, CK:CK + 1],
                                     in1=filt_halves[:, 0, :], op0=ALU.mult, op1=ALU.subtract).then_inc(filt_lo_ready, 1)
            for i in range(EARLY):
                weight_lo(dve, t, staged(i), i)


COEF_LAG, MIX_LAG, TR_LAG, PV_LAG, O_LO_LAG = 1, 2, 3, 4, 5
O_SLOTS, RESID_SLOTS, STATS_SLOTS, Y1_SLOTS, YT_SLOTS = (5, 7), (6, 8), (7, 9), (11, 12), (13, 15)
V_SLOTS = (9, 11)
SUM_SLOTS = (8, 10, 13)
X_HI_SLOTS, X_LO_SLOTS = (9, 11), (12, 14)
LATE_HI_SLOTS, LATE_LO_SLOTS = (2, 6), (3, 7)
CTX_SLOTS = (3, 5, 7, 10)
CHUNK = WCOLS // B
TOEP_FILTERS = 8
TOEP_PARTS = 3 * FILTERS // TOEP_FILTERS
PAIRS = 2 * NBLK
COPIES = PER_BLK * 3


def attention(nc, t, d):
    with ExitStack() as ctx:
        sb = lambda name, shape, dt: ctx.enter_context(nc.sbuf_tensor(name, shape, dt))
        sem = lambda name: ctx.enter_context(nc.semaphore(name))
        w_hi, w_lo, ident = 0, 1, t["ident"]
        w4 = lambda half, i: t["w"](half, i).rearrange("p (c n) -> p c n", c=KC)
        xT = sb("xT", [P, 2, KC * S], F32)
        x_hi, x_lo = t["x_hi"], t["x_lo"]
        qk = sb("qk", [P, 2, 4, 2, S], F16)
        stack = sb("stack", [3 * HD, 2, NBLK, PER_BLK, 2, S], F16)
        v = sb("v", [P, 2, SB, D], F32)
        row_max = sb("row_max", [P, 2, 2, SB], F32)
        neg_bias = sb("neg_bias", [P, 2, 2, SB], F32)
        probs = t["probs"]
        sums = sb("sums", [P, 4, 2, SB], F32)
        inv = sb("inv", [P, 4, 2, SB], F32)
        coef = sb("coef", [P, 4, 2, SB], F32)
        scaled2 = sb("scaled2", [P, 2, SB, S], F32)
        mixed = sb("mixed", [P, 2, SB, S], F32)
        mixedT = sb("mixedT", [P, 2, SB, S], F32)
        o_hi = sb("o_hi", [P, NBLK, S], F16)
        o_lo = sb("o_lo", [P, NBLK, S], F16)
        x_rows = sb("x_rows", [P, SB, D], F32)
        resid = sb("resid", [P, SB, D], F32)
        stats = sb("stats", [P, SB, 6], F32)
        moments = sb("moments", [P, SB, 2], F32)
        rstd = sb("rstd", [P, SB], F32)
        nt = [sb(f"newton{k}", [P, SB], F32) for k in range(2)]
        y1 = sb("y1", [P, 2, SB, D], F32)
        w_chunk = sb("w_chunk", [P, 3, CHUNK], F32)
        ps_s = ctx.enter_context(nc.psum_tensor("ps_s", [P, 4, SB, S], F32))
        ps_t = ctx.enter_context(nc.psum_tensor("ps_t", [P, SB, S], F32))
        ps_o = ctx.enter_context(nc.psum_tensor("ps_o", [P, 512], F32))
        ps_p = ctx.enter_context(nc.psum_tensor("ps_p", [P, 2, S], F32))
        ps_g = ctx.enter_context(nc.psum_tensor("ps_g", [P, 512], F32))

        xT_loaded, rows_loaded, chunk_loaded, y1_stored = sem("xT_loaded"), sem("rows_loaded"), sem("chunk_loaded"), sem("y1_stored")
        chunk_summed = sem("chunk_summed")
        x_hi_ready, x_lo_ready = t["x_hi_ready"], t["x_lo_ready"]
        qk_done, qk_hi, qk_lo, stacked = sem("qk_done"), sem("qk_hi"), sem("qk_lo"), sem("stacked")
        v_done, v_ready = sem("v_done"), sem("v_ready")
        scores_done, max_done, bias_ready, exp_done = sem("scores_done"), sem("max_done"), sem("bias_ready"), sem("exp_done")
        inv_done, coef_ready, scaled2_ready, mix_done = sem("inv_done"), sem("coef_ready"), sem("scaled2_ready"), sem("mix_done")
        tr_done, mixedT_ready, pv_done, o_hi_ready, o_lo_ready = (
            sem("tr_done"), sem("mixedT_ready"), sem("pv_done"), sem("o_hi_ready"), sem("o_lo_ready"))
        proj_done, resid_done, stats_done, moments_done = sem("proj_done"), sem("resid_done"), sem("stats_done"), sem("moments_done")
        rstd_chain, y1_ready, yT_done, yT_ready = sem("rstd_chain"), sem("y1_ready"), sem("yT_done"), sem("yT_ready")
        ctx_loaded = [sem(f"ctx_loaded{c}") for c in range(KC)]
        cmax_chain, cmax_ready, call_max_ready, ctx_scale_ready = sem("cmax_chain"), sem("cmax_ready"), sem("call_max_ready"), sem("ctx_scale_ready")
        ctx_chunk = lambda c: t["ctx_T"][:, c * B:c * B + B, :]
        passed = sem("passed_attention")
        block = ctx.enter_context(nc.Block())

        def pair_sum(slot, now):
            return ps_p if now["attend"] else ps_s[:, slot // 2 % 4]

        PREPARE, FIRST, FULL, LAST, DRAIN = (
            dict(project=p, attend=a, close=c) for p, a, c in
            ((True, False, False), (True, True, False), (True, True, True), (False, True, True), (False, False, True)))

        def steps(eng, step):
            step(-1, 1, PREPARE, None)
            step(0, 0, FIRST, PREPARE)
            with eng.Fori(1, B - 2, 2) as b:
                step(b, 1, FULL, FIRST)
                step(b + 1, 0, FULL, FULL)
            step(B - 1, 1, LAST, FULL)
            step(B, 0, DRAIN, LAST)

        def lagging(b, par, slot, lag, now):
            if slot >= lag:
                return (b, slot - lag, par) if now["attend"] else None
            return (b - 1, slot - lag + H, 1 - par) if now["close"] else None

        @block.sync
        def _(sp):
            def step(b, par, now, before):
                n, m = b + 1, b - 1
                if now["project"]:
                    wait_alone(sp, x_hi_ready, n * 2, passed)
                    wait_alone(sp, x_lo_ready, n * 2, passed)
                    wait_alone(sp, xT_loaded, 16 * n, passed)
                    sp.dma_start(xT[:, par, :], d["xT"][:, ds((n + 1) * (KC * S), KC * S)]).then_inc(xT_loaded, 16)
                    wait_alone(sp, chunk_summed, n * 3, passed)
                    sp.dma_start(w_chunk[:], d["wffn"][:, :, ds(n * CHUNK, CHUNK)]).then_inc(chunk_loaded, 16)
                if now == LAST:
                    sp.wait_ge(qk_done, B * PAIRS)
                    sp.wait_ge(v_done, B * SB)
                    for c in range(KC):
                        sp.dma_start(ctx_chunk(c), d["ctxT"][:, c * B:c * B + B, :]).then_inc(ctx_loaded[c], 16)
                for blk in range(NBLK):
                    if now["attend"] and blk == 2:
                        wait_alone(sp, resid_done, b * SB, passed)
                        sp.dma_start(x_rows[:].rearrange("p (o s) n -> p o s n", o=1),
                                     d["x"][ds(b, 1)].rearrange("o (s p) n -> p o s n", p=P)).then_inc(rows_loaded, 16)
                    if now["close"] and blk == 3:
                        wait_alone(sp, y1_ready, (m + 1) * SB, passed)
                        sp.dma_start(d["y1_rows"][ds(m, 1)].rearrange("o (s p) n -> p o s n", p=P),
                                     y1[:, 1 - par, :, :].rearrange("p (o s) n -> p o s n", o=1)).then_inc(y1_stored, 16)
                        wait_alone(sp, y1_stored, 16 * (m + 1), passed)
                    if now["project"]:
                        wait_alone(sp, qk_lo, n * PAIRS + 2 * blk + 2, passed)
                        if now["attend"]:
                            wait_alone(sp, scores_done, b * H + 4 * blk + 4, passed)
                        wait_alone(sp, stacked, (n * NBLK + blk) * COPIES * 16, passed)
                        for j in range(PER_BLK):
                            for row, halves in enumerate((slice(0, 3, 2), slice(0, 4, 3), slice(1, 3))):
                                sp.dma_start(stack[HD * row:HD * row + HD, :, blk, j, :, :],
                                             qk[HD * j:HD * j + HD, blk % 2, halves, :, :]).then_inc(stacked, 16)

            steps(sp, step)

        @block.tensor
        def _(pe):
            def freed(b, now, kind, k):
                n, m = b + 1, b - 1
                if k == 1:
                    s, value = {"o": (resid_done, m * SB + 1), "v": (v_ready, n * SB + 1), "yT": (yT_ready, m * 2 + 1)}[kind]
                elif kind == "o":
                    s, value = yT_ready, m * 2
                elif kind == "v" and now["close"]:
                    s, value = resid_done, (m + 1) * SB
                elif now["project"]:
                    s, value = v_ready, (n + (kind == "yT")) * SB
                else:
                    s, value = resid_done, (m + 1) * SB
                wait(pe, s, value)

            def step(b, par, now, before):
                n, m = b + 1, b - 1
                if now["project"]:
                    pe.wait_ge(x_lo_ready, (n + 1) * 2)
                for slot in range(H):
                    if now["attend"]:
                        blk, j = slot // PER_BLK, slot % PER_BLK
                        if j == 0:
                            pe.wait_ge(stacked, (b * NBLK + blk + 1) * COPIES * 16)
                        wait(pe, exp_done, b * H + slot - 1)
                        for w in range(2):
                            for s in range(SB):
                                ins = pe.matmul(ps_s[:, 2 * (slot % 2) + w, s, :], stack[:, 0, blk, j, w, s * P:s * P + P],
                                                stack[:, 1, blk, j, w, :], start=True, stop=True)
                        ins.then_inc(scores_done, 1)
                    if now["project"] and slot % 2 == 0:
                        blk, w_at = slot // 4, slot % 4
                        wait(pe, qk_lo, n * PAIRS + slot // 2 if now["attend"] else slot // 2 - 3)
                        for i in range(2):
                            for c in range(KC):
                                for k, (w, x) in enumerate(((w_hi, x_hi), (w_hi, x_lo), (w_lo, x_hi))):
                                    ins = pe.matmul(pair_sum(slot, now)[:, i, :], w4(w, w_at + i)[:, c, blk * P:blk * P + P],
                                                    x[:, 1 - par, c * S:c * S + S], start=(c == 0 and k == 0), stop=(c == KC - 1 and k == 2))
                        ins.then_inc(qk_done, 1)
                    if now["project"] and slot in V_SLOTS:
                        s = V_SLOTS.index(slot)
                        if before is None:
                            pe.wait_ge(t["w_lo_ready"], 5)
                        freed(b, now, "v", s)
                        for c in range(KC):
                            for k, (x, w) in enumerate(((x_hi, w_hi), (x_lo, w_hi), (x_hi, w_lo))):
                                ins = pe.matmul(ps_g[:], x[:, 1 - par, c * S + s * P:c * S + s * P + P], w4(w, 4)[:, c, :],
                                                start=(c == 0 and k == 0), stop=(c == KC - 1 and k == 2))
                        ins.then_inc(v_done, 1)
                    if now["close"] and slot in O_SLOTS:
                        s = O_SLOTS.index(slot)
                        pe.wait_ge(o_lo_ready, (m + 1) * NBLK)
                        freed(b, now, "o", s)
                        for c in range(KC):
                            for k, (o, w) in enumerate(((o_hi, w_hi), (o_lo, w_hi), (o_hi, w_lo))):
                                ins = pe.matmul(ps_g[:], o[:, c, s * P:s * P + P], w4(w, 5)[:, c, :],
                                                start=(c == 0 and k == 0), stop=(c == KC - 1 and k == 2))
                        ins.then_inc(proj_done, 1)
                    if now["close"] and slot in YT_SLOTS:
                        k = YT_SLOTS.index(slot)
                        pe.wait_ge(y1_ready, (m + 1) * SB)
                        freed(b, now, "yT", k)
                        for c in range(2):
                            for s in range(SB):
                                ins = pe.matmul(ps_g[:, c * S + s * P:c * S + s * P + P],
                                                y1[:, 1 - par, s, (2 * k + c) * P:(2 * k + c + 1) * P], ident[:],
                                                start=True, stop=True, is_transpose=True, skip_group_check=True)
                        ins.then_inc(yT_done, 1)
                    if (at := lagging(b, par, slot, TR_LAG, now)) is not None:
                        q, h, _ = at
                        pe.wait_ge(mix_done, q * H + h + 1)
                        wait(pe, mixedT_ready, q * H + h)
                        for kb in range(SB):
                            for s in range(SB):
                                ins = pe.matmul(ps_t[:, kb, s * P:s * P + P], mixed[:, h % 2, s, kb * P:kb * P + P], ident[:],
                                                start=True, stop=True, is_transpose=True, skip_group_check=True)
                        ins.then_inc(tr_done, 1)
                    if (at := lagging(b, par, slot, PV_LAG, now)) is not None:
                        q, h, qp = at
                        blk, j = h // PER_BLK, h % PER_BLK
                        if h == 0:
                            pe.wait_ge(v_ready, (q + 1) * SB)
                        if j == 0:
                            wait(pe, o_lo_ready, q * NBLK + blk)
                        pe.wait_ge(mixedT_ready, q * H + h + 1)
                        for kb in range(SB):
                            ins = pe.matmul(ps_o[HD * j:HD * j + HD, 0:S], v[:, qp, kb, h * HD:h * HD + HD], mixedT[:, h % 2, kb, :],
                                            start=(kb == 0), stop=(kb == SB - 1), skip_group_check=True)
                        if j == PER_BLK - 1:
                            ins.then_inc(pv_done, 1)

                if before is None:
                    pe.wait_ge(t["w_lo_ready"], 6)
                    pe.wait_ge(qk_lo, PAIRS)

            steps(pe, step)

        @block.scalar
        def _(act):
            def load_scale(name, at):
                reg = act.alloc_register(name)
                act.reg_load(reg, at.bitcast(I32))
                return reg

            x_scale = load_scale("x_scale", t["scale"][0:1, CX:CX + 1])
            score_scale = [load_scale(f"score_scale{w}", t["score_scale"][0:1, w:w + 1]) for w in range(2)]

            def split_x(n, par, k):
                act.wait_ge(xT_loaded, n * 16)
                wait(act, v_done, (n - 1) * SB)
                act.activation(x_hi[:, par, x_part(k)], xT[:, par, x_part(k)], ACT.Copy, scale=x_scale).then_inc(x_hi_ready, 1)

            def toeplitz(part):
                which, at = part % 3, part // 3 * TOEP_FILTERS
                if which < 2:
                    src, width, dst = d["filt_halves"], D, d["toeplitz"][at:at + TOEP_FILTERS, which]
                else:
                    src, width, dst = d["filt_whole"], NEAR, d["toeplitz_near"][at:at + TOEP_FILTERS]
                src = bass.AP(tensor=src.tensor, offset=(which % 2 * FILTERS + at) * (width + P) + P,
                              ap=[[width + P, TOEP_FILTERS], [-1, P], [1, width]])
                act.dma_start(dst, src).then_inc(t["toep_written"], 16)

            def step(b, par, now, before):
                n, m = b + 1, b - 1
                for slot in range(H):
                    if before == PREPARE and slot == 0:
                        act.wait_ge(t["w_lo_ready"], 6)
                    if before == PREPARE and slot >= H - TOEP_PARTS:
                        toeplitz(slot - (H - TOEP_PARTS))
                    if now["attend"]:
                        act.wait_ge(bias_ready, b * H + slot + 1)
                        wait(act, mix_done, b * H + slot - 3)
                        for w in range(2):
                            for s in range(SB):
                                ins = act.activation(probs[:, slot % 4, w, s, :], ps_s[:, 2 * (slot % 2) + w, s, :], ACT.Exp,
                                                     bias=neg_bias[:, slot % 2, w, s:s + 1], scale=score_scale[w],
                                                     accum_out=sums[:, slot % 4, w, s:s + 1])
                        ins.then_inc(exp_done, 1)
                    if (at := lagging(b, par, slot, TR_LAG, now)) is not None:
                        q, h, _ = at
                        act.wait_ge(tr_done, q * H + h + 1)
                        act.copy(mixedT[:, h % 2, :, :], ps_t[:]).then_inc(mixedT_ready, 1)
                    if now["project"] and slot % 2 == 0:
                        blk, w = slot // 4, slot // 2 % 2
                        act.wait_ge(qk_done, n * PAIRS + slot // 2 + 1)
                        if w == 0:
                            wait(act, stacked, (n * NBLK + blk - 1) * COPIES * 16)
                        act.copy(qk[:, blk % 2, 0:4:2, w, :], pair_sum(slot, now)[:]).then_inc(qk_hi, 1)
                    if (at := lagging(b, par, slot, PV_LAG, now)) is not None and at[1] % PER_BLK == PER_BLK - 1:
                        q, h, _ = at
                        blk = h // PER_BLK
                        act.wait_ge(pv_done, q * NBLK + blk + 1)
                        act.copy(o_hi[:, blk, :], ps_o[:, 0:S]).then_inc(o_hi_ready, 1)
                    if now["project"] and slot in V_SLOTS:
                        s = V_SLOTS.index(slot)
                        act.wait_ge(v_done, n * SB + s + 1)
                        wait(act, pv_done, (n - 1) * NBLK)
                        act.copy(v[:, 1 - par, s, :], ps_g[:]).then_inc(v_ready, 1)
                    if now["close"] and slot in YT_SLOTS:
                        k = YT_SLOTS.index(slot)
                        act.wait_ge(yT_done, m * 2 + k + 1)
                        act.copy(t["y1T"][:, 2 * k:2 * k + 2, ds(m, 1), :],
                                 ps_g[:].rearrange("p (c o s) -> p c o s", c=2, o=1)).then_inc(yT_ready, 1)
                    if before is None and slot in LATE_HI_SLOTS:
                        i = EARLY + LATE_HI_SLOTS.index(slot)
                        weight_hi(act, t, t["late_stage"](i), i)
                    if now["project"] and slot in X_HI_SLOTS:
                        split_x(n + 1, par, X_HI_SLOTS.index(slot))

            steps(act, step)
            act.wait_ge(ctx_scale_ready, 1)
            for c in (2, 3):
                act.activation(ctx_chunk(c), ctx_chunk(c), ACT.Copy, scale=t["ctx_scal"][:, 1:2]).then_inc(t["ctx_scaled"], 1)
            act.wait_ge(yT_ready, 2 * B)

        @block.gpsimd
        def _(pool):
            def step(b, par, now, before):
                m = b - 1
                for slot in range(H):
                    if (at := lagging(b, par, slot, COEF_LAG, now)) is not None:
                        q, h, _ = at
                        wait_alone(pool, coef_ready, q * H + h + 1, passed)
                        wait_alone(pool, mix_done, q * H + h - 1, passed)
                        pool.tensor_tensor(scaled2[:, h % 2], probs[:, h % 4, 1], coef[:, h % 4, 1].unsqueeze(2).broadcast_to([P, SB, S]),
                                           ALU.mult).then_inc(scaled2_ready, 1)
                    if now["close"] and slot == STATS_SLOTS[-1]:
                        wait_alone(pool, moments_done, (m + 1) * SB, passed)
                        rsqrt(Chain(pool, rstd_chain, m * RSQRT_STEPS, passed), pool, rstd[:], moments[:, :, 1], nt)

            steps(pool, step)
            pool.wait_ge(cmax_ready, 1)
            pool.partition_all_reduce(t["ctx_scal"][:, 3:4], t["ctx_max"][:, KC:KC + 1], P, RMAX).then_inc(call_max_ready, 1)

        @block.vector
        def _(dve):
            def ctx_maximum(c):
                dve.wait_ge(ctx_loaded[c], 16)
                dve.tensor_reduce(t["ctx_max"][:, c:c + 1], ctx_chunk(c).rearrange("p b s -> p (b s)"), AX, ALU.max,
                                  apply_absolute_value=True).then_inc(cmax_chain, 1)

            def split_x(n, par, k):
                dve.wait_ge(x_hi_ready, n * 2 + k + 1)
                wait(dve, v_done, (n - 1) * SB)
                dve.scalar_tensor_tensor(out=x_lo[:, par, x_part(k)], in0=xT[:, par, x_part(k)], scalar=t["scale"][:, CX:CX + 1],
                                         in1=x_hi[:, par, x_part(k)], op0=ALU.mult, op1=ALU.subtract).then_inc(x_lo_ready, 1)

            def step(b, par, now, before):
                n, m = b + 1, b - 1
                for slot in range(H):
                    if now == DRAIN and slot in CTX_SLOTS:
                        ctx_maximum(CTX_SLOTS.index(slot))
                    if now["attend"]:
                        dve.wait_ge(scores_done, b * H + slot + 1)
                        if isinstance(b, int) and b * H + slot >= 2 or not isinstance(b, int):
                            dve.wait_ge(exp_done, b * H + slot - 1)
                        hp = slot % 2
                        dve.tensor_reduce(row_max[:, hp], ps_s[:, 2 * hp:2 * hp + 2], AX, ALU.max).then_inc(max_done, 1)
                    coefs = lagging(b, par, slot, COEF_LAG, now)
                    if coefs is not None:
                        q, h, _ = coefs
                        dve.wait_ge(exp_done, q * H + h + 1)
                        dve.reciprocal(inv[:, h % 4], sums[:, h % 4]).then_inc(inv_done, 1)
                    if now["attend"]:
                        dve.wait_ge(max_done, b * H + slot + 1)
                        dve.tensor_tensor(neg_bias[:, hp], row_max[:, hp], t["neg_score_scale"][:].unsqueeze(2).broadcast_to([P, 2, SB]),
                                          ALU.mult).then_inc(bias_ready, 1)
                    if coefs is not None:
                        q, h, _ = coefs
                        dve.wait_ge(inv_done, q * H + h + 1)
                        dve.tensor_tensor(coef[:, h % 4], inv[:, h % 4], t["mix_factor"][:, h, :].unsqueeze(2).broadcast_to([P, 2, SB]),
                                          ALU.mult).then_inc(coef_ready, 1)
                    if now["project"] and slot % 2 == 1:
                        blk, w = slot // 4, slot // 2 % 2
                        dve.wait_ge(qk_hi, n * PAIRS + slot // 2 + 1)
                        dve.tensor_tensor(qk[:, blk % 2, 1:4:2, w, :], pair_sum(slot, now)[:], qk[:, blk % 2, 0:4:2, w, :], ALU.subtract).then_inc(qk_lo, 1)
                    if (at := lagging(b, par, slot, MIX_LAG, now)) is not None:
                        q, h, _ = at
                        dve.wait_ge(scaled2_ready, q * H + h + 1)
                        wait(dve, tr_done, q * H + h - 1)
                        for s in range(SB):
                            ins = dve.scalar_tensor_tensor(out=mixed[:, h % 2, s, :], in0=probs[:, h % 4, 0, s, :], scalar=coef[:, h % 4, 0, s:s + 1],
                                                           in1=scaled2[:, h % 2, s, :], op0=ALU.mult, op1=ALU.add)
                        ins.then_inc(mix_done, 1)
                    if (at := lagging(b, par, slot, O_LO_LAG, now)) is not None and at[1] % PER_BLK == PER_BLK - 1:
                        q, h, _ = at
                        blk = h // PER_BLK
                        dve.wait_ge(o_hi_ready, q * NBLK + blk + 1)
                        dve.tensor_tensor(o_lo[:, blk, :], ps_o[:, 0:S], o_hi[:, blk, :], ALU.subtract).then_inc(o_lo_ready, 1)
                    if now["close"] and slot in STATS_SLOTS:
                        s = STATS_SLOTS.index(slot)
                        dve.wait_ge(resid_done, m * SB + s + 1)
                        dve.bn_stats(stats[:, s, :], resid[:, s, :]).then_inc(stats_done, 1)
                    if now["close"] and slot in RESID_SLOTS:
                        s = RESID_SLOTS.index(slot)
                        dve.wait_ge(proj_done, m * SB + s + 1)
                        if s == 0:
                            dve.wait_ge(rows_loaded, (m + 1) * 16)
                            if isinstance(b, int):
                                wait(dve, y1_ready, m * SB)
                        dve.scalar_tensor_tensor(out=resid[:, s, :], in0=ps_g[:], scalar=t["attn_unscale"][:, 0:1],
                                                 in1=x_rows[:, s, :], op0=ALU.mult, op1=ALU.add).then_inc(resid_done, 1)
                    if now["project"] and slot in SUM_SLOTS:
                        k = SUM_SLOTS.index(slot)
                        dve.wait_ge(chunk_loaded, (n + 1) * 16)
                        dve.tensor_reduce(t["w_sums"][:, ds(n, 1), k:k + 1], w_chunk[:, k:k + 1, :].unsqueeze(1), AX, ALU.add,
                                          apply_absolute_value=True).then_inc(chunk_summed, 1)
                    if now["close"] and slot in STATS_SLOTS:
                        s = STATS_SLOTS.index(slot)
                        wait_alone(dve, stats_done, m * SB + s + 1, passed)
                        dve.bn_aggr(moments[:, s, :], stats[:, s, :]).then_inc(moments_done, 1)
                    if now["close"] and slot in Y1_SLOTS:
                        s = Y1_SLOTS.index(slot)
                        dve.wait_ge(rstd_chain, (m + 1) * RSQRT_STEPS)
                        if isinstance(b, int):
                            wait(dve, yT_done, (m - 1) * 2)
                            wait(dve, y1_stored, (m - 1) * 16)
                        dve.tensor_scalar(y1[:, 1 - par, s, :], resid[:, s, :], moments[:, s, 0:1], rstd[:, s:s + 1],
                                          ALU.subtract, ALU.mult).then_inc(y1_ready, 1)
                    if before is None and slot in LATE_LO_SLOTS:
                        i = EARLY + LATE_LO_SLOTS.index(slot)
                        weight_lo(dve, t, t["late_stage"](i), i)
                    if now["project"] and slot in X_LO_SLOTS:
                        split_x(n + 1, par, X_LO_SLOTS.index(slot))

            steps(dve, step)
            dve.wait_ge(cmax_chain, KC)
            dve.tensor_reduce(t["ctx_max"][:, KC:KC + 1], t["ctx_max"][:, 0:KC], AX, ALU.max).then_inc(cmax_ready, 1)
            dve.wait_ge(call_max_ready, 1)
            ch = Chain(dve, cmax_chain, KC)
            pow2, scale, unscale, squared = (t["ctx_scal"][:, k:k + 1] for k in range(4))
            ch.then(dve.tensor_scalar(unscale, squared, 1e-30, None, ALU.max))
            ch.then(dve.tensor_scalar(pow2.bitcast(I32), unscale.bitcast(I32), EXP_MASK, None, ALU.bitwise_and))
            ch.then(dve.reciprocal(scale, pow2))
            ch.then(dve.tensor_scalar(scale, scale, 512.0, None, ALU.mult))
            dve.nop().then_inc(ctx_scale_ready, 1)
            for c in (0, 1):
                dve.tensor_scalar(ctx_chunk(c), ctx_chunk(c), scale, None, ALU.mult).then_inc(t["ctx_scaled"], 1)
            ch.then(dve.tensor_scalar(unscale, pow2, 1.0 / 512.0, None, ALU.mult))
            ch.then(dve.tensor_tensor(squared, unscale, unscale, ALU.mult))
            ch.then(dve.tensor_tensor(t["conv_unscale"][:], squared, t["unscale"][:, CK:CK + 1], ALU.mult))
            dve.wait_ge(y1_ready, B * SB)
            dve.wait_ge(t["ctx_scaled"], KC)


FW = WCOLS // FILTERS
GROUPS = KC * B


def convolution(nc, t, d):
    with ExitStack() as ctx:
        sb = lambda name, shape, dt: ctx.enter_context(nc.sbuf_tensor(name, shape, dt))
        sem = lambda name: ctx.enter_context(nc.semaphore(name))
        ctx_T = t["ctx_T"]
        skip = sb("skip", [P, S], F32)
        toep = sb("toep", [P, 2, 2, D], F16)
        toep_near = sb("toep_near", [P, 2, NEAR], F32)
        prod = sb("prod", [P, 2, GROUPS, CH, CH], F32)
        prod_hi = sb("prod_hi", [P, 2, CUT * B, CH, CH], F16)
        prod_lo = sb("prod_lo", [P, 2, CUT * B, CH, CH], F16)
        gated = sb("gated", [P, 2, GROUPS, CH, CH], F32)
        half_sum = sb("half_sum", [P, 2, GROUPS, CH // 2, CH], F32)
        summed = sb("summed", [P, GROUPS, CH], F32)
        vx = sb("vx", [P, GROUPS, CH], F32)
        vxs = sb("vxs", [P, 2, GROUPS, CH], F32)
        u = sb("u", [P, 2, GROUPS], F32)
        skip_term = sb("skip_term", [P, 2, GROUPS, CH], F32)
        w_part = sb("w_part", [P, 2, 2, FW], F32)
        sign = sb("sign", [P, 2, FW], F16)
        below = sb("below", [P, 2, 2, FW], F16)
        wsum = sb("wsum", [P, 3], F32)
        wall = sb("wall", [P, 3], F32)
        limit = t["limit"]
        ps = ctx.enter_context(nc.psum_tensor("ps_conv", [P, 2, KC, 512], F32))

        skip_loaded, toep_loaded, part_loaded = sem("skip_loaded"), sem("toep_loaded"), sem("part_loaded")
        conv_chain, wsum_ready, wall_ready, skip_scaled = sem("conv_chain"), sem("wsum_ready"), sem("wall_ready"), sem("skip_scaled")
        cut_ready, whole_ready, hi_ready, lo_ready = sem("cut_ready"), sem("whole_ready"), sem("hi_ready"), sem("lo_ready")
        conv_done, gated_done, half_done, summed_done = sem("conv_done"), sem("gated_done"), sem("half_done"), sem("summed_done")
        vx_done, vxs_done, u_done, skip_done, out_done = sem("vx_done"), sem("vxs_done"), sem("u_done"), sem("skip_done"), sem("out_done")
        limit_ready, sign_done, below_done, ternary_done = sem("limit_ready"), sem("sign_done"), sem("below_done"), sem("ternary_done")
        passed = sem("passed_convolution")
        block = ctx.enter_context(nc.Block())
        y1T = t["y1T"][:].rearrange("p c b s -> p (c b) s")
        conv_T = t["conv_T"]

        @block.sync
        def _(sp):
            sp.dma_start(skip[:], d["skip"].rearrange("(o n) -> o n", o=1).broadcast_to([P, S])).then_inc(skip_loaded, 16)

            def load(h, par):
                wait_alone(sp, conv_done, (h - 1) * 2, passed)
                wait_alone(sp, toep_loaded, h * 32, passed)
                sp.dma_start(toep[:, par, :, :].unsqueeze(1), d["toeplitz"][ds(h, 1)].rearrange("o a p n -> p o a n")).then_inc(toep_loaded, 16)
                sp.dma_start(toep_near[:, par, :].unsqueeze(1), d["toeplitz_near"][ds(h, 1)].rearrange("o p n -> p o n")).then_inc(toep_loaded, 16)
                wait_alone(sp, ternary_done, (h - 1) * 2, passed)
                wait_alone(sp, part_loaded, h * 16, passed)
                sp.dma_start(w_part[:, par], d["wffn"][:, 0:2, ds(h * FW, FW)]).then_inc(part_loaded, 16)

            sp.wait_ge(t["toep_written"], 16 * TOEP_PARTS)
            filters(sp, load)

        @block.tensor
        def _(pe):
            def conv(h, par):
                wait(pe, gated_done, (h - 1) * 2)
                pe.wait_ge(toep_loaded, (h + 1) * 32)
                pe.wait_ge(hi_ready, h + 1)
                near = lambda lb, mb: toep_near[:, par, (lb - mb) * P:(lb - mb + 1) * P]
                cut = lambda half, lb, mb: toep[:, par, half, (lb - mb) * P:(lb - mb + 1) * P]
                for k in range(2):
                    if k == 1:
                        pe.wait_ge(whole_ready, h + 1)
                    lbs = range(2 * k, 2 * k + 2)
                    terms = [(lb, cut(w, lb, mb), prod_hi, mb) for lb in lbs for mb in range(min(lb + 1, CUT)) for w in range(2)]
                    terms += [(lb, near(lb, mb), prod, mb) for lb in lbs for mb in range(CUT, lb + 1)]
                    terms += [(lb, cut(0, lb, mb), prod_lo, mb) for lb in lbs for mb in range(min(lb + 1, CUT))]
                    for n, (lb, w, products, mb) in enumerate(terms):
                        if k == 0 and products is prod_lo:
                            pe.wait_ge(lo_ready, h + 1)
                        ins = pe.matmul(ps[:, par, lb, :], w, products[:, par, mb * B:mb * B + B].rearrange("p b i j -> p (b i j)"),
                                        start=all(x[0] != lb for x in terms[:n]), stop=all(x[0] != lb for x in terms[n + 1:]),
                                        skip_group_check=True)
                    ins.then_inc(conv_done, 1)

            filters(pe, conv)

        of_filter = lambda tile, h: tile[:, :, ds(h * CH, CH)]
        cut, whole = slice(0, CUT * B), slice(CUT * B, GROUPS)

        @block.scalar
        def _(act):
            def below_limit(h, par):
                act.wait_ge(part_loaded, (h + 1) * 16)
                wait(act, ternary_done, (h - 1) * 2)
                for k in range(2):
                    wait(act, below_done, (h - 1) * 2 + k + 1)
                    act.activation(sign[:, k, :], w_part[:, par, k, :], ACT.Sign, bias=limit[:, 1, k:k + 1], scale=-1.0).then_inc(sign_done, 1)
                for k in range(2):
                    act.wait_ge(sign_done, h * 2 + k + 1)
                    act.activation(below[:, par, k, :], sign[:, k, :], ACT.Relu).then_inc(below_done, 1)

            def step(h, par):
                below_limit(h, par)
                if not isinstance(h, int) or h < FILTERS - 2:
                    split(h + 2, par)

            def split(h, par):
                act.wait_ge(cut_ready, h + 1)
                wait(act, conv_done, (h - 1) * 2)
                act.copy(prod_hi[:, par], prod[:, par, cut]).then_inc(hi_ready, 1)

            split(0, 0)
            split(1, 1)
            act.wait_ge(limit_ready, 1)
            filters(act, step)

        @block.gpsimd
        def _(pool):
            pool.wait_ge(wsum_ready, 1)
            pool.partition_all_reduce(wall[:], wsum[:], P, RADD).then_inc(wall_ready, 1)

            def low(h, par):
                wait_alone(pool, hi_ready, h + 1, passed)
                wait_alone(pool, conv_done, (h - 1) * 2, passed)
                pool.tensor_tensor(prod_lo[:, par], prod[:, par, cut], prod_hi[:, par], ALU.subtract).then_inc(lo_ready, 1)

            def halve(h, par):
                wait_alone(pool, gated_done, h * 2 + 2, passed)
                wait_alone(pool, summed_done, h - 1, passed)
                pool.tensor_tensor(half_sum[:, par], gated[:, par, :, 0:CH // 2], gated[:, par, :, CH // 2:CH], ALU.add).then_inc(half_done, 1)

            def skip_rows(h, par):
                wait_alone(pool, vxs_done, h, passed)
                pool.tensor_tensor(vx[:], of_filter(y1T, h), of_filter(ctx_T, h), ALU.mult).then_inc(vx_done, 1)
                wait_alone(pool, vx_done, h + 1, passed)
                wait_alone(pool, u_done, h - 1, passed)
                pool.tensor_tensor(vxs[:, par], vx[:], skip[:, ds(h * CH, CH)].unsqueeze(1).broadcast_to([P, GROUPS, CH]),
                                   ALU.mult).then_inc(vxs_done, 1)

            def step(h, par):
                static = isinstance(h, int)
                if not static or h < FILTERS - 2:
                    low(h + 2, par)
                halve(h, par)
                if not static or h < FILTERS - 1:
                    skip_rows(h + 1, 1 - par)
                wait_alone(pool, u_done, h + 1, passed)
                wait_alone(pool, out_done, h - 1, passed)
                pool.tensor_tensor(skip_term[:, par], of_filter(ctx_T, h), u[:, par].unsqueeze(2).broadcast_to([P, GROUPS, CH]),
                                   ALU.mult).then_inc(skip_done, 1)

            low(0, 0)
            low(1, 1)
            pool.wait_ge(skip_scaled, 1)
            skip_rows(0, 0)
            filters(pool, step)

        @block.vector
        def _(dve):
            ch = Chain(dve, conv_chain)
            dve.tensor_reduce(wsum[:], t["w_sums"][:].rearrange("p b k -> p k b"), AX, ALU.add).then_inc(wsum_ready, 1)

            def product(h, par, groups, ready):
                n = groups.stop - groups.start
                at = (slice(None), groups, ds(h * CH, CH))
                dve.tensor_tensor(prod[:, par, groups], y1T[at].unsqueeze(3).broadcast_to([P, n, CH, CH]),
                                  ctx_T[at].unsqueeze(2).broadcast_to([P, n, CH, CH]), ALU.mult).then_inc(ready, 1)

            def product_cut(h, par):
                wait(dve, lo_ready, h - 1)
                product(h, par, cut, cut_ready)

            def product_whole(h, par):
                wait(dve, conv_done, (h - 1) * 2)
                product(h, par, whole, whole_ready)

            def row_sum(h, par):
                dve.wait_ge(half_done, h + 1)
                wait(dve, out_done, h)
                dve.tensor_reduce(summed[:], half_sum[:, par].rearrange("p g i j -> p g j i"), AX, ALU.add).then_inc(summed_done, 1)

            def add_skip(h, par):
                dve.wait_ge(summed_done, h + 1)
                dve.wait_ge(skip_done, h + 1)
                dve.tensor_tensor(of_filter(conv_T, h), summed[:], skip_term[:, par], ALU.add).then_inc(out_done, 1)

            def skip_sum(h, par):
                dve.wait_ge(vxs_done, h + 1)
                wait(dve, skip_done, h - 1)
                dve.tensor_reduce(u[:, par], vxs[:, par], AX, ALU.add).then_inc(u_done, 1)

            def gate(h, par, k):
                half = GROUPS // 2
                if k == 0:
                    wait(dve, half_done, h - 1)
                dve.wait_ge(conv_done, h * 2 + k + 1)
                dve.tensor_tensor(gated[:, par, k * half:(k + 1) * half], ps[:, par, 2 * k:2 * k + 2, :].rearrange("p c (b i j) -> p (c b) i j", b=B, i=CH),
                                  ctx_T[:, k * half:(k + 1) * half, ds(h * CH, CH)].unsqueeze(3).broadcast_to([P, half, CH, CH]),
                                  ALU.mult).then_inc(gated_done, 1)

            def step(h, par):
                static = isinstance(h, int)
                gate(h, par, 0)
                if not static or h < FILTERS - 1:
                    product_whole(h + 1, 1 - par)
                if not static or h < FILTERS - 2:
                    product_cut(h + 2, par)
                for k in range(2):
                    dve.wait_ge(below_done, h * 2 + k + 1)
                    dve.scalar_tensor_tensor(out=t["ternary"][:, k, ds(h * FW, FW)], in0=w_part[:, par, k, :], scalar=limit[:, 0, k:k + 1],
                                             in1=below[:, par, k, :], op0=ALU.is_gt, op1=ALU.subtract).then_inc(ternary_done, 1)
                if not static or h > 0:
                    row_sum(h - 1, 1 - par)
                gate(h, par, 1)
                skip_sum(h, par)
                if not static or h > 0:
                    add_skip(h - 1, 1 - par)

            product_cut(0, 0)
            product_whole(0, 0)
            product_cut(1, 1)
            dve.wait_ge(skip_loaded, 16)
            dve.tensor_scalar(skip[:], skip[:], t["scale"][:, CK:CK + 1], None, ALU.mult).then_inc(skip_scaled, 1)
            dve.wait_ge(wall_ready, 1)
            ch.then(dve.tensor_scalar(t["w_mean"][:], wall[:], float(np.float32(1.0 / (HID * D))), None, ALU.mult))
            ch.then(dve.tensor_scalar(limit[:, 0, :], t["w_mean"][:], 0.5, None, ALU.mult))
            ch.then(dve.tensor_scalar(limit[:, 1, :], t["w_mean"][:], -0.5, None, ALU.mult))
            dve.nop().then_inc(limit_ready, 1)
            filters(dve, step)
            row_sum(FILTERS - 1, 1)
            add_skip(FILTERS - 1, 1)
            dve.wait_ge(out_done, FILTERS)
            dve.wait_ge(ternary_done, 2 * FILTERS)


def filters(eng, step):
    step(0, 0)
    step(1, 1)
    with eng.Fori(2, FILTERS - 3, 2) as h:
        step(h, 0)
        step(h + 1, 1)
    step(FILTERS - 2, 0)
    step(FILTERS - 1, 1)


OUT_LAG = 2
BACK_AT, RESID_AT, STATS_AT, Y2_AT, Y2T_AT, Y2_HI_AT, Y2_LO_AT = 1, (2, 3), (3, 4), 7, HC - 1, HC - 1, HC
RESID3_AT, STATS3_AT, OUT_AT = 0, (1, 2), 8


def feed_forward(nc, t, d):
    with ExitStack() as ctx:
        sb = lambda name, shape, dt: ctx.enter_context(nc.sbuf_tensor(name, shape, dt))
        sem = lambda name: ctx.enter_context(nc.semaphore(name))
        ident = t["ident"]
        conv_b = sb("conv_b", [P, 2, KC, S], F32)
        y1 = sb("y1_back", [P, 2, SB, D], F32)
        resid = sb("resid2", [P, SB, D], F32)
        resid3 = sb("resid3", [P, SB, D], F32)
        stats = sb("stats2", [P, 2, SB, 6], F32)
        moments = sb("moments2", [P, 2, SB, 2], F32)
        rstd = sb("rstd2", [P, 2, SB], F32)
        nt = [sb(f"newton2_{k}", [P, 2, SB], F32) for k in range(2)]
        y2 = sb("y2", [P, 2, SB, D], F32)
        y2_hi = sb("y2_hi", [P, 2, KC, S], F16)
        y2_lo = sb("y2_lo", [P, 2, KC, S], F16)
        th = sb("th", [P, 2, S], F32)
        act_h1 = sb("act_h1", [P, 2, S], F32)
        g = sb("g", [P, 2, S], F32)
        g_hi = sb("g_hi", [P, 4, S], F16)
        g_lo = sb("g_lo", [P, 4, S], F16)
        out = sb("out", [P, 2, SB, D], F32)
        w2_raw = t["ctx_T"][:].rearrange("p g s -> p (g s)")[:, 0:WCOLS]
        w2_below = sb("w2_below", [P, 2, D], F16)
        scal = sb("ffn_scal", [P, 2], F32)
        ps_f = ctx.enter_context(nc.psum_tensor("ps_f", [P, 2, 512], F32))
        ps_h = ctx.enter_context(nc.psum_tensor("ps_h", [P, 4, 2, S], F32))
        ps_y = ctx.enter_context(nc.psum_tensor("ps_y", [P, SB, D], F32))

        conv_loaded, y1_loaded, stored = sem("conv_loaded"), sem("y1_loaded"), sem("stored")
        scal_chain, scal_ready = sem("scal_chain"), sem("scal_ready")
        back_done, resid_done, stats_done, moments_done = sem("back_done"), sem("resid2_done"), sem("stats2_done"), sem("moments2_done")
        rstd_chain, y2_ready, y2T_done, y2_hi_ready, y2_lo_ready = (
            sem("rstd2_chain"), sem("y2_ready"), sem("y2T_done"), sem("y2_hi_ready"), sem("y2_lo_ready"))
        h_done, th_ready, h1_ready, g_ready, g_hi_ready, g_lo_ready, y_done = (
            sem("h_done"), sem("th_ready"), sem("h1_ready"), sem("g_ready"), sem("g_hi_ready"), sem("g_lo_ready"), sem("y_done"))
        resid3_done, stats3_done, moments3_done, out_ready = sem("resid3_done"), sem("stats3_done"), sem("moments3_done"), sem("out_ready")
        w2_loaded, w2_below_done, w2_ready = sem("w2_loaded"), sem("w2_below_done"), sem("w2_ready")
        passed = sem("passed_feed_forward")
        block = ctx.enter_context(nc.Block())
        conv_T = t["conv_T"][:].rearrange("p (c b) s -> p c b s", c=KC)
        w13 = t["ternary"][:].rearrange("p k (c n) -> p k c n", c=KC)
        w2 = t["ternary"][:, 2, :].rearrange("p (c n) -> p c n", c=HC)

        def steps(eng, step):
            step(-1, 1, True, False, False)
            step(0, 0, True, True, False)
            step(1, 1, True, True, True)
            with eng.Fori(2, B - 3, 2) as b:
                step(b, 0, True, True, True)
                step(b + 1, 1, True, True, True)
            step(B - 2, 0, True, True, True)
            step(B - 1, 1, False, True, True)
            step(B, 0, False, False, True)

        @block.sync
        def _(sp):
            def store(m, par):
                wait_alone(sp, out_ready, (m + 1) * SB, passed)
                sp.dma_start(d["out"][ds(m, 1)].rearrange("o (s p) n -> p o s n", p=P),
                             out[:, par, :, :].rearrange("p (o s) n -> p o s n", o=1)).then_inc(stored, 16)
                wait_alone(sp, stored, (m + 1) * 16, passed)

            def step(b, par, front, main, finish):
                if front:
                    n = b + 1
                    wait_alone(sp, back_done, (n - 1) * SB, passed)
                    wait_alone(sp, resid_done, (n - 1) * SB, passed)
                    wait_alone(sp, conv_loaded, n * 16, passed)
                    sp.dma_start(conv_b[:, 1 - par].unsqueeze(2), conv_T[:, :, ds(n, 1), :]).then_inc(conv_loaded, 16)
                    wait_alone(sp, y1_loaded, n * 16, passed)
                    sp.dma_start(y1[:, 1 - par].rearrange("p (o s) n -> p o s n", o=1),
                                 d["y1_rows"][ds(n, 1)].rearrange("o (s p) n -> p o s n", p=P)).then_inc(y1_loaded, 16)
                    if not main:
                        sp.dma_start(w2_raw, d["wffn"][:, 2, :]).then_inc(w2_loaded, 16)
                if finish:
                    store(b - 1, 1 - par)

            steps(sp, step)

        @block.tensor
        def _(pe):
            def back(n, par):
                pe.wait_ge(conv_loaded, (n + 1) * 16)
                for s in range(SB):
                    wait(pe, y2_lo_ready, n * 2)
                    for c in range(KC):
                        ins = pe.matmul(ps_f[:, s, c * P:c * P + P], conv_b[:, par, c, s * P:s * P + P], ident[:],
                                        start=True, stop=True, is_transpose=True, skip_group_check=True)
                    ins.then_inc(back_done, 1)

            def y2_transposes(n, par):
                pe.wait_ge(y2_ready, (n + 1) * SB)
                for k in range(2):
                    for c in range(2):
                        for s in range(SB):
                            ins = pe.matmul(ps_f[:, k, c * S + s * P:c * S + s * P + P], y2[:, par, s, (2 * k + c) * P:(2 * k + c + 1) * P],
                                            ident[:], start=True, stop=True, is_transpose=True, skip_group_check=True)
                    ins.then_inc(y2T_done, 1)

            def hidden(b, par, c):
                wait(pe, g_ready, b * HC + c - 3)
                for k in range(2):
                    for kc in range(KC):
                        for half, x in enumerate((y2_hi, y2_lo)):
                            ins = pe.matmul(ps_h[:, c % 4, k, :], w13[:, k, kc, c * P:c * P + P], x[:, par, kc, :],
                                            start=(kc == 0 and half == 0), stop=(kc == KC - 1 and half == 1), skip_group_check=True)
                ins.then_inc(h_done, 1)

            def down(b, par, c):
                pe.wait_ge(g_lo_ready, b * HC + c + 1)
                if isinstance(b, int) and b == 0:
                    pe.wait_ge(w2_ready, c + 1)
                if c == 0:
                    wait(pe, resid3_done, b * SB)
                for s in range(SB):
                    for half, x in enumerate((g_hi, g_lo)):
                        ins = pe.matmul(ps_y[:, s, :], x[:, c % 4, s * P:s * P + P], w2[:, c, :],
                                        start=(c == 0 and half == 0), stop=(c == HC - 1 and half == 1), skip_group_check=True)
                    if c == HC - 1:
                        ins.then_inc(y_done, 1)

            def step(b, par, front, main, finish):
                if not main:
                    if front:
                        back(b + 1, 1 - par)
                        y2_transposes(b + 1, 1 - par)
                    return
                pe.wait_ge(y2_lo_ready, (b + 1) * 2)
                for c in range(HC + OUT_LAG):
                    if c < HC:
                        hidden(b, par, c)
                    if c == BACK_AT and front:
                        back(b + 1, 1 - par)
                    if c == Y2T_AT and front:
                        y2_transposes(b + 1, 1 - par)
                    if c >= OUT_LAG:
                        down(b, par, c - OUT_LAG)

            steps(pe, step)

        @block.scalar
        def _(act):
            act.wait_ge(scal_ready, 1)
            tanh_scale = act.alloc_register("tanh_scale")
            act.reg_load(tanh_scale, scal[0:1, 0:1].bitcast(I32))

            def y2_split(n, par):
                for k in range(2):
                    act.wait_ge(y2T_done, n * 2 + k + 1)
                    if k == 0:
                        wait(act, h_done, (n - 1) * HC)
                    act.activation(y2_hi[:, par, 2 * k:2 * k + 2, :], ps_f[:, k, :].rearrange("p (c s) -> p c s", c=2), ACT.Copy,
                                   scale=Y2_SCALE).then_inc(y2_hi_ready, 1)

            def step(b, par, front, main, finish):
                if not main:
                    if front:
                        y2_split(b + 1, 1 - par)
                    return
                for c in range(HC + 1):
                    if c < HC:
                        u = b * HC + c
                        act.wait_ge(h_done, u + 1)
                        wait(act, h1_ready, u - 1)
                        act.activation(th[:, c % 2, :], ps_h[:, c % 4, 0, :], ACT.Tanh, scale=tanh_scale).then_inc(th_ready, 1)
                    if c >= 1:
                        u = b * HC + c - 1
                        act.wait_ge(g_ready, u + 1)
                        act.copy(g_hi[:, (c - 1) % 4, :], g[:, (c - 1) % 2, :]).then_inc(g_hi_ready, 1)
                    if c == Y2_HI_AT and front:
                        y2_split(b + 1, 1 - par)

            steps(act, step)

        @block.gpsimd
        def _(pool):
            def step(b, par, front, main, finish):
                if front:
                    wait_alone(pool, moments_done, (b + 2) * SB, passed)
                if finish:
                    wait_alone(pool, moments3_done, b * SB, passed)
                which = slice(0 if front else 1, 2 if finish else 1)
                if front or finish:
                    rsqrt(Chain(pool, rstd_chain, (b + 1) * RSQRT_STEPS, passed), pool, rstd[:, which], moments[:, which, :, 1], nt, which)

            steps(pool, step)

        @block.vector
        def _(dve):
            ch = Chain(dve, scal_chain)
            mean = t["w_mean"]
            ch.then(dve.tensor_scalar(scal[:, 0:1], mean[:, 0:1], 0.5 / Y2_SCALE, None, ALU.mult))
            ch.then(dve.tensor_tensor(scal[:, 1:2], mean[:, 0:1], mean[:, 1:2], ALU.mult))
            ch.then(dve.tensor_scalar(scal[:, 1:2], scal[:, 1:2], mean[:, 2:3], 0.5 / (Y2_SCALE * Y2_SCALE * G_SCALE), ALU.mult, ALU.mult))
            dve.nop().then_inc(scal_ready, 1)

            def resid2_of(n, par, s):
                dve.wait_ge(y1_loaded, (n + 1) * 16)
                dve.wait_ge(back_done, n * SB + s + 1)
                dve.scalar_tensor_tensor(out=resid[:, s, :], in0=ps_f[:, s, :], scalar=t["conv_unscale"][:, 0:1], in1=y1[:, par, s, :],
                                         op0=ALU.mult, op1=ALU.add).then_inc(resid_done, 1)

            def stats2_of(n, s):
                dve.wait_ge(resid_done, n * SB + s + 1)
                dve.bn_stats(stats[:, 0, s, :], resid[:, s, :]).then_inc(stats_done, 1)
                wait_alone(dve, stats_done, n * SB + s + 1, passed)
                dve.bn_aggr(moments[:, 0, s, :], stats[:, 0, s, :]).then_inc(moments_done, 1)

            def y2_of(n, par):
                dve.wait_ge(rstd_chain, (n + 1) * RSQRT_STEPS)
                for s in range(SB):
                    dve.tensor_scalar(y2[:, par, s, :], resid[:, s, :], moments[:, 0, s, 0:1], rstd[:, 0, s:s + 1],
                                      ALU.subtract, ALU.mult).then_inc(y2_ready, 1)

            def resid3_of(m, par, s):
                dve.wait_ge(y_done, m * SB + s + 1)
                dve.scalar_tensor_tensor(out=resid3[:, s, :], in0=ps_y[:, s, :], scalar=scal[:, 1:2], in1=y2[:, par, s, :],
                                         op0=ALU.mult, op1=ALU.add).then_inc(resid3_done, 1)

            def stats3_of(m, s):
                dve.wait_ge(resid3_done, m * SB + s + 1)
                dve.bn_stats(stats[:, 1, s, :], resid3[:, s, :]).then_inc(stats3_done, 1)
                wait_alone(dve, stats3_done, m * SB + s + 1, passed)
                dve.bn_aggr(moments[:, 1, s, :], stats[:, 1, s, :]).then_inc(moments3_done, 1)

            def out_of(m, par):
                dve.wait_ge(rstd_chain, (m + 3) * RSQRT_STEPS)
                if not isinstance(m, int) or m >= 2:
                    dve.wait_ge(stored, (m - 1) * 16)
                for s in range(SB):
                    dve.tensor_scalar(out[:, par, s, :], resid3[:, s, :], moments[:, 1, s, 0:1], rstd[:, 1, s:s + 1],
                                      ALU.subtract, ALU.mult).then_inc(out_ready, 1)

            def around(b, par, front, finish, c):
                n, m = b + 1, b - 1
                if finish:
                    if c == RESID3_AT:
                        for s in range(SB):
                            resid3_of(m, 1 - par, s)
                    if c in STATS3_AT:
                        stats3_of(m, STATS3_AT.index(c))
                if front:
                    if c in STATS_AT:
                        stats2_of(n, STATS_AT.index(c))
                    if c in RESID_AT:
                        resid2_of(n, 1 - par, RESID_AT.index(c))
                    if c == Y2_AT:
                        y2_of(n, 1 - par)
                    if c == Y2_LO_AT:
                        y2_split(n, 1 - par)
                if finish and c == OUT_AT:
                    out_of(m, 1 - par)

            def y2_split(n, par):
                for k in range(2):
                    dve.wait_ge(y2_hi_ready, n * 2 + k + 1)
                    dve.scalar_tensor_tensor(out=y2_lo[:, par, 2 * k:2 * k + 2, :], in0=ps_f[:, k, :].rearrange("p (c s) -> p c s", c=2),
                                             scalar=Y2_SCALE, in1=y2_hi[:, par, 2 * k:2 * k + 2, :], op0=ALU.mult, op1=ALU.subtract)\
                       .then_inc(y2_lo_ready, 1)

            def ternary_w2(c):
                at = slice(c * D, (c + 1) * D)
                if c == 0:
                    dve.wait_ge(w2_loaded, 16)
                dve.tensor_scalar(w2_below[:, c % 2, :], w2_raw[:, at], t["limit"][:, 1, 2:3], None, ALU.is_lt).then_inc(w2_below_done, 1)
                dve.wait_ge(w2_below_done, c + 1)
                dve.scalar_tensor_tensor(out=t["ternary"][:, 2, at], in0=w2_raw[:, at], scalar=t["limit"][:, 0, 2:3],
                                         in1=w2_below[:, c % 2, :], op0=ALU.is_gt, op1=ALU.subtract).then_inc(w2_ready, 1)

            def step(b, par, front, main, finish):
                for c in range(HC + 1):
                    if isinstance(b, int) and b == 0 and c < HC:
                        ternary_w2(c)
                    if main and c < HC:
                        u = b * HC + c
                        dve.wait_ge(th_ready, u + 1)
                        dve.scalar_tensor_tensor(out=act_h1[:, c % 2, :], in0=th[:, c % 2, :], scalar=1.0, in1=ps_h[:, c % 4, 0, :],
                                                 op0=ALU.add, op1=ALU.mult).then_inc(h1_ready, 1)
                    if main and c >= 1:
                        dve.wait_ge(g_hi_ready, b * HC + c)
                        dve.tensor_tensor(g_lo[:, (c - 1) % 4, :], g[:, (c - 1) % 2, :], g_hi[:, (c - 1) % 4, :], ALU.subtract)\
                           .then_inc(g_lo_ready, 1)
                    if main and c < HC:
                        dve.wait_ge(h1_ready, u + 1)
                        dve.scalar_tensor_tensor(out=g[:, c % 2, :], in0=act_h1[:, c % 2, :], scalar=G_SCALE, in1=ps_h[:, c % 4, 1, :],
                                                 op0=ALU.mult, op1=ALU.mult).then_inc(g_ready, 1)
                    around(b, par, front, finish, c)

            steps(dve, step)


def build(nc, d):
    t = {}
    with ExitStack() as ctx:
        def keep(scope, name, shape, dt=F32):
            t[name] = scope.enter_context(nc.sbuf_tensor(name, shape, dt))

        keep(ctx, "ident", [P, P])
        keep(ctx, "scale", [P, NMAX])
        keep(ctx, "unscale", [P, NMAX])
        keep(ctx, "score_scale", [P, 2])
        keep(ctx, "neg_score_scale", [P, 2])
        keep(ctx, "attn_unscale", [P, 1])
        keep(ctx, "conv_unscale", [P, 1])
        keep(ctx, "mix_factor", [P, H, 2])
        keep(ctx, "w_sums", [P, B, 3])
        keep(ctx, "w_mean", [P, 3])
        keep(ctx, "limit", [P, 2, 3])
        keep(ctx, "y1T", [P, KC, B, S])
        keep(ctx, "w_qkv", [P, 2, 5, KC * D], F16)
        t["ctx_T"] = t["w_qkv"][:].rearrange("p a i n -> p (a i n)").bitcast(F32)[:, 0:GROUPS * S].rearrange("p (g s) -> p g s", g=GROUPS)
        keep(ctx, "ctx_max", [P, KC + 1])
        keep(ctx, "ctx_scal", [P, 4])
        for name in ("x_hi_ready", "x_lo_ready", "w_hi_ready", "w_lo_ready"):
            t[name] = ctx.enter_context(nc.semaphore(name))
        t["ctx_scaled"] = ctx.enter_context(nc.semaphore("ctx_scaled"))
        t["toep_written"] = ctx.enter_context(nc.semaphore("toep_written"))
        with ExitStack() as first:
            keep(first, "w_out", [P, 2, KC * D], F16)
            keep(first, "x_hi", [P, 2, KC * S], F16)
            keep(first, "x_lo", [P, 2, KC * S], F16)
            keep(first, "probs", [P, 4, 2, SB, S])
            t["late_stage"] = lambda i: t["probs"][:, 2 * (i - EARLY):2 * (i - EARLY) + 2].rearrange("p a w s n -> p (a w s n)")
            t["w"] = lambda half, i: t["w_qkv"][:, half, i, :] if i < 5 else t["w_out"][:, half, :]
            prepare(nc, t, d)
            attention(nc, t, d)
        keep(ctx, "conv_T", [P, GROUPS, S])
        keep(ctx, "ternary", [P, 3, WCOLS], F16)
        convolution(nc, t, d)
        feed_forward(nc, t, d)


def kernel(x, fside_S2_0, ctx_2048, L0_attn_q1_w, L0_attn_k1_w, L0_attn_q2_w, L0_attn_k2_w, L0_attn_v_w, L0_attn_o_w,
           L0_attn_lambda_param, L0_xattn_k, L0_ffn_w1, L0_ffn_w3, L0_ffn_w2):
    import concourse.bacc as bacc
    from concourse.bass_utils import run_bass_kernel_spmd

    f = lambda a: np.asarray(a)
    chunks = lambda a: a.reshape(-1, P, a.shape[1]).transpose(1, 0, 2)
    x = f(x)
    xT = x.transpose(2, 0, 1).reshape(KC, P, B, S).transpose(1, 2, 0, 3).reshape(P, B * KC * S)
    xT = np.concatenate([xT, np.zeros((P, KC * S), xT.dtype)], axis=1)
    ctxT = f(ctx_2048).transpose(2, 0, 1).reshape(KC, P, B, S).transpose(1, 0, 2, 3).reshape(P, KC * B, S)
    wproj = np.stack([chunks(f(w).T) for w in (L0_attn_q1_w, L0_attn_k1_w, L0_attn_q2_w, L0_attn_k2_w, L0_attn_v_w, L0_attn_o_w)], axis=1)
    pad = lambda a, n, axis: np.concatenate([a, np.zeros([n - s if i == axis else s for i, s in enumerate(a.shape)], a.dtype)], axis=axis)
    w1, w3 = (chunks(pad(f(w).T, HC * P, 1)).reshape(P, WCOLS) for w in (L0_ffn_w1, L0_ffn_w3))
    w2 = chunks(pad(f(L0_ffn_w2).T, HC * P, 0)).reshape(P, WCOLS)
    filt = f(L0_xattn_k)
    filt = np.concatenate([np.zeros((FILTERS, P), filt.dtype), filt], axis=1)
    arrays = {"x": x, "xT": xT, "ctxT": ctxT, "skip": f(fside_S2_0), "wproj": wproj.reshape(P, 6, KC * D), "lam": f(L0_attn_lambda_param),
              "filt": filt, "wffn": np.stack([w1, w3, w2], axis=1)}
    arrays = {k: np.ascontiguousarray(a) for k, a in arrays.items()}

    nc = bacc.Bacc("TRN2", target_bir_lowering=False, num_devices=1)
    d = {k: nc.dram_tensor(f"in_{k}", a.shape, mybir.dt.from_np(a.dtype), kind="ExternalInput").ap() for k, a in arrays.items()}
    d["out"] = nc.dram_tensor("out_y", (B, S, D), F32, kind="ExternalOutput").ap()
    d["y1_rows"] = nc.dram_tensor("y1_rows", (B, S, D), F32, kind="Internal").ap()
    d["filt_halves"] = nc.dram_tensor("filt_halves_dram", (2, FILTERS, D + P), F16, kind="Internal").ap()
    d["filt_whole"] = nc.dram_tensor("filt_whole_dram", (FILTERS, NEAR + P), F32, kind="Internal").ap()
    d["toeplitz_near"] = nc.dram_tensor("toeplitz_near", (FILTERS, P, NEAR), F32, kind="Internal").ap()
    d["toeplitz"] = nc.dram_tensor("toeplitz", (FILTERS, 2, P, D), F16, kind="Internal").ap()
    build(nc, d)
    r = run_bass_kernel_spmd(nc, [{f"in_{k}": a for k, a in arrays.items()}], core_ids=[0])
    return r.results[0]["out_y"]
```
